# Optimizing a Trainium2 kernel written in Bass

```python
import numpy as np
import jax
import jax.numpy as jnp

def _softmax(x, axis=-1):
    return jax.nn.softmax(x, axis=axis)

def _gelu(x):
    return jax.nn.gelu(x, approximate=True)

def _silu(x):
    return jax.nn.silu(x)

def _sigmoid(x):
    return jax.nn.sigmoid(x)

def _layernorm(x, axis=-1, eps=1e-05):
    m = jnp.mean(x, axis=axis, keepdims=True)
    v = jnp.var(x, axis=axis, keepdims=True)
    return (x - m) / jnp.sqrt(v + eps)

def _scatter_add(tgt, idx, src, axis=0):
    return tgt.at[idx].add(src)

def _segment_sum(src, seg, n):
    return jax.ops.segment_sum(src, seg, n)
kernel_name = 'mk_xattn_ffn_d4_seqx_r8_bc16e9'

def setup_inputs(seed: int=0):
    np.random.seed(seed)
    _w = jnp.asarray

    def _rec_inputs():
        import jax
        import jax.numpy as jnp
        _rk = jax.random.key(seed)
        x = -0.0003929 + 0.9999 * jax.random.normal(jax.random.fold_in(_rk, 1), (8, 128, 512), jnp.float32)
        _lenS = 128 - jax.random.randint(jax.random.fold_in(_rk, 7), (8,), 0, max(1, 128 // 4) + 1, jnp.int32)
        _lenS2 = 128 - jax.random.randint(jax.random.fold_in(_rk, 8), (8,), 0, max(1, 128 // 4) + 1, jnp.int32)
        _ctx_4096P = jax.random.normal(jax.random.fold_in(_rk, 11), (8, 16, 512), jnp.float32)
        _ctx_4096c = jax.random.dirichlet(jax.random.fold_in(_rk, 511), 0.3 * jnp.ones((16,), jnp.float32), (8, 128))
        _ctx_4096t = jnp.einsum('bsk,bkd->bsd', _ctx_4096c, _ctx_4096P)
        _ctx_4096t = _ctx_4096t * jax.lax.rsqrt(jnp.mean(jnp.square(_ctx_4096t)) + 1e-12) * 0.953939
        ctx_4096 = 2.81802e-05 + 1.00001 * (_ctx_4096t + 0.3 * jax.random.normal(jax.random.fold_in(_rk, 611), (8, 128, 512), jnp.float32))
        return (x, ctx_4096)
    x, ctx_4096 = _rec_inputs()

    def _L0_xattn_setup():
        import jax, jax.numpy as jnp
        import numpy as np
        B, D, N, H, K = (4, 128, 512, 16, 128)
        DH = D // H
        BN_EPS = 0.001

        def conv1(x, w, b):
            return jnp.einsum('oi,bin->bon', w, x) + b[None, :, None]
        key = jax.random.key(seed)
        ks = jax.random.split(key, 16)
        s = 0.02
        proj_std = 1.0 / np.sqrt(K)
        return {'x': jax.random.normal(ks[0], (B, D, N), jnp.float32), 'source': jax.random.normal(ks[1], (B, D, N), jnp.float32), 'to_q_w': jax.random.normal(ks[2], (D, D), jnp.float32) * s, 'to_q_b': jnp.zeros((D,), jnp.float32), 'to_k_w': jax.random.normal(ks[3], (D, D), jnp.float32) * s, 'to_k_b': jnp.zeros((D,), jnp.float32), 'proj_k': jax.random.uniform(ks[4], (N, K), jnp.float32, -proj_std, proj_std), 'merge_w': jax.random.normal(ks[5], (D, D), jnp.float32) * s, 'merge_b': jnp.zeros((D,), jnp.float32), 'mlp_w1': jax.random.normal(ks[6], (2 * D, 2 * D), jnp.float32) * s, 'mlp_b1': jnp.zeros((2 * D,), jnp.float32), 'bn_gamma': jnp.ones((2 * D,), jnp.float32), 'bn_beta': jnp.zeros((2 * D,), jnp.float32), 'bn_mean': jnp.zeros((2 * D,), jnp.float32), 'bn_var': jnp.ones((2 * D,), jnp.float32), 'mlp_w2': jax.random.normal(ks[7], (D, 2 * D), jnp.float32) * s, 'mlp_b2': jnp.zeros((D,), jnp.float32)}
    _L0_xattn_all = _L0_xattn_setup()
    _L0_xattn_in = {k: v for k, v in _L0_xattn_all.items() if k in ('to_q_w', 'to_q_b', 'to_k_w', 'to_k_b', 'proj_k', 'merge_w', 'merge_b', 'mlp_w1', 'mlp_b1', 'bn_gamma', 'bn_beta', 'bn_mean', 'bn_var', 'mlp_w2', 'mlp_b2')}
    del _L0_xattn_all

    def _L0_ffn_setup():
        import jax, jax.numpy as jnp
        import numpy as np
        HID, INTER = (512, 1792)
        B, S = (2, 256)

        def _binary_diff_weight(w, base):
            d = w - base
            coeff = jnp.mean(jnp.abs(d))
            return base + coeff * jnp.sign(d)
        key = jax.random.key(seed)
        ks = jax.random.split(key, 7)
        return {'hidden_states': jax.random.normal(ks[0], (B, S, HID), dtype=jnp.float32), 'w1': jax.random.normal(ks[1], (INTER, HID), dtype=jnp.float32) * 0.02, 'mean_w1': jax.random.normal(ks[2], (INTER, HID), dtype=jnp.float32) * 0.02, 'w2': jax.random.normal(ks[3], (HID, INTER), dtype=jnp.float32) * 0.02, 'mean_w2': jax.random.normal(ks[4], (HID, INTER), dtype=jnp.float32) * 0.02, 'w3': jax.random.normal(ks[5], (INTER, HID), dtype=jnp.float32) * 0.02, 'mean_w3': jax.random.normal(ks[6], (INTER, HID), dtype=jnp.float32) * 0.02}
    _L0_ffn_all = _L0_ffn_setup()
    _L0_ffn_in = {k: v for k, v in _L0_ffn_all.items() if k in ('w1', 'mean_w1', 'w2', 'mean_w2', 'w3', 'mean_w3')}
    del _L0_ffn_all

    def _L1_xattn_setup():
        import jax, jax.numpy as jnp
        import numpy as np
        TEXT_DIM = 512
        FEATURE_DIM = 512

        def _xavier_uniform(key, shape):
            fan_in, fan_out = (shape[1], shape[0])
            limit = float(np.sqrt(6.0 / (fan_in + fan_out)))
            return jax.random.uniform(key, shape, jnp.float32, -limit, limit)
        key = jax.random.key(seed)
        k1, k2, k3, k4 = jax.random.split(key, 4)
        text = jax.random.normal(k1, (8, 256, TEXT_DIM), jnp.float32)
        features = jax.random.normal(k2, (8, 72, FEATURE_DIM), jnp.float32)
        Wq = _xavier_uniform(k3, (FEATURE_DIM, TEXT_DIM))
        bq = jnp.zeros((FEATURE_DIM,), jnp.float32)
        Wk = _xavier_uniform(k4, (FEATURE_DIM, FEATURE_DIM))
        bk = jnp.zeros((FEATURE_DIM,), jnp.float32)
        return {'text': text, 'features': features, 'Wq': Wq, 'bq': bq, 'Wk': Wk, 'bk': bk}
    _L1_xattn_all = _L1_xattn_setup()
    _L1_xattn_in = {k: v for k, v in _L1_xattn_all.items() if k in ('Wq', 'bq', 'Wk', 'bk')}
    del _L1_xattn_all

    def _L1_ffn_setup():
        import jax, jax.numpy as jnp
        import numpy as np
        B, S, IN, OUT = (4, 256, 512, 512)
        E, K, R = (8, 2, 16)
        CAP_FACTOR = 3.0
        ALPHA = 1.0 / R
        LN_EPS = 1e-05
        key = jax.random.key(seed)
        ks = jax.random.split(key, 6)
        return {'x': jax.random.normal(ks[0], (B, S, IN), dtype=jnp.float32), 'weight': jax.random.normal(ks[1], (OUT, IN), dtype=jnp.float32) * 0.02, 'lora_A': jax.random.normal(ks[2], (E, IN, R), dtype=jnp.float32) / np.sqrt(R), 'lora_B': jax.random.normal(ks[3], (E, R, OUT), dtype=jnp.float32) * 0.02, 'gw1': jax.random.normal(ks[4], (4 * E, IN), dtype=jnp.float32) * 0.02, 'gb1': jnp.zeros((4 * E,), dtype=jnp.float32), 'ln_gamma': jnp.ones((4 * E,), dtype=jnp.float32), 'ln_beta': jnp.zeros((4 * E,), dtype=jnp.float32), 'gw2': jax.random.normal(ks[5], (E, 4 * E), dtype=jnp.float32) * 0.02, 'gb2': jnp.zeros((E,), dtype=jnp.float32)}
    _L1_ffn_all = _L1_ffn_setup()
    _L1_ffn_in = {k: v for k, v in _L1_ffn_all.items() if k in ('weight', 'lora_A', 'lora_B', 'gw1', 'gb1', 'ln_gamma', 'ln_beta', 'gw2', 'gb2')}
    del _L1_ffn_all

    def _L2_xattn_setup():
        import jax, jax.numpy as jnp
        import numpy as np
        DIM = 512
        NUM_HEADS = 32
        NUM_KV_HEADS = 8
        HEAD_DIM = DIM // NUM_HEADS
        KV_DIM = DIM // (NUM_HEADS // NUM_KV_HEADS)
        B, S = (1, 256)
        key = jax.random.key(seed)
        ks = jax.random.split(key, 7)
        w_scale = DIM ** (-0.5)
        return {'query': jax.random.normal(ks[0], (B, S, DIM), jnp.float32), 'key': jax.random.normal(ks[1], (B, S, DIM), jnp.float32), 'value': jax.random.normal(ks[2], (B, S, DIM), jnp.float32), 'Wq': jax.random.normal(ks[3], (DIM, DIM), jnp.float32) * w_scale, 'Wk': jax.random.normal(ks[4], (DIM, KV_DIM), jnp.float32) * w_scale, 'Wv': jax.random.normal(ks[5], (DIM, KV_DIM), jnp.float32) * w_scale, 'Wo': jax.random.normal(ks[6], (DIM, DIM), jnp.float32) * w_scale}
    _L2_xattn_all = _L2_xattn_setup()
    _L2_xattn_in = {k: v for k, v in _L2_xattn_all.items() if k in ('Wq', 'Wk', 'Wv', 'Wo')}
    del _L2_xattn_all

    def _L2_ffn_setup():
        import jax, jax.numpy as jnp
        import numpy as np
        SCALING = 16.0 / 8.0
        GAMMA = 1.0
        EPS = 1e-12
        key = jax.random.key(seed)
        ks = jax.random.split(key, 8)
        B, T, H, O = (4, 256, 512, 512)
        E_tot, E_act, r = (16, 4, 8)
        return {'x': jax.random.normal(ks[0], (B, T, H), jnp.float32), 'W_base': jax.random.normal(ks[1], (O, H), jnp.float32) * 0.02, 'b_base': jax.random.normal(ks[2], (O,), jnp.float32) * 0.02, 'lora_A': jax.random.normal(ks[3], (E_tot, r, H), jnp.float32) * 0.02, 'lora_B': jax.random.normal(ks[4], (E_tot, O, r), jnp.float32) * 0.02, 'router_W': jax.random.normal(ks[5], (E_tot, H), jnp.float32) * 0.02, 'router_b': jax.random.normal(ks[6], (E_tot,), jnp.float32) * 0.02, 'domain_prior': jax.random.uniform(ks[7], (E_tot,), jnp.float32), 'active': jnp.arange(E_act, dtype=jnp.int32)}
    _L2_ffn_all = _L2_ffn_setup()
    _L2_ffn_in = {k: v for k, v in _L2_ffn_all.items() if k in ('W_base', 'b_base', 'lora_A', 'lora_B', 'router_W', 'router_b', 'domain_prior', 'active')}
    del _L2_ffn_all

    def _L3_xattn_setup():
        import jax, jax.numpy as jnp
        import numpy as np
        key = jax.random.key(seed)
        k1, k2 = jax.random.split(key)
        B, Lq, Lk, D = (16, 128, 256, 512)
        query = jax.random.normal(k1, (B, Lq, D), dtype=jnp.float32)
        key_t = jax.random.normal(k2, (B, Lk, D), dtype=jnp.float32)
        return {'query': query, 'key': key_t}
    _L3_xattn_all = _L3_xattn_setup()
    _L3_xattn_in = {k: v for k, v in _L3_xattn_all.items() if k in ()}
    del _L3_xattn_all

    def _L3_ffn_setup():
        import jax, jax.numpy as jnp
        import numpy as np
        B_L, B_H = (4, 8)
        LIN_SLOPE, LIN_INTER, EST_T = (1.0, 0.0, 64.0)
        BATCH, SEQ, IN_F, OUT_F = (4, 256, 512, 512)
        MAX_BITS = 8

        def dequant_kbit(qweight, lut, bit):
            O, I32 = (qweight.shape[1], qweight.shape[2])
            shifts = jnp.arange(32, dtype=jnp.int32)
            idx = jnp.zeros((O, I32 * 32), dtype=jnp.int32)
            for p in range(bit):
                bits = (qweight[p][:, :, None] >> shifts & 1).reshape(O, I32 * 32)
                idx = idx | bits << p
            return jnp.take_along_axis(lut, idx, axis=1)
        key = jax.random.key(seed)
        k = jax.random.split(key, 5)
        x = jax.random.normal(k[0], (BATCH, SEQ, IN_F), dtype=jnp.float32)
        qweight = jax.random.randint(k[1], (MAX_BITS, OUT_F, IN_F // 32), 0, 2147483647, dtype=jnp.int32)
        lut4 = jax.random.normal(k[2], (OUT_F, 2 ** B_L), dtype=jnp.float32) * 0.02
        lut8 = jax.random.normal(k[3], (OUT_F, 2 ** B_H), dtype=jnp.float32) * 0.02
        bias = jax.random.normal(k[4], (OUT_F,), dtype=jnp.float32) * 0.01
        return {'x': x, 'qweight': qweight, 'lut4': lut4, 'lut8': lut8, 'bias': bias}
    _L3_ffn_all = _L3_ffn_setup()
    _L3_ffn_in = {k: v for k, v in _L3_ffn_all.items() if k in ('qweight', 'lut4', 'lut8', 'bias')}
    del _L3_ffn_all
    return {'x': x, 'ctx_4096': ctx_4096, 'L0_xattn_to_q_w': _L0_xattn_in['to_q_w'], 'L0_xattn_to_q_b': _L0_xattn_in['to_q_b'], 'L0_xattn_to_k_w': _L0_xattn_in['to_k_w'], 'L0_xattn_to_k_b': _L0_xattn_in['to_k_b'], 'L0_xattn_proj_k': _L0_xattn_in['proj_k'], 'L0_xattn_merge_w': _L0_xattn_in['merge_w'], 'L0_xattn_merge_b': _L0_xattn_in['merge_b'], 'L0_xattn_mlp_w1': _L0_xattn_in['mlp_w1'], 'L0_xattn_mlp_b1': _L0_xattn_in['mlp_b1'], 'L0_xattn_bn_gamma': _L0_xattn_in['bn_gamma'], 'L0_xattn_bn_beta': _L0_xattn_in['bn_beta'], 'L0_xattn_bn_mean': _L0_xattn_in['bn_mean'], 'L0_xattn_bn_var': _L0_xattn_in['bn_var'], 'L0_xattn_mlp_w2': _L0_xattn_in['mlp_w2'], 'L0_xattn_mlp_b2': _L0_xattn_in['mlp_b2'], 'L0_ffn_w1': _L0_ffn_in['w1'], 'L0_ffn_mean_w1': _L0_ffn_in['mean_w1'], 'L0_ffn_w2': _L0_ffn_in['w2'], 'L0_ffn_mean_w2': _L0_ffn_in['mean_w2'], 'L0_ffn_w3': _L0_ffn_in['w3'], 'L0_ffn_mean_w3': _L0_ffn_in['mean_w3'], 'L1_xattn_Wq': _L1_xattn_in['Wq'], 'L1_xattn_bq': _L1_xattn_in['bq'], 'L1_xattn_Wk': _L1_xattn_in['Wk'], 'L1_xattn_bk': _L1_xattn_in['bk'], 'L1_ffn_weight': _L1_ffn_in['weight'], 'L1_ffn_lora_A': _L1_ffn_in['lora_A'], 'L1_ffn_lora_B': _L1_ffn_in['lora_B'], 'L1_ffn_gw1': _L1_ffn_in['gw1'], 'L1_ffn_gb1': _L1_ffn_in['gb1'], 'L1_ffn_ln_gamma': _L1_ffn_in['ln_gamma'], 'L1_ffn_ln_beta': _L1_ffn_in['ln_beta'], 'L1_ffn_gw2': _L1_ffn_in['gw2'], 'L1_ffn_gb2': _L1_ffn_in['gb2'], 'L2_xattn_Wq': _L2_xattn_in['Wq'], 'L2_xattn_Wk': _L2_xattn_in['Wk'], 'L2_xattn_Wv': _L2_xattn_in['Wv'], 'L2_xattn_Wo': _L2_xattn_in['Wo'], 'L2_ffn_W_base': _L2_ffn_in['W_base'], 'L2_ffn_b_base': _L2_ffn_in['b_base'], 'L2_ffn_lora_A': _L2_ffn_in['lora_A'], 'L2_ffn_lora_B': _L2_ffn_in['lora_B'], 'L2_ffn_router_W': _L2_ffn_in['router_W'], 'L2_ffn_router_b': _L2_ffn_in['router_b'], 'L2_ffn_domain_prior': _L2_ffn_in['domain_prior'], 'L2_ffn_active': _L2_ffn_in['active'], 'L3_ffn_qweight': _L3_ffn_in['qweight'], 'L3_ffn_lut4': _L3_ffn_in['lut4'], 'L3_ffn_lut8': _L3_ffn_in['lut8'], 'L3_ffn_bias': _L3_ffn_in['bias']}

def reference(x, ctx_4096, L0_xattn_to_q_w, L0_xattn_to_q_b, L0_xattn_to_k_w, L0_xattn_to_k_b, L0_xattn_proj_k, L0_xattn_merge_w, L0_xattn_merge_b, L0_xattn_mlp_w1, L0_xattn_mlp_b1, L0_xattn_bn_gamma, L0_xattn_bn_beta, L0_xattn_bn_mean, L0_xattn_bn_var, L0_xattn_mlp_w2, L0_xattn_mlp_b2, L0_ffn_w1, L0_ffn_mean_w1, L0_ffn_w2, L0_ffn_mean_w2, L0_ffn_w3, L0_ffn_mean_w3, L1_xattn_Wq, L1_xattn_bq, L1_xattn_Wk, L1_xattn_bk, L1_ffn_weight, L1_ffn_lora_A, L1_ffn_lora_B, L1_ffn_gw1, L1_ffn_gb1, L1_ffn_ln_gamma, L1_ffn_ln_beta, L1_ffn_gw2, L1_ffn_gb2, L2_xattn_Wq, L2_xattn_Wk, L2_xattn_Wv, L2_xattn_Wo, L2_ffn_W_base, L2_ffn_b_base, L2_ffn_lora_A, L2_ffn_lora_B, L2_ffn_router_W, L2_ffn_router_b, L2_ffn_domain_prior, L2_ffn_active, L3_ffn_qweight, L3_ffn_lut4, L3_ffn_lut8, L3_ffn_bias):
    import jax
    import jax.numpy as jnp

    def _L0_xattn_ref(x, source, to_q_w, to_q_b, to_k_w, to_k_b, proj_k, merge_w, merge_b, mlp_w1, mlp_b1, bn_gamma, bn_beta, bn_mean, bn_var, mlp_w2, mlp_b2):
        import jax, jax.numpy as jnp
        import numpy as np
        B, D, N, H, K = (4, 128, 512, 16, 128)
        DH = D // H
        BN_EPS = 0.001

        def conv1(x, w, b):
            return jnp.einsum('oi,bin->bon', w, x) + b[None, :, None]
        b = x.shape[0]
        q = conv1(x, to_q_w, to_q_b)
        k = conv1(source, to_k_w, to_k_b)
        v = k
        k = jnp.einsum('bdm,mk->bdk', k, proj_k)
        v = jnp.einsum('bdm,mk->bdk', v, proj_k)
        qh = q.reshape(b, DH, H, N)
        kh = k.reshape(b, DH, H, K)
        vh = v.reshape(b, DH, H, K)
        scores = jnp.einsum('bdhn,bdhk->bhnk', qh, kh) / DH ** 0.5
        prob = jax.nn.softmax(scores, axis=-1)
        msg = jnp.einsum('bhnk,bdhk->bdhn', prob, vh).reshape(b, D, N)
        msg = conv1(msg, merge_w, merge_b)
        h = jnp.concatenate([x, msg], axis=1)
        h = conv1(h, mlp_w1, mlp_b1)
        h = bn_gamma[None, :, None] * (h - bn_mean[None, :, None]) * jax.lax.rsqrt(bn_var + BN_EPS)[None, :, None] + bn_beta[None, :, None]
        h = jax.nn.relu(h)
        return conv1(h, mlp_w2, mlp_b2)

    def _L0_ffn_ref(hidden_states, w1, mean_w1, w2, mean_w2, w3, mean_w3):
        import jax, jax.numpy as jnp
        import numpy as np
        HID, INTER = (512, 1792)
        B, S = (2, 256)

        def _binary_diff_weight(w, base):
            d = w - base
            coeff = jnp.mean(jnp.abs(d))
            return base + coeff * jnp.sign(d)
        W1 = _binary_diff_weight(w1, mean_w1)
        W2 = _binary_diff_weight(w2, mean_w2)
        W3 = _binary_diff_weight(w3, mean_w3)
        gate = jnp.einsum('bsh,ih->bsi', hidden_states, W1)
        up = jnp.einsum('bsh,ih->bsi', hidden_states, W3)
        h = jax.nn.silu(gate) * up
        return jnp.einsum('bsi,hi->bsh', h, W2)

    def _L1_xattn_ref(text, features, Wq, bq, Wk, bk):
        import jax, jax.numpy as jnp
        import numpy as np
        TEXT_DIM = 512
        FEATURE_DIM = 512

        def _xavier_uniform(key, shape):
            fan_in, fan_out = (shape[1], shape[0])
            limit = float(np.sqrt(6.0 / (fan_in + fan_out)))
            return jax.random.uniform(key, shape, jnp.float32, -limit, limit)
        Q = jnp.einsum('btx,dx->btd', text, Wq) + bq
        K = jnp.einsum('bpx,dx->bpd', features, Wk) + bk
        scale = 1.0 / jnp.sqrt(jnp.asarray(K.shape[-1], K.dtype))
        scores = jnp.einsum('btd,bpd->btp', Q, K) * scale
        attn = jax.nn.softmax(scores, axis=-1)
        attended = jnp.einsum('btp,bpd->btd', attn, features)
        return attended

    def _L1_ffn_ref(x, weight, lora_A, lora_B, gw1, gb1, ln_gamma, ln_beta, gw2, gb2):
        import jax, jax.numpy as jnp
        import numpy as np
        B, S, IN, OUT = (4, 256, 512, 512)
        E, K, R = (8, 2, 16)
        CAP_FACTOR = 3.0
        ALPHA = 1.0 / R
        LN_EPS = 1e-05
        orig_shape = x.shape
        xf = x.reshape(-1, orig_shape[-1])
        N = xf.shape[0]
        capacity = int(CAP_FACTOR * N / E)
        h = xf @ gw1.T + gb1
        mu = jnp.mean(h, axis=-1, keepdims=True)
        var = jnp.mean((h - mu) ** 2, axis=-1, keepdims=True)
        h = (h - mu) * jax.lax.rsqrt(var + LN_EPS) * ln_gamma + ln_beta
        h = jax.nn.relu(h)
        gates = h @ gw2.T + gb2
        top_v, top_i = jax.lax.top_k(gates, K)
        top_g = jax.nn.softmax(top_v, axis=-1)
        onehot = (top_i[..., None] == jnp.arange(E)).astype(xf.dtype)
        counts = onehot.sum(axis=0)
        allowed = (counts <= capacity).astype(xf.dtype)
        w = jnp.einsum('nke,nk,ke->ne', onehot, top_g, allowed)
        main = xf @ weight.T
        tmp = jnp.einsum('ni,eir->enr', xf, lora_A)
        tmp = tmp * w.T[:, :, None]
        lora = jnp.einsum('enr,ero->no', tmp, lora_B) * ALPHA
        out = main + lora
        return out.reshape(*orig_shape[:-1], weight.shape[0])

    def _L2_xattn_ref(query, key, value, Wq, Wk, Wv, Wo):
        import jax, jax.numpy as jnp
        import numpy as np
        DIM = 512
        NUM_HEADS = 32
        NUM_KV_HEADS = 8
        HEAD_DIM = DIM // NUM_HEADS
        KV_DIM = DIM // (NUM_HEADS // NUM_KV_HEADS)
        B, S = (1, 256)
        b, sq, _ = query.shape
        _, sk, _ = key.shape
        rep = NUM_HEADS // NUM_KV_HEADS
        q = (query @ Wq).reshape(b, sq, NUM_HEADS, HEAD_DIM).transpose(0, 2, 1, 3)
        k = (key @ Wk).reshape(b, sk, NUM_KV_HEADS, HEAD_DIM).transpose(0, 2, 1, 3)
        v = (value @ Wv).reshape(b, sk, NUM_KV_HEADS, HEAD_DIM).transpose(0, 2, 1, 3)
        k = jnp.repeat(k, rep, axis=1)
        v = jnp.repeat(v, rep, axis=1)
        scale = HEAD_DIM ** (-0.5)
        scores = jnp.einsum('bhqd,bhkd->bhqk', q, k) * scale
        probs = jax.nn.softmax(scores, axis=-1)
        out = jnp.einsum('bhqk,bhkd->bhqd', probs, v)
        out = out.transpose(0, 2, 1, 3).reshape(b, sq, DIM)
        return out @ Wo

    def _L2_ffn_ref(x, W_base, b_base, lora_A, lora_B, router_W, router_b, domain_prior, active):
        import jax, jax.numpy as jnp
        import numpy as np
        SCALING = 16.0 / 8.0
        GAMMA = 1.0
        EPS = 1e-12
        y = jnp.einsum('bth,oh->bto', x, W_base) + b_base
        A = lora_A[active]
        Bm = lora_B[active]
        z = jnp.einsum('bth,erh->bter', x, A)
        contribs = jnp.einsum('bter,eor->bteo', z, Bm) * SCALING
        logits = jnp.einsum('bth,eh->bte', x, router_W) + router_b
        logits = logits[..., active]
        prior = domain_prior[active]
        alpha = jax.nn.softmax(jnp.log(prior + EPS) + logits / GAMMA, axis=-1)
        return y + jnp.einsum('bteo,bte->bto', contribs, alpha)

    def _L3_xattn_ref(query, key):
        import jax, jax.numpy as jnp
        import numpy as np
        a = jnp.einsum('bqd,bkd->bqk', query, key)
        e = jax.nn.softmax(a, axis=-1)
        c = jnp.einsum('bqk,bkd->bqd', e, key)
        return c

    def _L3_ffn_ref(x, qweight, lut4, lut8, bias):
        import jax, jax.numpy as jnp
        import numpy as np
        B_L, B_H = (4, 8)
        LIN_SLOPE, LIN_INTER, EST_T = (1.0, 0.0, 64.0)
        BATCH, SEQ, IN_F, OUT_F = (4, 256, 512, 512)
        MAX_BITS = 8

        def dequant_kbit(qweight, lut, bit):
            O, I32 = (qweight.shape[1], qweight.shape[2])
            shifts = jnp.arange(32, dtype=jnp.int32)
            idx = jnp.zeros((O, I32 * 32), dtype=jnp.int32)
            for p in range(bit):
                bits = (qweight[p][:, :, None] >> shifts & 1).reshape(O, I32 * 32)
                idx = idx | bits << p
            return jnp.take_along_axis(lut, idx, axis=1)
        e = jnp.linalg.norm(x, axis=-1) * LIN_SLOPE + LIN_INTER
        mask = e > EST_T
        w_l = dequant_kbit(qweight, lut4, B_L)
        w_h = dequant_kbit(qweight, lut8, B_H)
        y_l = jnp.einsum('bsi,oi->bso', x, w_l)
        y_h = jnp.einsum('bsi,oi->bso', x, w_h)
        y = jnp.where(mask[..., None], y_h, y_l) + bias
        return y
    x = x + _L0_xattn_ref(_layernorm(x, axis=-1), ctx_4096, L0_xattn_to_q_w, L0_xattn_to_q_b, L0_xattn_to_k_w, L0_xattn_to_k_b, L0_xattn_proj_k, L0_xattn_merge_w, L0_xattn_merge_b, L0_xattn_mlp_w1, L0_xattn_mlp_b1, L0_xattn_bn_gamma, L0_xattn_bn_beta, L0_xattn_bn_mean, L0_xattn_bn_var, L0_xattn_mlp_w2, L0_xattn_mlp_b2)
    x = x + _L0_ffn_ref(_layernorm(x, axis=-1), L0_ffn_w1, L0_ffn_mean_w1, L0_ffn_w2, L0_ffn_mean_w2, L0_ffn_w3, L0_ffn_mean_w3)
    x = x + _L1_xattn_ref(_layernorm(x, axis=-1), ctx_4096, L1_xattn_Wq, L1_xattn_bq, L1_xattn_Wk, L1_xattn_bk)
    x = x + _L1_ffn_ref(_layernorm(x, axis=-1), L1_ffn_weight, L1_ffn_lora_A, L1_ffn_lora_B, L1_ffn_gw1, L1_ffn_gb1, L1_ffn_ln_gamma, L1_ffn_ln_beta, L1_ffn_gw2, L1_ffn_gb2)
    x = x + _L2_xattn_ref(_layernorm(x, axis=-1), ctx_4096, ctx_4096, L2_xattn_Wq, L2_xattn_Wk, L2_xattn_Wv, L2_xattn_Wo)
    x = x + _L2_ffn_ref(_layernorm(x, axis=-1), L2_ffn_W_base, L2_ffn_b_base, L2_ffn_lora_A, L2_ffn_lora_B, L2_ffn_router_W, L2_ffn_router_b, L2_ffn_domain_prior, L2_ffn_active)
    x = x + _L3_xattn_ref(_layernorm(x, axis=-1), ctx_4096)
    x = x + _L3_ffn_ref(_layernorm(x, axis=-1), L3_ffn_qweight, L3_ffn_lut4, L3_ffn_lut8, L3_ffn_bias)
    return x

_drawn_inputs = setup_inputs


def setup_inputs(seed=0):
    import zlib

    import numpy as np

    out = dict(_drawn_inputs(seed))
    spreads = {'L0_xattn_to_q_b': (0.0, 0.8),
     'L0_xattn_to_k_b': (0.0, 0.8),
     'L0_xattn_merge_b': (0.0, 2.0),
     'L0_xattn_mlp_b1': (0.0, 0.8),
     'L0_xattn_bn_gamma': (1.0, 0.6),
     'L0_xattn_bn_beta': (0.0, 0.8),
     'L0_xattn_bn_mean': (0.0, 0.8),
     'L0_xattn_bn_var': (1.0, 0.6),
     'L0_xattn_mlp_b2': (0.0, 0.482),
     'L1_xattn_bq': (0.0, 0.272),
     'L1_xattn_bk': (0.0, 2.0),
     'L1_ffn_gb1': (0.0, 0.663),
     'L1_ffn_ln_gamma': (1.0, 0.6),
     'L1_ffn_ln_beta': (0.0, 0.794),
     'L1_ffn_gb2': (0.0, 0.437)}
    factors = {'L0_xattn_to_q_w': 8.0,
     'L0_xattn_to_k_w': 8.0,
     'L0_xattn_proj_k': 8.0,
     'L0_xattn_merge_w': 8.0,
     'L1_ffn_lora_A': 3.572,
     'L1_ffn_lora_B': 3.64,
     'L1_ffn_gw1': 3.953,
     'L1_ffn_gw2': 4.0,
     'L2_ffn_b_base': 11.815,
     'L2_ffn_router_W': 47.384,
     'L2_ffn_router_b': 64.0,
     'L2_ffn_domain_prior': 43.968,
     'L3_ffn_bias': 34.224,
     'L0_ffn_mean_w1': 3.06,
     'L0_ffn_mean_w2': 2.789,
     'L0_ffn_mean_w3': 3.006,
     'L2_ffn_lora_A': 5.595,
     'L2_ffn_lora_B': 5.995}
    for name, (base, spread) in spreads.items():
        noise = np.random.default_rng([zlib.crc32(name.encode()), seed]).standard_normal(out[name].shape)
        drawn = base * np.exp(spread * noise) if base else spread * noise
        out[name] = jnp.asarray(drawn.astype(out[name].dtype))
    for name, factor in factors.items():
        out[name] = (out[name] * factor).astype(out[name].dtype)
    return out
```

```python
from contextlib import ExitStack

import concourse.bass as bass
from concourse import mybir

F32 = mybir.dt.float32
F32R = mybir.dt.float32r
BF16 = mybir.dt.bfloat16
I32 = mybir.dt.int32
U8 = mybir.dt.uint8
ALU = mybir.AluOpType
ACT = mybir.ActivationFunctionType
AX = mybir.AxisListType

P = 128
NB = 8
D = 512
DC = D // P
LN_EPS = 1e-5
BN_EPS = 1e-3


CONSTANTS = 5


class Shared:
    pass


def symbolic(b):
    return not isinstance(b, int)


def has_before(b, n):
    return symbolic(b) or b >= n


def has_after(b, n):
    return symbolic(b) or b + n < NB


def slots(engine, slot):
    slot(0, 0)
    slot(1, 1)
    with engine.Fori(1, NB // 2 - 1) as i:
        for p in range(2):
            slot(2 * i + p, p)
    slot(NB - 2, 0)
    slot(NB - 1, 1)


def packed_attention(nc, s, name, HL, scale, load, prep, tail):
    J = 4 * HL
    W = P * HL
    PER = 512 // W
    Q, KB, VE = s.Q, s.KB, s.VE
    sem = s.sem
    q_packed = sem(name + "_q_packed")
    kb_ready = sem(name + "_kb_ready")
    s_ready = sem(name + "_s_ready")
    s_taken = sem(name + "_s_taken")
    max_split = sem(name + "_max_split")
    max_turned = sem(name + "_max_turned")
    max_rows = sem(name + "_max_rows")
    max_packed = sem(name + "_max_packed")
    t_ready = sem(name + "_t_ready")
    exp_done = sem(name + "_exp_done")
    pv_done = sem(name + "_pv_done")
    rden_done = sem(name + "_rden_done")
    msg_done = sem(name + "_msg_done")
    hi_done = sem(name + "_hi_done")
    s.q_may_pack = sem(name + "_q_may_pack")

    def s_tile(j):
        return j * PER // 4, j * PER % 4

    def pe_scores(pe, b, p, j):
        g, q0 = s_tile(j)
        if j == 0:
            pe.wait_ge(q_packed, (b + 1) * 192)
            pe.wait_ge(kb_ready, b + 1)
        if j >= 2:
            pe.wait_ge(s_taken, b * J + j - 1)
        for r in range(PER):
            last = nc.tensor.matmul(s.ps[:, j % 2, r * W:(r + 1) * W], Q[0:96, p, g, (q0 + r) * P:(q0 + r + 1) * P],
                                    KB[0:96, p, g, 0:W], start=True, stop=True)
        last.then_inc(s_ready, 1)

    def dve_max(dve, b, p, j):
        g, q0 = s_tile(j)
        dve.wait_ge(s_ready, b * J + j + 1)
        if j == 0:
            dve.wait_ge(max_split, b)
        nc.vector.tensor_reduce(s.mx[:, q0:q0 + PER, g, 0:HL],
                                s.ps[:, j % 2, :].rearrange("p (q h k) -> p q h k", q=PER, h=HL), AX.X, ALU.max
                                ).then_inc(s_taken, 1)
        if j == J - 1:
            dve.wait_ge(s_taken, (b + 1) * J)
            dve.wait_ge(max_turned, b)
            nc.vector.tensor_copy(s.m8[:, :, :, 0, 0:HL], s.mx[:, :, :, 0:HL]).then_inc(hi_done, 1)
            dve.wait_ge(hi_done, b + 1)
            nc.vector.tensor_tensor(s.m8[:, :, :, 1, 0:HL], s.mx[:, :, :, 0:HL], s.m8[:, :, :, 0, 0:HL],
                                    ALU.subtract).then_inc(max_split, 1)

    def pe_max_turn(pe, b):
        pe.wait_ge(max_split, b + 1)
        s.wait_bank_a(pe, b)
        for q in range(4):
            last = nc.tensor.matmul(s.ps[96:96 + 8 * HL, s.A, q * P:(q + 1) * P],
                                    s.m8[:, q, :, :, :].rearrange("p g t h -> p (g t h)"),
                                    s.ident_bf[:, :], start=True, stop=True)
        last.then_inc(max_turned, 1)

    def dve_max_rows(dve, b):
        dve.wait_ge(max_turned, b + 1)
        if has_before(b, 1):
            dve.wait_ge(max_packed, b * 64)
        nc.vector.tensor_copy(s.mrow[96:96 + 8 * HL, :], s.ps[96:96 + 8 * HL, s.A, :]).then_inc(max_rows, 1)

    def sp_max_pack(sp, b, p):
        sp.wait_ge(max_rows, b + 1)
        for g in range(4):
            sp.dma_start(Q[96:128, p, g, :].bitcast(F32), s.mrow[96:128, :].bitcast(F32)).then_inc(max_packed, 16)

    def pe_turned(pe, b, p, h, g):
        j = 4 * h + g
        if j == 0:
            pe.wait_ge(max_packed, (b + 1) * 64)
        if j >= 2:
            pe.wait_ge(exp_done, b * J + j - 1)
        nc.tensor.matmul(s.ps[:, 2 + j % 2, :], KB[:, p, g, h * P:(h + 1) * P], Q[:, p, g, :],
                         start=True, stop=True).then_inc(t_ready, 1)

    def act_exp(act, b, h, g):
        j = 4 * h + g
        act.wait_ge(t_ready, b * J + j + 1)
        if h >= 2 and g == 0:
            act.wait_ge(pv_done, b * HL + h - 1)
        nc.scalar.activation(s.PT[:, j % 8, :], s.ps[:, 2 + j % 2, :], ACT.Exp, scale=scale).then_inc(exp_done, 1)

    def pe_values(pe, b, p, h):
        pe.wait_ge(exp_done, b * J + 4 * h + 4)
        if h == 0:
            pe.wait_ge(msg_done, b)
        for g in range(4):
            w = s.PT[:, (4 * h + g) % 8, :]
            nc.tensor.matmul(s.ps[32 * g:32 * g + 32, 4, :], VE[:, p, g, h, :], w, start=(h == 0), stop=(h == HL - 1))
        for g in range(4):
            w = s.PT[:, (4 * h + g) % 8, :]
            last = nc.tensor.matmul(s.ps[32 * g:32 * g + 32, 5, :], s.ones_blk[HL][:, h, :], w, start=(h == 0), stop=(h == HL - 1))
        last.then_inc(pv_done, 1)

    def dve_normalise(dve, b):
        dve.wait_ge(pv_done, (b + 1) * HL)
        nc.vector.reciprocal(s.rden[:, :], s.ps[:, 5, :]).then_inc(rden_done, 1)
        dve.wait_ge(rden_done, b + 1)
        tail.wait_msg_free(dve, b)
        nc.vector.tensor_tensor(s.msg[:, :], s.ps[:, 4, :], s.rden[:, :], ALU.mult).then_inc(msg_done, 1)

    s.q_packed, s.kb_ready, s.msg_done, s.max_rows, s.pv_done, s.t_ready = q_packed, kb_ready, msg_done, max_rows, pv_done, t_ready
    s.J = J

    with nc.Block() as block:
        @block.sync
        def _(sp):
            load(sp, 0, 0)
            load(sp, 1, 1)
            prep.sp(sp, 0, 0)
            sp_max_pack(sp, 0, 0)
            prep.sp(sp, 1, 1)

            def slot(b, p):
                if has_after(b, 2):
                    load(sp, b + 2, p)
                    prep.sp(sp, b + 2, p)
                if has_after(b, 1):
                    sp_max_pack(sp, b + 1, 1 - p)
            slots(sp, slot)

        @block.gpsimd
        def _(pool):
            def slot(b, p):
                if has_after(b, 2):
                    prep.pool(pool, b + 2, p)
                if has_before(b, 2):
                    s.front.pool_rstd(pool, b - 2, p)
            prep.pool(pool, 0, 0)
            prep.pool(pool, 1, 1)
            slots(pool, slot)
            s.front.pool_rstd(pool, NB - 2, 0)
            s.front.pool_rstd(pool, NB - 1, 1)

        @block.tensor
        def _(pe):
            prep.pe(pe, 0, 0)
            for j in range(J):
                pe_scores(pe, 0, 0, j)
            pe_max_turn(pe, 0)
            prep.pe(pe, 1, 1)

            def slot(b, p):
                for h in range(HL):
                    if h == HL // 2 and has_after(b, 2):
                        prep.pe(pe, b + 2, p)
                    for g in range(4):
                        pe_turned(pe, b, p, h, g)
                        if has_after(b, 1):
                            pe_scores(pe, b + 1, 1 - p, 4 * h + g)
                    if h:
                        pe_values(pe, b, p, h - 1)
                pe_values(pe, b, p, HL - 1)
                if has_after(b, 1):
                    pe_max_turn(pe, b + 1)
                tail.pe(pe, b, p)

            slots(pe, slot)

        @block.scalar
        def _(act):
            prep.act(act, 0, 0)
            prep.act(act, 1, 1)

            def slot(b, p):
                for h in range(HL):
                    if h == HL // 2 and has_after(b, 2):
                        prep.act(act, b + 2, p)
                    for g in range(4):
                        act_exp(act, b, h, g)
                tail.act(act, b, p)

            slots(act, slot)

        @block.vector
        def _(dve):
            prep.dve(dve, 0, 0)
            for j in range(J):
                dve_max(dve, 0, 0, j)
            dve_max_rows(dve, 0)
            prep.dve(dve, 1, 1)

            def slot(b, p):
                for j in range(J):
                    if j == J // 2 and has_after(b, 2):
                        prep.dve(dve, b + 2, p)
                    if has_after(b, 1):
                        dve_max(dve, b + 1, 1 - p, j)
                dve_normalise(dve, b)
                if has_after(b, 1):
                    dve_max_rows(dve, b + 1)
                tail.dve(dve, b, p)

            slots(dve, slot)
            s.front.dve_last_moments(dve, tail.written)
    s.front.mbase += NB


def linked(engine, semaphore):
    count = [0]

    def link(instruction):
        count[0] += 1
        instruction.then_inc(semaphore, 1)
        engine.wait_ge(semaphore, count[0])
    return link


def setup(nc, s, t):
    x_in = [s.sem(f"x_in{b}") for b in range(NB)]
    w_in = s.sem("l0_w_in")
    fold_ready, fold_taken = s.sem("l0_fold_ready"), s.sem("l0_fold_taken")
    chain, stats, moments, rstd, bn_chain, bn_rstd, eps_added = (s.sem(n) for n in ("setup_chain", "ln0_stats", "ln0_moments", "ln0_rstd", "bn_chain", "bn_rstd", "eps_added"))
    loads = [(s.ident, t["ident"]), (s.wq0, t["wq0"]), (s.wk0, t["wk0"]), (s.wk0_rep, t["wk0_rep"]),
             (s.proj, t["proj_k"].rearrange("(c p) k -> p c k", p=P)), (s.wm0, t["wm0"]), (s.w1m0, t["w1m0"]),
             (s.w1x0, t["w1x0"]), (s.w2_0, t["w2_0"]), (s.cols0, t["cols0"]), (s.bk0_row, t["bk0_row"].broadcast_to([P, P])),
             (s.ones_blk[4], t["ones4"]), (s.ones_blk[2], t["ones2"]), (s.mask4, t["mask4"]), (s.mask2, t["mask2"]),
             (s.neg[96:128], t["neg4"])]
    with nc.Block() as block:
        @block.sync
        def _(sp):
            for b in range(NB):
                sp.dma_start(s.X[:, b, :], t["x"][b]).then_inc(x_in[b], 16)

        @block.scalar
        def _(act):
            for to, of in loads:
                act.dma_start(to, of).then_inc(w_in, 16)

        @block.gpsimd
        def _(pool):
            nc.gpsimd.memset(s.ones[:, :], 1.0).then_inc(s.ones_ready, 1)
            nc.gpsimd.memset(s.eps[:, :], LN_EPS).then_inc(s.ones_ready, 1)
            nc.gpsimd.memset(s.minus_half[:, :], -0.5).then_inc(s.ones_ready, 1)
            nc.gpsimd.memset(s.mrow[:, :].bitcast(F32), 0.0).then_inc(s.ones_ready, 1)
            nc.gpsimd.memset(s.VE[:, :, :, :, :], 0.0).then_inc(s.ones_ready, 1)
            pool.wait_ge(w_in, 16 * len(loads))
            pool.wait_ge(s.ones_ready, CONSTANTS)
            nc.gpsimd.tensor_scalar(s.bn[:, 12:14], s.cols0[:, 14:16], BN_EPS, None, ALU.add).then_inc(eps_added, 1)
            pool.wait_ge(eps_added, 1)
            nc.gpsimd.tensor_tensor(s.bn[:, 0:2], s.bn[:, 12:14], s.minus_half[:, 0:2], ALU.pow).then_inc(bn_rstd, 1)
            pool.wait_ge(moments, NB)
            nc.gpsimd.tensor_scalar(s.var_eps[:, :], s.mv[:, :, 1], LN_EPS, None, ALU.add).then_inc(eps_added, 1)
            pool.wait_ge(eps_added, 2)
            nc.gpsimd.tensor_tensor(s.rstd[:, :, 0], s.var_eps[:, :], s.minus_half[:, :], ALU.pow).then_inc(rstd, 1)

        @block.tensor
        def _(pe):
            pe.wait_ge(w_in, 16 * len(loads))
            pe.wait_ge(s.ones_ready, CONSTANTS)
            for c in range(DC):
                nc.tensor.matmul(s.ps[:, 0, 0:1], s.proj[:, c, :], s.ones[:, 0:1], start=(c == 0), stop=(c == DC - 1))
            for c in range(DC):
                nc.tensor.matmul(s.ps[:, 1, 0:P], s.ones[:, :], s.proj[:, c, :], start=(c == 0), stop=(c == DC - 1))
            nc.tensor.matmul(s.ps[:, 2, 0:256], s.wm0, s.w1m0, start=True, stop=True)
            for h in range(2):
                last = nc.tensor.matmul(s.ps[:, 3, h:h + 1], s.w1m0[:, h * P:(h + 1) * P], s.cols0[:, 6:7], start=(h == 0), stop=(h == 1), skip_group_check=True)
            last.then_inc(fold_ready, 1)

        @block.vector
        def _(dve):
            link = linked(dve, bn_chain)
            dve.wait_ge(w_in, 16 * len(loads))
            nc.vector.tensor_copy(s.ident_bf[:, :], s.ident).then_inc(fold_taken, 1)
            for p in range(2):
                nc.vector.tensor_copy(s.KB[96:128, p, :, :], s.neg[96:128, :, :]).then_inc(fold_taken, 1)
            dve.wait_ge(fold_ready, 1)
            nc.vector.tensor_copy(s.colsum[:, :], s.ps[:, 0, 0:1]).then_inc(fold_taken, 1)
            nc.vector.tensor_copy(s.colsum_row[:, :], s.ps[:, 1, 0:P]).then_inc(fold_taken, 1)
            nc.vector.tensor_copy(s.weff[:, :], s.ps[:, 2, 0:256]).then_inc(fold_taken, 1)
            c = s.cols0
            dve.wait_ge(bn_rstd, 1)
            link(nc.vector.tensor_tensor(s.bn[:, 2:4], s.bn[:, 0:2], c[:, 8:10], ALU.mult))
            link(nc.vector.tensor_tensor(s.bn[:, 4:6], c[:, 16:18], s.ps[:, 3, 0:2], ALU.add))
            link(nc.vector.tensor_tensor(s.bn[:, 6:8], s.bn[:, 4:6], c[:, 12:14], ALU.subtract))
            link(nc.vector.tensor_tensor(s.bn[:, 8:10], s.bn[:, 6:8], s.bn[:, 2:4], ALU.mult))
            link(nc.vector.tensor_tensor(s.bn[:, 10:12], s.bn[:, 8:10], c[:, 10:12], ALU.add))
            for b in range(NB):
                dve.wait_ge(x_in[b], 16)
            for b in range(NB):
                nc.vector.bn_stats(s.stats[:, b, :], s.X[:, b, :]).then_inc(stats, 1)
            for b in range(NB):
                dve.wait_ge(stats, b + 1)
                nc.vector.bn_aggr(s.mv[:, b, :], s.stats[:, b, :]).then_inc(moments, 1)
            dve.wait_ge(rstd, 1)
            with dve.Fori(0, NB) as b:
                nc.vector.tensor_scalar(s.XN[:, b, :], s.X[:, b, :], s.mv[:, b, 0:1], s.rstd[:, b, :], ALU.subtract, ALU.mult).then_inc(chain, 1)


def linear_attention_of_channels(nc, s, t):
    sem = s.sem
    ct_in, c_ready, c_taken = (sem("l0_ct_in0"), sem("l0_ct_in1")), sem("l0_c_ready"), sem("l0_c_taken")
    q_ready, qhi_done, qlo_done = sem("l0_q_ready"), sem("l0_qhi_done"), sem("l0_qlo_done")
    kr_ready, v_ready, kf_done, kh_done, kx_done, v_done = (sem("l0_" + n) for n in (
        "kr_ready", "v_ready", "kf_done", "kh_done", "kx_done", "v_done"))
    h_ready, relu_done, o_ready, res_done = sem("l0_h_ready"), sem("l0_relu_done"), sem("l0_o_ready"), sem("l0_res_done")
    A, B = s.A, s.B
    ps = s.ps
    fe = s.front

    def load(sp, b, p):
        if has_before(b, 2):
            sp.wait_ge(c_ready, b - 1)
        sp.dma_start(s.ctxT_s[:, p, :, :], t["ctxT"][b].rearrange("(c p) k -> p c k", p=P)).then_inc(ct_in[p], 16)

    class prep:
        @staticmethod
        def pe(pe, b, p):
            pe.wait_ge(ct_in[p], 8 * (b - p) + 16)
            if has_before(b, 2):
                pe.wait_ge(res_done, b - 2)
            if has_before(b, 1):
                pe.wait_ge(kf_done, b)
            for c in range(DC):
                last = nc.tensor.matmul(ps[:, B, 0:P], s.ctxT_s[:, p, c, :], s.proj[:, c, :], start=(c == 0), stop=(c == DC - 1))
            last.then_inc(c_ready, 1)
            if has_before(b, 2):
                pe.wait_ge(relu_done, 2 * (b - 2))
            elif b:
                pe.wait_ge(s.max_rows, 1)
            if has_before(b, 1):
                pe.wait_ge(v_done, b)
            nc.tensor.matmul(ps[:, A, :], s.wq0, s.XN[:, b, :], start=True, stop=True).then_inc(q_ready, 1)
            pe.wait_ge(c_taken, b + 1)
            for g in range(4):
                last = nc.tensor.matmul(ps[0:96, B, g * P:(g + 1) * P], s.wk0_rep[:, g, :], s.C[:, :], start=(g == 0), stop=(g == 3), skip_group_check=True)
            last.then_inc(kr_ready, 1)
            pe.wait_ge(qlo_done, b + 1)
            nc.tensor.matmul(ps[:, A, 0:P], s.C[:, :], s.wk0, start=True, stop=True).then_inc(v_ready, 1)

        @staticmethod
        def act(act, b, p):
            act.wait_ge(c_ready, b + 1)
            if has_before(b, 1):
                act.wait_ge(v_ready, b)
            nc.scalar.activation(s.C[:, :], ps[:, B, 0:P], ACT.Copy).then_inc(c_taken, 1)
            act.wait_ge(q_ready, b + 1)
            if has_before(b, 1):
                act.wait_ge(s.q_packed, 192 * b)
            nc.scalar.activation(s.QH[:, :], ps[:, A, :], ACT.Identity, bias=s.cols0[:, 0:1]).then_inc(qhi_done, 1)

        @staticmethod
        def dve(dve, b, p):
            dve.wait_ge(qhi_done, b + 1)
            nc.vector.scalar_tensor_tensor(s.QL[:, :], ps[:, A, :], s.cols0[:, 0:1], s.QH[:, :].bitcast(F32), ALU.add, ALU.subtract).then_inc(qlo_done, 1)
            dve.wait_ge(kr_ready, b + 1)
            for g in range(4):
                last = nc.vector.scalar_tensor_tensor(s.KF[0:96, g, :], s.colsum_row[0:96, :], s.cols0[0:96, 1 + g:2 + g],
                                                      ps[0:96, B, g * P:(g + 1) * P], ALU.mult, ALU.add)
            last.then_inc(kf_done, 1)
            dve.wait_ge(kf_done, b + 1)
            if has_before(b, 1):
                dve.wait_ge(s.kb_ready, b)
            nc.vector.tensor_copy(s.KH[0:96, :, :], s.KF[0:96, :, :]).then_inc(kh_done, 1)
            dve.wait_ge(kh_done, b + 1)
            nc.vector.tensor_tensor(s.KH[32:64, :, :], s.KF[32:64, :, :], s.KH[32:64, :, :], ALU.subtract).then_inc(kx_done, 1)
            dve.wait_ge(v_ready, b + 1)
            nc.vector.scalar_tensor_tensor(s.VS[:, :], s.bk0_row, s.colsum[:, 0:1], ps[:, A, 0:P], ALU.mult, ALU.add).then_inc(v_done, 1)

        @staticmethod
        def pool(pool, b, p):
            spread(nc, s, pool, b, p, 4, s.mask4, kx_done, v_done)

        @staticmethod
        def sp(sp, b, p):
            pack_queries(nc, s, sp, b, p)

    class tail:
        written = res_done

        @staticmethod
        def wait_msg_free(dve, b):
            dve.wait_ge(h_ready, 2 * b)

        @staticmethod
        def pe(pe, b, p):
            pe.wait_ge(s.msg_done, b + 1)
            for h, bank in enumerate((A, B)):
                if h == 0:
                    pe.wait_ge(s.max_rows, b + 2 if symbolic(b) else min(b + 2, NB))
                    pe.wait_ge(relu_done, 2 * b)
                else:
                    pe.wait_ge(kf_done, b + 3 if symbolic(b) else min(b + 3, NB))
                    pe.wait_ge(res_done, b)
                nc.tensor.matmul(ps[:, bank, :], s.w1x0[:, h * P:(h + 1) * P], s.XN[:, b, :], start=True, stop=False)
                nc.tensor.matmul(ps[:, bank, :], s.weff[:, h * P:(h + 1) * P], s.msg[:, :], start=False, stop=True).then_inc(h_ready, 1)
            pe.wait_ge(relu_done, 2 * b + 2)
            nc.tensor.matmul(ps[:, B, :], s.w2_0[:, 0, :], s.H[:, 0, :], start=True, stop=False)
            nc.tensor.matmul(ps[:, B, :], s.w2_0[:, 1, :], s.H[:, 1, :], start=False, stop=True).then_inc(o_ready, 1)

        @staticmethod
        def act(act, b, p):
            act.wait_ge(o_ready, b)
            for h, bank in enumerate((A, B)):
                act.wait_ge(h_ready, 2 * b + h + 1)
                nc.scalar.activation(s.H[:, h, :], ps[:, bank, :], ACT.Relu, bias=s.bn[:, 10 + h:11 + h], scale=s.bn[:, 2 + h:3 + h]).then_inc(relu_done, 1)

        @staticmethod
        def dve(dve, b, p):
            dve.wait_ge(o_ready, b + 1)
            fe.before_write(dve, b, res_done)
            nc.vector.scalar_tensor_tensor(s.X[:, b, :], ps[:, B, :], s.cols0[:, 7:8], s.X[:, b, :], ALU.add, ALU.add).then_inc(res_done, 1)
            fe.after_write(b, p)

    def bank_a(pe, b):
        if not symbolic(b):
            pe.wait_ge(v_done, min(b + 2, NB) if b else 1)
        else:
            pe.wait_ge(v_done, b + 2)
        if has_before(b, 1):
            pe.wait_ge(relu_done, 2 * (b - 1))
    s.wait_bank_a = bank_a
    packed_attention(nc, s, "l0", 4, 8 ** -0.5, load, prep, tail)


def spread(nc, s, pool, b, p, HL, mask, kx_done, v_done):
    W = 32 // HL
    pool.wait_ge(v_done, b + 1)
    if has_before(b, 2):
        pool.wait_ge(s.t_ready, (b - 1) * s.J)
        pool.wait_ge(s.pv_done, (b - 1) * HL)
    pool.wait_ge(kx_done, b + 1)
    for g in range(4):
        part = nc.gpsimd.tensor_tensor(s.KB[0:96, p, g, 0:HL * P].rearrange("p (h k) -> p h k", h=HL),
                                       s.KH[0:96, g, :].bitcast(F32).unsqueeze(1).broadcast_to([96, HL, P]),
                                       mask[0:96].unsqueeze(2).broadcast_to([96, HL, P]), ALU.mult)
        if g == 0:
            part.then_inc(s.q_may_pack, 1)
    for h in range(HL):
        last = nc.gpsimd.tensor_copy(s.VE[:, p, :, h, h * W:(h + 1) * W], s.VS[:, :].rearrange("p (g h d) -> p g h d", g=4, h=HL)[:, :, h, :])
    last.then_inc(s.kb_ready, 1)


def pack_queries(nc, s, sp, b, p):
    sp.wait_ge(s.q_may_pack, b + 1)
    for g in range(4):
        for quadrant, part in enumerate((s.QH, s.QH, s.QL)):
            sp.dma_start(s.Q[32 * quadrant:32 * quadrant + 32, p, g, :].bitcast(F32),
                         part[32 * g:32 * g + 32, :].bitcast(F32)).then_inc(s.q_packed, 16)


class Front:
    def __init__(self, nc, s):
        self.nc, self.s, self.base, self.mbase = nc, s, 0, 0
        sem = s.sem
        self.stats, self.moments, self.eps_added, self.rstd = (sem("fe_" + n) for n in ("stats", "moments", "eps_added", "rstd"))
        self.xn_ready = sem("fe_xn_ready")
        self.turned = sem("fe_turned")
        self.ready = sem("fe_xnT_ready")

    def before_write(self, dve, b, written):
        n = self.mbase + b
        if has_before(b, 1):
            dve.wait_ge(written, b)
            dve.wait_ge(self.stats, n - 1)
        if has_before(b, 2) or self.mbase:
            dve.wait_ge(self.rstd, n - 2)

    def after_write(self, b, p):
        if has_before(b, 1):
            self.dve_stats(b - 1, 1 - p)
        if has_before(b, 2):
            self.dve_moments(p)

    def dve_stats(self, b, p):
        self.nc.vector.bn_stats(self.s.mstats[:, p, :], self.s.X[:, b, :]).then_inc(self.stats, 1)

    def dve_moments(self, p):
        self.nc.vector.bn_aggr(self.s.mmv[:, p, :], self.s.mstats[:, p, :]).then_inc(self.moments, 1)

    def dve_last_moments(self, dve, written):
        n = self.mbase + NB
        dve.wait_ge(written, NB)
        dve.wait_ge(self.rstd, n - 2)
        self.dve_stats(NB - 1, 1)
        dve.wait_ge(self.stats, n - 1)
        self.dve_moments(0)
        dve.wait_ge(self.stats, n)
        self.dve_moments(1)

    def late_waits(self, dve, b, written):
        if has_before(b, 2):
            dve.wait_ge(written, b - 1)
            dve.wait_ge(self.moments, self.mbase + b - 3)

    def late_stats(self, b, p):
        if has_before(b, 2):
            self.dve_stats(b - 2, p)

    def late_before_write(self, dve, b):
        if has_before(b, 2):
            dve.wait_ge(self.stats, self.mbase + b - 1)
            dve.wait_ge(self.rstd, self.mbase + b - 3)

    def late_after_write(self, b, p):
        if has_before(b, 2):
            self.dve_moments(p)

    def late_last_moments(self, dve, written):
        for b in (NB, NB + 1):
            self.late_waits(dve, b, written)
            self.late_stats(b, b % 2)
            self.late_before_write(dve, b)
            self.late_after_write(b, b % 2)

    def dve_all_moments(self, dve, written):
        for b in range(NB):
            dve.wait_ge(written, b + 1)
            if b >= 2:
                dve.wait_ge(self.moments, self.mbase + b - 1)
            self.dve_stats(b, b % 2)
            dve.wait_ge(self.stats, self.mbase + b + 1)
            if b >= 2:
                dve.wait_ge(self.rstd, self.mbase + b - 1)
            self.dve_moments(b % 2)

    def pool_rstd(self, pool, b, p):
        s, n, g = self.s, self.mbase + b, self.nc.gpsimd
        pool.wait_ge(self.moments, n + 1)
        g.tensor_tensor(s.var_eps[:, p:p + 1], s.mmv[:, p, 1:2], s.eps[:, 0:1], ALU.add).then_inc(self.eps_added, 1)
        g.tensor_copy(s.mean[:, b, :], s.mmv[:, p, 0:1])
        pool.wait_ge(self.eps_added, n + 1)
        g.tensor_tensor(s.rstd[:, b, :], s.var_eps[:, p:p + 1], s.minus_half[:, 0:1], ALU.pow).then_inc(self.rstd, 1)

    def dve_normalise(self, dve, b, p):
        s, n = self.s, self.base + b
        if has_before(b, 2):
            dve.wait_ge(self.turned, n - 1)
        self.nc.vector.tensor_scalar(s.xn[:, p, :], s.X[:, b, :], s.mean[:, b, :], s.rstd[:, b, :], ALU.subtract, ALU.mult
                                     ).then_inc(self.xn_ready, 1)

    def pe_turn(self, pe, b, p, bank=0):
        s, n = self.s, self.base + b
        pe.wait_ge(self.xn_ready, n + 1)
        pe.wait_ge(self.ready, n)
        for c in range(DC):
            last = self.nc.tensor.transpose(s.ps[:, bank, c * P:(c + 1) * P], s.xn[:, p, c * P:(c + 1) * P], s.ident)
        last.then_inc(self.turned, 1)


def binary_weights(nc, s, t):
    N = 7168
    PART = 1792
    K = N // PART
    sem = s.sem
    base_in = [sem(f"bw_base_in{m}") for m in range(3)]
    w_in = [sem(f"bw_w_in{q}") for q in range(2)]
    diff_done, sign_done, sums_done, total_done, coeff_done = (sem("bw_" + n) for n in ("diff", "sign", "sums", "total", "coeff"))
    with nc.Block() as block:
        @block.gpsimd
        def _(pool):
            for handle in s.retired:
                pool.sem_clear(handle)

        @block.sync
        def _(sp):
            for m in range(3):
                sp.dma_start(s.WF[:, m, :], t["base"][m]).then_inc(base_in[m], 16)
                for k in range(K):
                    j = K * m + k
                    if j >= 2:
                        sp.wait_ge(sign_done, 2 * (j - 1))
                    sp.dma_start(s.WS[:, j % 2, :], t["w"][m][:, k * PART:(k + 1) * PART]).then_inc(w_in[j % 2], 16)

        @block.vector
        def _(dve):
            for j in range(3 * K):
                m, k = divmod(j, K)
                dve.wait_ge(base_in[m], 16)
                dve.wait_ge(w_in[j % 2], 16 * (j // 2 + 1))
                nc.vector.tensor_tensor(s.WS[:, j % 2, :], s.WS[:, j % 2, :], s.WF[:, m, k * PART:(k + 1) * PART], ALU.subtract).then_inc(diff_done, 1)
            dve.wait_ge(sign_done, 6 * K)
            nc.vector.tensor_reduce(s.wsum[:, 0:3], s.wabs[:, :].rearrange("p (m k) -> p m k", m=3), AX.X, ALU.add).then_inc(sums_done, 1)
            dve.wait_ge(total_done, 1)
            nc.vector.tensor_scalar(s.coeff[:, 0:3], s.ps[:, 0, 0:3], 1.0 / (N * P), None, ALU.mult).then_inc(coeff_done, 1)
            dve.wait_ge(coeff_done, 1)
            for m in range(3):
                nc.vector.scalar_tensor_tensor(s.WF[:, m, :], s.SG[:, m, :], s.coeff[:, m:m + 1], s.WF[:, m, :], ALU.mult, ALU.add).then_inc(coeff_done, 1)

        @block.scalar
        def _(act):
            for j in range(3 * K):
                m, k = divmod(j, K)
                act.wait_ge(diff_done, j + 1)
                nc.scalar.activation(s.SG[:, m, k * PART:(k + 1) * PART], s.WS[:, j % 2, :], ACT.Sign).then_inc(sign_done, 1)
                if j:
                    act.wait_ge(sign_done, 2 * j)
                nc.scalar.activation(s.wscr[:, :], s.WS[:, j % 2, :], ACT.Abs, accum_out=s.wabs[:, j:j + 1]).then_inc(sign_done, 1)

        @block.tensor
        def _(pe):
            pe.wait_ge(sums_done, 1)
            nc.tensor.matmul(s.ps[:, 0, 0:3], s.ones[:, :], s.wsum[:, 0:3], start=True, stop=True).then_inc(total_done, 1)


def gated_ffn(nc, s, t):
    sem = s.sem
    fe = s.front
    I = 14
    g_ready, u_ready, silu_done, h_done, o_ready, res_done = (sem("ff_" + n) for n in ("gate", "up", "silu", "hidden", "out", "res"))
    xt_taken = sem("ff_xt_taken")
    W1 = s.WF[:, 0, :].rearrange("p (c i) -> p c i", c=DC)
    W3 = s.WF[:, 1, :].rearrange("p (c i) -> p c i", c=DC)
    W2 = s.WF[:, 2, :].rearrange("p (c d) -> p c d", c=I)
    with nc.Block() as block:
        @block.vector
        def _(dve):
            slots(dve, lambda b, p: fe.dve_normalise(dve, b, p))

        @block.tensor
        def _(pe):
            slots(pe, lambda b, p: fe.pe_turn(pe, b, p))

        @block.scalar
        def _(act):
            def slot(b, p):
                act.wait_ge(fe.turned, fe.base + b + 1)
                nc.scalar.activation(s.XNT[:, :, b, :], s.ps[:, 0, :].rearrange("p (c t) -> p c t", c=DC), ACT.Copy).then_inc(fe.ready, 1)
            slots(act, slot)
    with nc.Block() as block:
        @block.tensor
        def _(pe):
            def gate_up(h, j):
                n = h * I + j
                rhs = lambda c: s.XNT[:, c, :, :].rearrange("p (h b) t -> p h (b t)", h=2)[:, h, :]
                if j >= 2:
                    pe.wait_ge(silu_done, n - 1)
                for c in range(DC):
                    last = nc.tensor.matmul(s.ps[:, j % 2, :], W1[:, c, j * P:(j + 1) * P], rhs(c), start=(c == 0), stop=(c == DC - 1))
                last.then_inc(g_ready, 1)
                if j >= 2:
                    pe.wait_ge(h_done, n - 1)
                for c in range(DC):
                    last = nc.tensor.matmul(s.ps[:, 2 + j % 2, :], W3[:, c, j * P:(j + 1) * P], rhs(c), start=(c == 0), stop=(c == DC - 1))
                last.then_inc(u_ready, 1)

            def down(h, j):
                pe.wait_ge(h_done, h * I + j + 1)
                for q in range(4):
                    last = nc.tensor.matmul(s.ps[:, 4 + q, :], s.HT[:, j % 2, q * P:(q + 1) * P], W2[:, j, :], start=(j == 0), stop=(j == I - 1))
                last.then_inc(o_ready, 1)

            with pe.Fori(0, 2) as h:
                gate_up(h, 0)
                for j in range(1, I):
                    gate_up(h, j)
                    down(h, j - 1)
                down(h, I - 1)

        @block.scalar
        def _(act):
            with act.Fori(0, 2) as h:
                for j in range(I):
                    act.wait_ge(g_ready, h * I + j + 1)
                    if j >= 2:
                        act.wait_ge(h_done, h * I + j - 1)
                    nc.scalar.activation(s.SL[:, j % 2, :], s.ps[:, j % 2, :], ACT.Silu).then_inc(silu_done, 1)

        @block.vector
        def _(dve):
            with dve.Fori(0, 2) as h:
                for j in range(I):
                    dve.wait_ge(silu_done, h * I + j + 1)
                    dve.wait_ge(u_ready, h * I + j + 1)
                    if j >= 2:
                        dve.wait_ge(o_ready, h * I + j - 1)
                    nc.vector.tensor_tensor(s.HT[:, j % 2, :], s.ps[:, 2 + j % 2, :], s.SL[:, j % 2, :], ALU.mult).then_inc(h_done, 1)
                dve.wait_ge(o_ready, h * I + I)
                for q in range(4):
                    nc.vector.tensor_tensor(s.X[:, 4 * h + q, :], s.X[:, 4 * h + q, :], s.ps[:, 4 + q, :], ALU.add).then_inc(res_done, 1)
            fe.dve_all_moments(dve, res_done)

        @block.gpsimd
        def _(pool):
            slots(pool, lambda b, p: fe.pool_rstd(pool, b, p))
    fe.base += NB
    fe.mbase += NB


def fold_text_attention(nc, s, t):
    sem = s.sem
    w_in, mt_ready, mt_taken, g_ready, g_taken, v_ready, v_taken, step = (sem("fa_" + n) for n in (
        "w_in", "mt_ready", "mt_taken", "g_ready", "g_taken", "v_ready", "v_taken", "step"))
    WQ, WK, MT = s.wq1, s.wk1, s.mt1
    loads = [(WQ[:, :, :], t["wq1"]), (WK[:, :, :], t["wk1"]), (s.cols1[:, :], t["cols1"]),
             (s.ctxT[:, :, :, :], t["ctxT_all"]), (s.ctx[:, :, :], t["ctx"])]
    with nc.Block() as block:
        @block.sync
        def _(sp):
            for to, of in loads:
                sp.dma_start(to, of).then_inc(w_in, 16)

        @block.tensor
        def _(pe):
            pe.wait_ge(w_in, 16 * len(loads))
            for y in range(DC):
                for c in range(DC):
                    nc.tensor.matmul(s.ps[:, 7, y:y + 1], WK[:, c, y * P:(y + 1) * P], s.cols1[:, c:c + 1], start=(y == 0 and c == 0), stop=False, skip_group_check=True)
            for y in range(DC):
                for c in range(DC):
                    last = nc.tensor.matmul(s.ps[:, 7, 4 + y:5 + y], WQ[:, c, y * P:(y + 1) * P], s.cols1[:, 4 + c:5 + c], start=False, stop=(y == DC - 1 and c == DC - 1), skip_group_check=True)
            last.then_inc(v_ready, 1)
            for y in range(DC):
                for c in range(DC):
                    last = nc.tensor.matmul(s.ps[:, y, :], WK[:, c, y * P:(y + 1) * P], WQ[:, c, :], start=(c == 0), stop=(c == DC - 1))
                last.then_inc(mt_ready, 1)
            pe.wait_ge(v_taken, 2)
            nc.tensor.matmul(s.ps[:, 7, 8:9], s.ones[:, :], s.bqk[:, 0:1], start=True, stop=True).then_inc(v_ready, 1)
            pe.wait_ge(mt_taken, DC)
            for n in range(2 * DC):
                x, h = divmod(n, 2)
                if n >= 2:
                    pe.wait_ge(g_taken, n - 1)
                for c in range(DC):
                    last = nc.tensor.matmul(s.ps[:, 4 + n % 2, :], MT[:, c, x * P:(x + 1) * P], s.ctxT[:, c, 4 * h:4 * h + 4, :].rearrange("p b k -> p (b k)"), start=(c == 0), stop=(c == DC - 1))
                last.then_inc(g_ready, 1)
            pe.wait_ge(v_taken, 4)
            for h in range(2):
                pe.wait_ge(g_taken, 2 * DC - 1 + h)
                for c in range(DC):
                    last = nc.tensor.matmul(s.ps[:, 4 + h, :], s.vrep[:, c, :], s.ctxT[:, c, 4 * h:4 * h + 4, :].rearrange("p b k -> p (b k)"), start=(c == 0), stop=(c == DC - 1))
                last.then_inc(g_ready, 1)

        @block.scalar
        def _(act):
            for y in range(DC):
                act.wait_ge(mt_ready, y + 1)
                nc.scalar.activation(MT[:, y, :], s.ps[:, y, :], ACT.Copy).then_inc(mt_taken, 1)

        @block.vector
        def _(dve):
            dve.wait_ge(w_in, 16 * len(loads))
            nc.vector.tensor_tensor(s.bqk[:, 4:8], s.cols1[:, 0:4], s.cols1[:, 4:8], ALU.mult).then_inc(step, 1)
            dve.wait_ge(step, 1)
            nc.vector.tensor_reduce(s.bqk[:, 0:1], s.bqk[:, 4:8], AX.X, ALU.add).then_inc(v_taken, 1)
            dve.wait_ge(v_ready, 1)
            nc.vector.tensor_copy(s.v1[:, :], s.ps[:, 7, 0:8]).then_inc(v_taken, 1)
            dve.wait_ge(v_ready, 2)
            nc.vector.tensor_copy(s.bqk[:, 1:2], s.ps[:, 7, 8:9]).then_inc(v_taken, 1)
            dve.wait_ge(v_taken, 3)
            for c in range(DC):
                last = nc.vector.tensor_copy(s.vrep[:, c, :], s.v1[:, c:c + 1].broadcast_to([P, P]))
            last.then_inc(v_taken, 1)
            for n in range(2 * DC):
                x, h = divmod(n, 2)
                dve.wait_ge(g_ready, n + 1)
                nc.vector.tensor_scalar(s.G[:, x, 4 * h:4 * h + 4, :].rearrange("p b k -> p (b k)"), s.ps[:, 4 + n % 2, :], s.v1[:, 4 + x:5 + x], None, ALU.add).then_inc(g_taken, 1)
            for h in range(2):
                dve.wait_ge(g_ready, 2 * DC + 1 + h)
                nc.vector.tensor_scalar(s.R[:, 4 * h:4 * h + 4, :].rearrange("p b k -> p (b k)"), s.ps[:, 4 + h, :], s.bqk[:, 1:2], None, ALU.add).then_inc(g_taken, 1)


def context_attention(nc, s, name, KT, R, scale):
    sem = s.sem
    fe = s.front
    s_ready, r_added, max_done, neg_done, e_done, et_ready, et_taken, den_done, o_ready, res_done = (sem(name + n) for n in (
        "_s_ready", "_r_added", "_max", "_neg", "_e", "_et_ready", "_et_taken", "_den", "_o_ready", "_res"))
    SC, OUT, ET = (1, 2), (4, 5), 3
    with nc.Block() as block:
        @block.gpsimd
        def _(pool):
            slots(pool, lambda b, p: fe.pool_rstd(pool, b, p))

        @block.tensor
        def _(pe):
            def turn_weights(b, p):
                pe.wait_ge(e_done, b + 1)
                pe.wait_ge(et_taken, b)
                nc.tensor.transpose(s.ps[:, ET, 0:P], s.E[:, p, :], s.ident).then_inc(et_ready, 1)

            def out(b, p):
                pe.wait_ge(et_taken, b + 1)
                if has_before(b, 2):
                    pe.wait_ge(res_done, b - 1)
                nc.tensor.matmul(s.ps[:, OUT[p], :], s.EWT[:, p, :], s.ctx[:, b, :], start=True, stop=True).then_inc(o_ready, 1)

            def slot(b, p):
                if has_before(b, 1):
                    turn_weights(b - 1, 1 - p)
                pe.wait_ge(fe.ready, fe.base + b + 1)
                if has_before(b, 2):
                    pe.wait_ge(e_done, b - 1)
                for c in range(DC):
                    last = nc.tensor.matmul(s.ps[:, SC[p], 0:P], s.xnT[:, p, c, :], KT[:, c, b, :], start=(c == 0), stop=(c == DC - 1))
                last.then_inc(s_ready, 1)
                if has_after(b, 2):
                    fe.pe_turn(pe, b + 2, p)
                if has_before(b, 1):
                    out(b - 1, 1 - p)
            fe.pe_turn(pe, 0, 0)
            fe.pe_turn(pe, 1, 1)
            slots(pe, slot)
            turn_weights(NB - 1, 1)
            out(NB - 1, 1)

        @block.scalar
        def _(act):
            def take_weights(b, p):
                act.wait_ge(et_ready, b + 1)
                if has_before(b, 2):
                    act.wait_ge(o_ready, b - 1)
                nc.scalar.activation(s.EWT[:, p, :], s.ps[:, ET, 0:P], ACT.Copy).then_inc(et_taken, 1)

            def take(b, p):
                act.wait_ge(fe.turned, fe.base + b + 1)
                if has_before(b, 2):
                    act.wait_ge(s_ready, b - 1)
                nc.scalar.activation(s.xnT[:, p, :, :].rearrange("p c t -> p (c t)"), s.ps[:, 0, :], ACT.Copy).then_inc(fe.ready, 1)

            def slot(b, p):
                if has_before(b, 1):
                    take_weights(b - 1, 1 - p)
                act.wait_ge(neg_done, b + 1)
                if has_before(b, 2):
                    act.wait_ge(et_ready, b - 1)
                    act.wait_ge(res_done, b - 1)
                source = s.SR[:, p, :] if R is not None else s.ps[:, SC[p], 0:P]
                nc.scalar.activation(s.E[:, p, :], source, ACT.Exp, bias=s.negm[:, p:p + 1], scale=scale, accum_out=s.den[:, p:p + 1]).then_inc(e_done, 1)
                if has_after(b, 2):
                    take(b + 2, p)
            take(0, 0)
            take(1, 1)
            slots(act, slot)
            take_weights(NB - 1, 1)

        @block.vector
        def _(dve):
            def add(b, p):
                dve.wait_ge(o_ready, b + 1)
                nc.vector.scalar_tensor_tensor(s.X[:, b, :], s.ps[:, OUT[p], :], s.rd[:, p:p + 1], s.X[:, b, :], ALU.mult, ALU.add).then_inc(res_done, 1)

            def invert(b, p):
                dve.wait_ge(e_done, b + 1)
                if has_before(b, 2):
                    dve.wait_ge(res_done, b - 1)
                nc.vector.reciprocal(s.rd[:, p:p + 1], s.den[:, p:p + 1]).then_inc(den_done, 1)
                dve.wait_ge(den_done, b + 1)

            def slot(b, p):
                dve.wait_ge(s_ready, b + 1)
                if R is not None:
                    if has_before(b, 2):
                        dve.wait_ge(e_done, b - 1)
                    nc.vector.tensor_tensor(s.SR[:, p, :], s.ps[:, SC[p], 0:P], R[:, b, :], ALU.add).then_inc(r_added, 1)
                    dve.wait_ge(r_added, b + 1)
                source = s.SR[:, p, :] if R is not None else s.ps[:, SC[p], 0:P]
                if has_before(b, 1):
                    dve.wait_ge(neg_done, b)
                fe.late_waits(dve, b, res_done)
                nc.vector.tensor_reduce(s.smax[:, p:p + 1], source, AX.X, ALU.max).then_inc(max_done, 1)
                fe.late_stats(b, p)
                dve.wait_ge(max_done, b + 1)
                if has_before(b, 2):
                    dve.wait_ge(e_done, b - 1)
                nc.vector.tensor_scalar(s.negm[:, p:p + 1], s.smax[:, p:p + 1], -scale, None, ALU.mult).then_inc(neg_done, 1)
                if has_before(b, 1):
                    invert(b - 1, 1 - p)
                if has_after(b, 2):
                    fe.dve_normalise(dve, b + 2, p)
                if has_before(b, 1):
                    fe.late_before_write(dve, b)
                    add(b - 1, 1 - p)
                    fe.late_after_write(b, p)
            for b in range(2):
                fe.dve_normalise(dve, b, b)
            slots(dve, slot)
            invert(NB - 1, 1)
            add(NB - 1, 1)
            fe.late_last_moments(dve, res_done)
    fe.base += NB
    fe.mbase += NB


def dense(nc, s, name, W, AG, bias, out=None):
    sem = s.sem
    fe = s.front
    y_ready, ag_ready, ag_taken, bias_done, res_done = (sem(name + n) for n in ("_y", "_ag", "_ag_taken", "_bias", "_res"))
    with nc.Block() as block:
        if out is not None:
            @block.sync
            def _(sp):
                with sp.Fori(0, NB) as b:
                    sp.wait_ge(res_done, b + 1)
                    sp.dma_start(out[b], s.X[:, b, :]).then_inc(s.x_out, 16)
                sp.wait_ge(s.x_out, 16 * NB)

        @block.gpsimd
        def _(pool):
            def slot(b, p):
                pool.wait_ge(fe.xn_ready, fe.base + b + 1)
                nc.gpsimd.tensor_tensor(s.X[:, b, :], s.X[:, b, :], bias, ALU.add).then_inc(bias_done, 1)
            if bias is not None:
                slots(pool, slot)

        @block.tensor
        def _(pe):
            def slot(b, p):
                pe.wait_ge(fe.ready, fe.base + b + 1)
                if AG is not None:
                    if has_before(b, 2):
                        pe.wait_ge(ag_taken, b - 1)
                    for c in range(DC):
                        last = nc.tensor.matmul(s.ps[:, 3 + p, 0:160], s.xnT[:, p, c, :], AG[:, c, :], start=(c == 0), stop=(c == DC - 1))
                    last.then_inc(ag_ready, 1)
                if has_before(b, 2):
                    pe.wait_ge(res_done, b - 1)
                for c in range(DC):
                    last = nc.tensor.matmul(s.ps[:, 1 + p, :], s.xnT[:, p, c, :], W[:, c, :], start=(c == 0), stop=(c == DC - 1))
                last.then_inc(y_ready, 1)
                if has_after(b, 2):
                    fe.pe_turn(pe, b + 2, p)
            fe.pe_turn(pe, 0, 0)
            fe.pe_turn(pe, 1, 1)
            slots(pe, slot)

        @block.scalar
        def _(act):
            def take(b, p):
                act.wait_ge(fe.turned, fe.base + b + 1)
                if has_before(b, 2):
                    act.wait_ge(y_ready, b - 1)
                nc.scalar.activation(s.xnT[:, p, :, :].rearrange("p c t -> p (c t)"), s.ps[:, 0, :], ACT.Copy).then_inc(fe.ready, 1)

            def slot(b, p):
                if AG is not None:
                    act.wait_ge(ag_ready, b + 1)
                    nc.scalar.activation(s.AGS[:, b, :], s.ps[:, 3 + p, 0:160], ACT.Copy).then_inc(ag_taken, 1)
                if has_after(b, 2):
                    take(b + 2, p)
            take(0, 0)
            take(1, 1)
            slots(act, slot)

        @block.vector
        def _(dve):
            def slot(b, p):
                if has_after(b, 2):
                    fe.dve_normalise(dve, b + 2, p)
                dve.wait_ge(y_ready, b + 1)
                if bias is not None:
                    dve.wait_ge(bias_done, b + 1)
                nc.vector.tensor_tensor(s.X[:, b, :], s.ps[:, 1 + p, :], s.X[:, b, :], ALU.add).then_inc(res_done, 1)
            for b in range(2):
                fe.dve_normalise(dve, b, b)
            slots(dve, slot)
    fe.base += NB


def expert_gates(nc, s, t):
    E, GH, R = 8, 32, 16
    CAPACITY = int(3.0 * NB * P / E)
    step, var_ready, rstd_ready, gap_ready, exp_ready, mine_ready, all_ready = (s.sem("eg_" + n) for n in (
        "step", "var", "rstd", "gap", "exp", "mine", "all"))
    row = s.rows1
    gb1, gamma, beta = (row[:, 32 * k:32 * k + 32].unsqueeze(1).broadcast_to([P, NB, GH]) for k in range(3))
    gw2 = row[:, 96:352].rearrange("p (e j) -> p e j", e=E).unsqueeze(1).broadcast_to([P, NB, E, GH])
    gb2 = row[:, 352:360].unsqueeze(1).broadcast_to([P, NB, E])
    first = row[:, 360:368].unsqueeze(1).broadcast_to([P, NB, E])
    h, sm = s.gh, s.gsm
    over_h = lambda k: sm[:, k, :].unsqueeze(2).broadcast_to([P, NB, GH])
    over_e = lambda k: sm[:, k, :].unsqueeze(2).broadcast_to([P, NB, E])
    g = lambda k: s.gg[:, k, :, :]
    with nc.Block() as block:
        @block.vector
        def _(dve):
            link = linked(dve, step)
            v = nc.vector
            link(v.tensor_tensor(h[:, :, :], s.AGS[:, :, 128:160], gb1, ALU.add))
            link(v.tensor_reduce(sm[:, 0, :], h[:, :, :], AX.X, ALU.add))
            link(v.tensor_scalar(sm[:, 1, :], sm[:, 0, :], 1.0 / GH, None, ALU.mult))
            link(v.tensor_tensor(h[:, :, :], h[:, :, :], over_h(1), ALU.subtract))
            link(v.tensor_tensor(s.gprod[:, :, 0, :], h[:, :, :], h[:, :, :], ALU.mult))
            link(v.tensor_reduce(sm[:, 2, :], s.gprod[:, :, 0, :], AX.X, ALU.add))
            v.tensor_scalar(sm[:, 3, :], sm[:, 2, :], 1.0 / GH, LN_EPS, ALU.mult, ALU.add).then_inc(var_ready, 1)
            dve.wait_ge(rstd_ready, 1)
            link(v.tensor_tensor(h[:, :, :], h[:, :, :], over_h(4), ALU.mult))
            link(v.tensor_tensor(h[:, :, :], h[:, :, :], gamma, ALU.mult))
            link(v.tensor_tensor(h[:, :, :], h[:, :, :], beta, ALU.add))
            link(v.tensor_scalar(h[:, :, :], h[:, :, :], 0.0, None, ALU.max))
            link(v.tensor_tensor(s.gprod[:, :, :, :], h[:, :, :].unsqueeze(2).broadcast_to([P, NB, E, GH]), gw2, ALU.mult))
            link(v.tensor_reduce(g(0), s.gprod[:, :, :, :], AX.X, ALU.add))
            link(v.tensor_tensor(g(0), g(0), gb2, ALU.add))
            for k in range(2):
                link(v.tensor_reduce(sm[:, 5 + k, :], g(0), AX.X, ALU.max))
                link(v.tensor_tensor(g(3), g(0), over_e(5 + k), ALU.is_equal))
                link(v.tensor_tensor(g(3), g(3), first, ALU.mult))
                link(v.tensor_reduce(sm[:, 7, :], g(3), AX.X, ALU.max))
                link(v.tensor_tensor(g(1 + k), g(3), over_e(7), ALU.is_equal))
                link(v.tensor_reduce(s.gcount[:, k, :], g(1 + k).rearrange("p b e -> p e b"), AX.X, ALU.add))
                if k == 0:
                    link(v.scalar_tensor_tensor(g(0), g(1), -1e30, g(0), ALU.mult, ALU.add))
            v.tensor_tensor(sm[:, 8, :], sm[:, 6, :], sm[:, 5, :], ALU.subtract).then_inc(gap_ready, 1)
            dve.wait_ge(exp_ready, 1)
            link(v.tensor_scalar(sm[:, 10, :], sm[:, 9, :], 1.0, None, ALU.add))
            link(v.reciprocal(sm[:, 11, :], sm[:, 10, :]))
            link(v.tensor_tensor(sm[:, 12, :], sm[:, 9, :], sm[:, 11, :], ALU.mult))
            dve.wait_ge(all_ready, 1)
            link(v.tensor_scalar(s.gallow[:, :], s.ps[:, 7, 0:16], float(CAPACITY), 1.0 / R, ALU.is_le, ALU.mult))
            for k in range(2):
                link(v.tensor_tensor(g(1 + k), g(1 + k), over_e(11 + k), ALU.mult))
                link(v.tensor_tensor(g(1 + k), g(1 + k), s.gallow[:, 8 * k:8 * k + 8].unsqueeze(1).broadcast_to([P, NB, E]), ALU.mult))
            link(v.tensor_tensor(s.gw[:, :, :], g(1), g(2), ALU.add))

        @block.gpsimd
        def _(pool):
            pool.wait_ge(var_ready, 1)
            nc.gpsimd.tensor_tensor(sm[:, 4, :], sm[:, 3, :], s.minus_half[:, :], ALU.pow).then_inc(rstd_ready, 1)

        @block.scalar
        def _(act):
            act.wait_ge(gap_ready, 1)
            nc.scalar.activation(sm[:, 9, :], sm[:, 8, :], ACT.Exp).then_inc(exp_ready, 1)

        @block.tensor
        def _(pe):
            pe.wait_ge(gap_ready, 1)
            nc.tensor.matmul(s.ps[:, 7, 0:16], s.ones[:, :], s.gcount[:, :, :].rearrange("p k e -> p (k e)"), start=True, stop=True).then_inc(all_ready, 1)

    fe = s.front
    tw_ready, tw_turned, tw_taken, y_ready, res_done = (s.sem("ex_" + n) for n in ("tw", "turned", "taken", "y", "res"))
    with nc.Block() as block:
        @block.vector
        def _(dve):
            def weigh(b, p):
                if has_before(b, 2):
                    dve.wait_ge(tw_turned, b - 1)
                nc.vector.tensor_tensor(s.tw[:, p, :].rearrange("p (e r) -> p e r", e=E), s.AGS[:, b, 0:128].rearrange("p (e r) -> p e r", e=E),
                                        s.gw[:, b, :].unsqueeze(2).broadcast_to([P, E, R]), ALU.mult).then_inc(tw_ready, 1)

            def slot(b, p):
                if has_after(b, 2):
                    weigh(b + 2, p)
                dve.wait_ge(y_ready, b + 1)
                fe.before_write(dve, b, res_done)
                nc.vector.tensor_tensor(s.X[:, b, :], s.ps[:, 2 + p, :], s.X[:, b, :], ALU.add).then_inc(res_done, 1)
                fe.after_write(b, p)
            weigh(0, 0)
            weigh(1, 1)
            slots(dve, slot)
            fe.dve_last_moments(dve, res_done)

        @block.gpsimd
        def _(pool):
            slots(pool, lambda b, p: fe.pool_rstd(pool, b, p))

        @block.tensor
        def _(pe):
            def turn(b, p):
                pe.wait_ge(tw_ready, b + 1)
                if has_before(b, 2):
                    pe.wait_ge(tw_taken, b - 1)
                nc.tensor.transpose(s.ps[:, p, 0:P], s.tw[:, p, :], s.ident).then_inc(tw_turned, 1)

            def slot(b, p):
                if has_after(b, 1):
                    turn(b + 1, 1 - p)
                pe.wait_ge(tw_taken, b + 1)
                if has_before(b, 2):
                    pe.wait_ge(res_done, b - 1)
                nc.tensor.matmul(s.ps[:, 2 + p, :], s.twT[:, p, :], s.lB1, start=True, stop=True).then_inc(y_ready, 1)
            turn(0, 0)
            slots(pe, slot)

        @block.scalar
        def _(act):
            def slot(b, p):
                act.wait_ge(tw_turned, b + 1)
                if has_before(b, 2):
                    act.wait_ge(y_ready, b - 1)
                nc.scalar.activation(s.twT[:, p, :], s.ps[:, p, 0:P], ACT.Copy).then_inc(tw_taken, 1)
            slots(act, slot)
    fe.mbase += NB


def grouped_query_attention(nc, s, t):
    sem = s.sem
    ct_in, w_in = (sem("l2_ct_in0"), sem("l2_ct_in1")), sem("l2_w_in")
    xn_ready, xt_ready, xt_taken, q_ready, qhi_done, qlo_done, kr_ready, khi_done, kx_done, v_ready, v_done = (sem("l2_" + n) for n in (
        "xn", "xt_ready", "xt_taken", "q_ready", "qhi", "qlo", "kr_ready", "khi", "kx", "v_ready", "v_done"))
    o_ready, res_done = sem("l2_o_ready"), sem("l2_res")
    cleared = sem("l2_cleared")
    A, B, ps, fe = s.A, s.B, s.ps, s.front
    loads = [(s.wq2[:, :, :, :], t["wq2"]), (s.wk2[:, :, :, :], t["wk2"]), (s.wv2[:, :, :], t["wv2"]), (s.wo2[:, :, :], t["wo2"]), (s.neg[96:128], t["neg2"])]
    with nc.Block() as block:
        @block.sync
        def _(sp):
            for to, of in loads:
                sp.dma_start(to, of).then_inc(w_in, 16)

        @block.gpsimd
        def _(pool):
            nc.gpsimd.memset(s.mrow[:, :].bitcast(F32), 0.0).then_inc(cleared, 1)
            nc.gpsimd.memset(s.VE[:, :, :, :, :], 0.0).then_inc(cleared, 1)

        @block.vector
        def _(dve):
            dve.wait_ge(w_in, 16 * len(loads))
            for p in range(2):
                nc.vector.tensor_copy(s.KB[96:128, p, :, :], s.neg[96:128, :, :]).then_inc(cleared, 1)

    def load(sp, b, p):
        if has_before(b, 2):
            sp.wait_ge(v_ready, b - 1)
        sp.dma_start(s.ctxT_s[:, p, :, :], t["ctxT"][b].rearrange("(c p) k -> p c k", p=P)).then_inc(ct_in[p], 16)

    class prep:
        @staticmethod
        def pe(pe, b, p):
            pe.wait_ge(xn_ready, b + 1)
            if has_before(b, 2):
                pe.wait_ge(res_done, b - 2)
            if has_before(b, 1):
                pe.wait_ge(kx_done, b)
            for c in range(DC):
                last = nc.tensor.transpose(ps[:, B, c * P:(c + 1) * P], s.xn[:, 0, c * P:(c + 1) * P], s.ident)
            last.then_inc(xt_ready, 1)
            pe.wait_ge(xt_taken, b + 1)
            if has_before(b, 1):
                pe.wait_ge(s.max_rows, b - 1 if has_before(b, 2) else 1)
            if has_before(b, 1):
                pe.wait_ge(v_done, b)
            for r in range(4):
                for c in range(DC):
                    last = nc.tensor.matmul(ps[:, A, r * P:(r + 1) * P], s.wq2[:, c, r, :], s.xnT[:, 0, c, :], start=(c == 0), stop=(c == DC - 1))
            last.then_inc(q_ready, 1)
            pe.wait_ge(ct_in[p], 8 * (b - p) + 16)
            for g in range(4):
                for c in range(DC):
                    last = nc.tensor.matmul(ps[0:96, B, g * P:(g + 1) * P], s.wk2[:, c, g, :], s.ctxT_s[:, p, c, :], start=(c == 0), stop=(c == DC - 1))
            last.then_inc(kr_ready, 1)
            pe.wait_ge(qlo_done, b + 1)
            for c in range(DC):
                last = nc.tensor.matmul(ps[:, A, 0:P], s.ctxT_s[:, p, c, :], s.wv2[:, c, :], start=(c == 0), stop=(c == DC - 1))
            last.then_inc(v_ready, 1)

        @staticmethod
        def act(act, b, p):
            act.wait_ge(xt_ready, b + 1)
            if has_before(b, 1):
                act.wait_ge(q_ready, b)
            nc.scalar.activation(s.xnT[:, 0, :, :].rearrange("p c t -> p (c t)"), ps[:, B, :], ACT.Copy).then_inc(xt_taken, 1)
            act.wait_ge(q_ready, b + 1)
            if has_before(b, 1):
                act.wait_ge(s.q_packed, 192 * b)
            nc.scalar.activation(s.QH[:, :], ps[:, A, :], ACT.Copy).then_inc(qhi_done, 1)

        @staticmethod
        def dve(dve, b, p):
            if has_before(b, 1):
                dve.wait_ge(xt_ready, b)
            nc.vector.tensor_scalar(s.xn[:, 0, :], s.X[:, b, :], s.mean[:, b, :], s.rstd[:, b, :], ALU.subtract, ALU.mult).then_inc(xn_ready, 1)
            dve.wait_ge(qhi_done, b + 1)
            nc.vector.tensor_tensor(s.QL[:, :], ps[:, A, :], s.QH[:, :].bitcast(F32), ALU.subtract).then_inc(qlo_done, 1)
            dve.wait_ge(kr_ready, b + 1)
            if has_before(b, 1):
                dve.wait_ge(s.kb_ready, b)
            nc.vector.tensor_copy(s.KH[0:96, :, :].rearrange("p g k -> p (g k)"), ps[0:96, B, :]).then_inc(khi_done, 1)
            dve.wait_ge(khi_done, b + 1)
            nc.vector.tensor_tensor(s.KH[32:64, :, :].rearrange("p g k -> p (g k)"), ps[32:64, B, :],
                                    s.KH[32:64, :, :].rearrange("p g k -> p (g k)").bitcast(F32), ALU.subtract).then_inc(kx_done, 1)
            dve.wait_ge(v_ready, b + 1)
            nc.vector.tensor_copy(s.VS[:, :], ps[:, A, 0:P]).then_inc(v_done, 1)

        @staticmethod
        def pool(pool, b, p):
            spread(nc, s, pool, b, p, 2, s.mask2, kx_done, v_done)

        @staticmethod
        def sp(sp, b, p):
            pack_queries(nc, s, sp, b, p)

    class tail:
        written = res_done

        @staticmethod
        def wait_msg_free(dve, b):
            dve.wait_ge(o_ready, b)

        @staticmethod
        def pe(pe, b, p):
            pe.wait_ge(s.msg_done, b + 1)
            pe.wait_ge(kx_done, b + 3 if symbolic(b) else min(b + 3, NB))
            pe.wait_ge(res_done, b)
            for r in range(4):
                last = nc.tensor.matmul(ps[:, B, :], s.msg[:, r * P:(r + 1) * P], s.wo2[:, r, :], start=(r == 0), stop=(r == 3))
            last.then_inc(o_ready, 1)

        @staticmethod
        def act(act, b, p):
            pass

        @staticmethod
        def dve(dve, b, p):
            dve.wait_ge(o_ready, b + 1)
            fe.before_write(dve, b, res_done)
            nc.vector.tensor_tensor(s.X[:, b, :], ps[:, B, :], s.X[:, b, :], ALU.add).then_inc(res_done, 1)
            fe.after_write(b, p)

    def bank_a(pe, b):
        if symbolic(b):
            pe.wait_ge(v_done, b + 2)
        else:
            pe.wait_ge(v_done, min(b + 2, NB) if b else 1)
        if symbolic(b) or b:
            pe.wait_ge(s.max_rows, b)
    s.wait_bank_a = bank_a
    packed_attention(nc, s, "l2", 2, 16 ** -0.5, load, prep, tail)


def routed_ffn(nc, s, t):
    E, R = 16, 8
    sem = s.sem
    fe = s.front
    step, log_done = sem("rf_step"), sem("rf_log")
    w_in = sem("rf_w_in")
    (y_open, y_ready, zl_ready, l_done, max_done, neg_done, exp_done, c_done, sum_done, inv_done, alpha_done, zw_done, z_turned, z_taken,
     bias_done, res_done) = (sem("rf_" + n) for n in ("y_open", "y", "zl", "l", "max", "neg", "exp", "c", "sum", "inv", "alpha", "zw", "turned", "taken", "bias", "res"))
    loads = [(s.w2f[:, :, :], t["w2f"]), (s.zl2[:, :, :], t["zl2"]), (s.lB2, t["lB2"]), (s.rows2[:, 0:512], t["b_base"].broadcast_to([P, D])),
             (s.rows2[:, 512:560], t["rows2"].broadcast_to([P, 48])), (s.active[:, :], t["active"].broadcast_to([P, 4]))]
    iota, rb, prior = (s.rows2[:, 512 + 16 * k:528 + 16 * k] for k in range(3))
    with nc.Block() as block:
        @block.sync
        def _(sp):
            for to, of in loads:
                sp.dma_start(to, of).then_inc(w_in, 16)

        @block.scalar
        def _(act):
            act.wait_ge(step, 1)
            nc.scalar.activation(s.ladj[:, 1, :], s.ladj[:, 0, :], ACT.Ln).then_inc(log_done, 1)

        @block.vector
        def _(dve):
            link = linked(dve, step)
            dve.wait_ge(w_in, 16 * len(loads))
            link(nc.vector.tensor_scalar(s.ladj[:, 0, :], prior, 1e-12, None, ALU.add))
            link(nc.vector.tensor_copy(s.activef[:, :], s.active[:, :]))
            link(nc.vector.tensor_scalar(s.cnt[:, :], iota, s.activef[:, 0:1], None, ALU.is_equal))
            for j in range(1, 4):
                link(nc.vector.scalar_tensor_tensor(s.cnt[:, :], iota, s.activef[:, j:j + 1], s.cnt[:, :], ALU.is_equal, ALU.add))
            link(nc.vector.tensor_scalar(s.ladj[:, 2, :], s.cnt[:, :], 0.0, -1e30, ALU.is_equal, ALU.mult))
            link(nc.vector.tensor_tensor(s.ladj[:, 3, :], s.ladj[:, 2, :], rb, ALU.add))
            dve.wait_ge(log_done, 1)
            link(nc.vector.tensor_tensor(s.ladj[:, 4, :], s.ladj[:, 3, :], s.ladj[:, 1, :], ALU.add))

    with nc.Block() as block:
        @block.gpsimd
        def _(pool):
            def slot(b, p):
                pool.wait_ge(fe.xn_ready, fe.base + b + 1)
                nc.gpsimd.tensor_tensor(s.X[:, b, :], s.X[:, b, :], s.rows2[:, 0:512], ALU.add).then_inc(bias_done, 1)
                if has_before(b, 2):
                    fe.pool_rstd(pool, b - 2, p)
            slots(pool, slot)
            fe.pool_rstd(pool, NB - 2, 0)
            fe.pool_rstd(pool, NB - 1, 1)

        @block.tensor
        def _(pe):
            def turn(b, p):
                pe.wait_ge(zw_done, b + 1)
                pe.wait_ge(z_taken, b)
                nc.tensor.transpose(s.ps[:, 5, 0:P], s.zw[:, p, :], s.ident).then_inc(z_turned, 1)

            def experts(b, p):
                pe.wait_ge(z_taken, b + 1)
                nc.tensor.matmul(s.ps[:, 1 + p, :], s.zwT[:, p, :], s.lB2, start=False, stop=True).then_inc(y_ready, 1)

            def slot(b, p):
                pe.wait_ge(fe.ready, fe.base + b + 1)
                if has_before(b, 2):
                    pe.wait_ge(zw_done, b - 1)
                for c in range(DC):
                    last = nc.tensor.matmul(s.ps[:, 3 + p, 0:144], s.xnT[:, p, c, :], s.zl2[:, c, :], start=(c == 0), stop=(c == DC - 1))
                last.then_inc(zl_ready, 1)
                if has_before(b, 1):
                    turn(b - 1, 1 - p)
                if has_before(b, 2):
                    pe.wait_ge(res_done, b - 1)
                for c in range(DC):
                    last = nc.tensor.matmul(s.ps[:, 1 + p, :], s.xnT[:, p, c, :], s.w2f[:, c, :], start=(c == 0), stop=False)
                last.then_inc(y_open, 1)
                if has_after(b, 2):
                    fe.pe_turn(pe, b + 2, p)
                if has_before(b, 1):
                    experts(b - 1, 1 - p)
            fe.pe_turn(pe, 0, 0)
            fe.pe_turn(pe, 1, 1)
            slots(pe, slot)
            turn(NB - 1, 1)
            experts(NB - 1, 1)

        @block.scalar
        def _(act):
            def take(b, p):
                act.wait_ge(fe.turned, fe.base + b + 1)
                if has_before(b, 2):
                    act.wait_ge(y_open, b - 1)
                nc.scalar.activation(s.xnT[:, p, :, :].rearrange("p c t -> p (c t)"), s.ps[:, 0, :], ACT.Copy).then_inc(fe.ready, 1)

            def take_z(b, p):
                act.wait_ge(z_turned, b + 1)
                if has_before(b, 2):
                    act.wait_ge(y_ready, b - 1)
                nc.scalar.activation(s.zwT[:, p, :], s.ps[:, 5, 0:P], ACT.Copy).then_inc(z_taken, 1)

            def slot(b, p):
                if has_before(b, 1):
                    take_z(b - 1, 1 - p)
                act.wait_ge(neg_done, b + 1)
                if has_before(b, 2):
                    act.wait_ge(c_done, b - 1)
                nc.scalar.activation(s.rex[:, p, :], s.rl[:, p, :], ACT.Exp, bias=s.negm[:, p:p + 1]).then_inc(exp_done, 1)
                if has_after(b, 2):
                    take(b + 2, p)
            take(0, 0)
            take(1, 1)
            slots(act, slot)
            take_z(NB - 1, 1)

        @block.vector
        def _(dve):
            v = nc.vector

            def add(b, p):
                dve.wait_ge(y_ready, b + 1)
                dve.wait_ge(bias_done, b + 1)
                v.tensor_tensor(s.X[:, b, :], s.ps[:, 1 + p, :], s.X[:, b, :], ALU.add).then_inc(res_done, 1)

            def slot(b, p):
                dve.wait_ge(zl_ready, b + 1)
                if has_before(b, 2):
                    dve.wait_ge(exp_done, b - 1)
                v.tensor_tensor(s.rl[:, p, :], s.ps[:, 3 + p, 128:144], s.ladj[:, 4, :], ALU.add).then_inc(l_done, 1)
                dve.wait_ge(l_done, b + 1)
                dve.wait_ge(neg_done, b)
                fe.late_waits(dve, b, res_done)
                v.tensor_reduce(s.smax[:, p:p + 1], s.rl[:, p, :], AX.X, ALU.max).then_inc(max_done, 1)
                fe.late_stats(b, p)
                dve.wait_ge(max_done, b + 1)
                v.tensor_scalar(s.negm[:, p:p + 1], s.smax[:, p:p + 1], -1.0, None, ALU.mult).then_inc(neg_done, 1)
                dve.wait_ge(exp_done, b + 1)
                dve.wait_ge(alpha_done, b)
                v.tensor_tensor(s.rc[:, p, :], s.rex[:, p, :], s.cnt[:, :], ALU.mult).then_inc(c_done, 1)
                dve.wait_ge(c_done, b + 1)
                dve.wait_ge(inv_done, b)
                v.tensor_reduce(s.den[:, p:p + 1], s.rc[:, p, :], AX.X, ALU.add).then_inc(sum_done, 1)
                dve.wait_ge(sum_done, b + 1)
                v.reciprocal(s.rd[:, p:p + 1], s.den[:, p:p + 1]).then_inc(inv_done, 1)
                dve.wait_ge(inv_done, b + 1)
                dve.wait_ge(zw_done, b)
                v.tensor_scalar(s.ra[:, p, :], s.rc[:, p, :], s.rd[:, p:p + 1], 16.0 / 8.0, ALU.mult, ALU.mult).then_inc(alpha_done, 1)
                dve.wait_ge(alpha_done, b + 1)
                if has_before(b, 2):
                    dve.wait_ge(z_turned, b - 1)
                v.tensor_tensor(s.zw[:, p, :].rearrange("p (e r) -> p e r", e=E), s.ps[:, 3 + p, 0:128].rearrange("p (e r) -> p e r", e=E),
                                s.ra[:, p, :].unsqueeze(2).broadcast_to([P, E, R]), ALU.mult).then_inc(zw_done, 1)
                if has_after(b, 2):
                    fe.dve_normalise(dve, b + 2, p)
                if has_before(b, 1):
                    fe.late_before_write(dve, b)
                    add(b - 1, 1 - p)
                    fe.late_after_write(b, p)
            for b in range(2):
                fe.dve_normalise(dve, b, b)
            slots(dve, slot)
            add(NB - 1, 1)
            fe.late_last_moments(dve, res_done)
    fe.base += NB
    fe.mbase += NB


def dequantise(nc, s, t):
    LANES = 0x11111111
    w_in, step, bit_step, code_done, hot_done, added, turned, taken = (s.sem("dq_" + n) for n in ("w_in", "step", "bit", "code", "hot", "added", "turned", "taken"))
    with nc.Block() as block:
        @block.sync
        def _(sp):
            sp.dma_start(s.qw[:, :, :], t["qw"]).then_inc(w_in, 16)
            sp.dma_start(s.lut[:, :, :], t["lut4"].rearrange("(c p) v -> p c v", p=P)).then_inc(w_in, 16)

        @block.vector
        def _(dve):
            v = nc.vector
            link = linked(dve, step)
            dve.wait_ge(w_in, 32)
            for r in range(4):
                link(v.tensor_scalar(s.T4[:, :, r], s.qw[:, 0, :], r, LANES, ALU.logical_shift_right, ALU.bitwise_and))
                for p in range(1, 4):
                    link(v.tensor_scalar(s.tq[:, :], s.qw[:, p, :], r, LANES, ALU.logical_shift_right, ALU.bitwise_and))
                    link(v.scalar_tensor_tensor(s.T4[:, :, r], s.tq[:, :], p, s.T4[:, :, r], ALU.logical_shift_left, ALU.bitwise_or))
            for a in range(8):
                link(v.tensor_scalar(s.code[:, :, a, :], s.T4[:, :, :], 4 * a, 15, ALU.logical_shift_right, ALU.bitwise_and))
            link(v.tensor_copy(s.codef[:, :, :], s.code[:, :, :, :].rearrange("p (o w) a r -> p o (w a r)", o=DC)))
            n = 0
            for o in range(DC):
                for k in range(16):
                    if n >= 2:
                        dve.wait_ge(added, n - 1)
                    v.tensor_scalar(s.hot[:, n % 2, :], s.codef[:, o, :], float(k), s.lut[:, o, k:k + 1], ALU.is_equal, ALU.mult).then_inc(hot_done, 1)
                    n += 1

        @block.gpsimd
        def _(pool):
            n = 0
            for o in range(DC):
                for k in range(16):
                    pool.wait_ge(hot_done, n + 1)
                    if k:
                        pool.wait_ge(added, n)
                        nc.gpsimd.tensor_tensor(s.WO[:, o, :], s.WO[:, o, :], s.hot[:, n % 2, :], ALU.add).then_inc(added, 1)
                    else:
                        nc.gpsimd.tensor_copy(s.WO[:, o, :], s.hot[:, n % 2, :]).then_inc(added, 1)
                    n += 1

        @block.tensor
        def _(pe):
            for o in range(DC):
                pe.wait_ge(added, 16 * (o + 1))
                if o >= 2:
                    pe.wait_ge(taken, o - 1)
                for c in range(DC):
                    last = nc.tensor.transpose(s.ps[:, o % 2, c * P:(c + 1) * P], s.WO[:, o, c * P:(c + 1) * P], s.ident)
                last.then_inc(turned, 1)

        @block.scalar
        def _(act):
            for o in range(DC):
                act.wait_ge(turned, o + 1)
                nc.scalar.activation(s.WL[:, :, o * P:(o + 1) * P], s.ps[:, o % 2, :].rearrange("p (c o) -> p c o", c=DC), ACT.Copy).then_inc(taken, 1)


def build(nc, t, out, stop=99):
    s = Shared()
    with ExitStack() as top:
        def sb_in(stack):
            return lambda name, shape, dt=F32: stack.enter_context(nc.sbuf_tensor(name, shape, dt))
        sb = sb_in(top)
        s.retired, s.current = [], []

        def sem(name):
            handle = nc.alloc_semaphore(name=name)
            s.current.append(handle)
            return handle
        s.sem = sem
        s.X = sb("X", [P, NB, D])
        s.ident = sb("ident", [P, P])[:]
        s.ident_bf = sb("ident_bf", [P, P], BF16)
        s.ones = sb("ones", [P, P])
        s.ones_blk = {4: sb("ones4", [P, 4, 32])[:], 2: sb("ones2", [P, 2, 32])[:]}
        s.mask4 = sb("mask4", [96, 4])[:]
        s.mask2 = sb("mask2", [96, 2])[:]
        s.ones_ready = s.sem("ones_ready")
        s.eps = sb("eps", [P, 1])
        s.minus_half, s.var_eps = sb("minus_half", [P, NB]), sb("var_eps", [P, NB])
        s.mstats, s.mmv, s.mean = sb("mstats", [P, 2, 6]), sb("mmv", [P, 2, 2]), sb("mean", [P, NB, 1])
        s.stats = sb("stats", [P, NB, 6])
        s.mv = sb("mv", [P, NB, 2])
        s.rstd = sb("rstd", [P, NB, 1])
        s.xn = sb("xn", [P, 2, D])
        s.xnT = sb("xnT", [P, 2, DC, P])
        s.ps = top.enter_context(nc.psum_tensor("ps", [P, 8, 512], F32))
        s.A, s.B = 6, 7
        s.x_out = s.sem("x_out")
        s.front = Front(nc, s)

        def packed_buffers(sb, tag, HL):
            s.Q = sb("Q" + tag, [P, 2, 4, 512], F32R)
            s.KB = sb("KB" + tag, [P, 2, 4, HL * P], F32R)
            s.VE = sb("VE" + tag, [P, 2, 4, HL, 32])
            s.QH, s.QL = sb("QH" + tag, [P, 512], F32R), sb("QL" + tag, [P, 512], F32R)
            s.KF, s.KH = sb("KF" + tag, [96, 4, P]), sb("KH" + tag, [96, 4, P], F32R)
            s.VS = sb("VS" + tag, [P, P])
            s.PT = sb("PT" + tag, [P, 8, 512])
            s.mx = sb("mx" + tag, [P, 4, 4, HL])
            s.m8 = sb("m8" + tag, [P, 4, 4, 2, HL], BF16)
            s.mrow = sb("mrow" + tag, [P, 512], F32R)
            s.rden, s.msg = sb("rden" + tag, [P, 512]), sb("msg" + tag, [P, 512])
            s.ctxT_s = sb("ctxT_s" + tag, [P, 2, DC, P])
            s.neg = sb("neg" + tag, [P, 4, HL * P])

        with ExitStack() as phase:
            sb = sb_in(phase)
            packed_buffers(sb, "0", 4)
            s.XN = sb("XN", [P, NB, D])
            s.wq0, s.wk0, s.wm0 = (sb(n, [P, P])[:] for n in ("wq0", "wk0", "wm0"))
            s.wk0_rep = sb("wk0_rep", [P, 4, 96])[:]
            s.proj = sb("proj", [P, DC, P])[:]
            s.w1m0, s.w1x0 = sb("w1m0", [P, 256])[:], sb("w1x0", [P, 256])[:]
            s.w2_0 = sb("w2_0", [P, 2, P])[:]
            s.cols0 = sb("cols0", [P, 18])[:]
            s.bk0_row = sb("bk0_row", [P, P])[:]
            s.colsum, s.colsum_row = sb("colsum", [P, 1]), sb("colsum_row", [P, P])
            s.weff, s.bn = sb("weff", [P, 256]), sb("bn", [P, 14])
            s.C, s.H = sb("C", [P, P]), sb("H", [P, 2, 512])
            s.current = []
            setup(nc, s, t)
            linear_attention_of_channels(nc, s, t)
        s.retired, s.current = s.current, []
        if stop >= 1:
            with ExitStack() as phase:
                sb = sb_in(phase)
                s.WF = sb("WF", [P, 3, 7168])
                with ExitStack() as prep:
                    sb = sb_in(prep)
                    s.SG = sb("SG", [P, 3, 7168], BF16)
                    s.WS, s.wscr = sb("WS", [P, 2, 1792]), sb("wscr", [P, 1792], BF16)
                    s.wabs, s.wsum, s.coeff = sb("wabs", [P, 12]), sb("wsum", [P, 3]), sb("coeff", [P, 3])
                    binary_weights(nc, s, t)
                for handle in s.retired:
                    nc.release_semaphore(handle)
                sb = sb_in(phase)
                s.XNT = sb("XNT", [P, DC, NB, P])
                s.SL, s.HT = sb("SL", [P, 2, 512]), sb("HT", [P, 2, 512])
                gated_ffn(nc, s, t)
        sb = sb_in(top)
        s.ctx = sb("ctx", [P, NB, D])
        s.ctxT = sb("ctxT", [P, DC, NB, P])
        s.E, s.EWT, s.SR = sb("E", [P, 2, P]), sb("EWT", [P, 2, P]), sb("SR", [P, 2, P])
        s.smax, s.negm, s.den, s.rd = (sb(n, [P, 2]) for n in ("smax", "negm", "den", "rd"))
        if stop >= 2:
            with ExitStack() as phase:
                sb = sb_in(phase)
                s.wq1, s.wk1, s.mt1 = (sb(n, [P, DC, D]) for n in ("wq1", "wk1", "mt1"))
                s.cols1, s.bqk, s.v1, s.vrep = sb("cols1", [P, 8]), sb("bqk", [P, 8]), sb("v1", [P, 8]), sb("vrep", [P, DC, P])
                s.G, s.R = sb("G", [P, DC, NB, P]), sb("R", [P, NB, P])
                fold_text_attention(nc, s, t)
                context_attention(nc, s, "l1", s.G, s.R, D ** -0.5)

        def load_all(loads):
            with nc.Block() as block:
                done = s.sem(f"in{len(loads)}_{load_all.n}")
                load_all.n += 1

                @block.sync
                def _(sp):
                    for to, of in loads:
                        sp.dma_start(to, of).then_inc(done, 16)
                    sp.wait_ge(done, 16 * len(loads))
        load_all.n = 0
        if stop >= 3:
            with ExitStack() as phase:
                sb = sb_in(phase)
                s.w1f, s.ag1 = sb("w1f", [P, DC, D]), sb("ag1", [P, DC, 160])
                s.rows1, s.lB1 = sb("rows1", [P, 368]), sb("lB1", [P, D])[:]
                s.AGS, s.gh, s.gsm, s.gg = sb("AGS", [P, NB, 160]), sb("gh", [P, NB, 32]), sb("gsm", [P, 13, NB]), sb("gg", [P, 4, NB, 8])
                s.gprod, s.gcount, s.gallow, s.gw = sb("gprod", [P, NB, 8, 32]), sb("gcount", [P, 2, 8]), sb("gallow", [P, 16]), sb("gw", [P, NB, 8])
                s.tw, s.twT = sb("tw", [P, 2, P]), sb("twT", [P, 2, P])
                load_all([(s.w1f[:, :, :], t["w1f"]), (s.ag1[:, :, :], t["ag1"]), (s.lB1, t["lB1"]), (s.rows1[:, :], t["rows1"].broadcast_to([P, 368]))])
                dense(nc, s, "l1f", s.w1f, s.ag1, None)
                expert_gates(nc, s, t)
        if stop >= 4:
            with ExitStack() as phase:
                sb = sb_in(phase)
                packed_buffers(sb, "2", 2)
                s.wq2, s.wk2, s.wv2, s.wo2 = sb("wq2", [P, DC, 4, P]), sb("wk2", [P, DC, 4, 96]), sb("wv2", [P, DC, P]), sb("wo2", [P, 4, D])
                grouped_query_attention(nc, s, t)
        if stop >= 5:
            with ExitStack() as phase:
                sb = sb_in(phase)
                s.w2f, s.zl2, s.lB2 = sb("w2f", [P, DC, D]), sb("zl2", [P, DC, 144]), sb("lB2", [P, D])[:]
                s.rows2, s.active, s.activef = sb("rows2", [P, 560]), sb("active", [P, 4], I32), sb("activef", [P, 4])
                s.ladj, s.cnt = sb("ladj", [P, 5, 16]), sb("cnt", [P, 16])
                s.rl, s.rex, s.rc, s.ra = (sb(n, [P, 2, 16]) for n in ("rl", "rex", "rc", "ra"))
                s.zw, s.zwT = sb("zw", [P, 2, P]), sb("zwT", [P, 2, P])
                routed_ffn(nc, s, t)
        if stop >= 6:
            with ExitStack() as phase:
                context_attention(nc, s, "l3", s.ctxT, None, 1.0)
        if stop >= 7:
            with ExitStack() as phase:
                sb = sb_in(phase)
                s.WL, s.b3 = sb("WL", [P, DC, D]), sb("b3", [P, D])
                s.qw, s.lut, s.T4, s.tq = sb("qw", [P, 4, 64], I32), sb("lut", [P, DC, 16]), sb("T4", [P, 64, 4], I32), sb("tq", [P, 64], I32)
                s.code, s.codef = sb("code", [P, 64, 8, 4], I32), sb("codef", [P, DC, D])
                s.hot, s.WO = sb("hot", [P, 2, D]), sb("WO", [P, DC, D])
                load_all([(s.b3[:, :], t["b3"].broadcast_to([P, D]))])
                dequantise(nc, s, t)
                dense(nc, s, "l3f", s.WL, None, s.b3[:, :], out)
                return

        with nc.Block() as block:
            @block.sync
            def _(sp):
                sp.dma_start(out.rearrange("b p d -> p b d"), s.X[:, :, :]).then_inc(s.x_out, 16)
                sp.wait_ge(s.x_out, 16)


def lay_out(inputs):
    import numpy as np
    a = {k: np.asarray(v) for k, v in inputs.items()}
    cont = np.ascontiguousarray
    m = {}
    m["x"] = a["x"]
    m["ctxT"] = cont(a["ctx_4096"].transpose(0, 2, 1))
    m["ident"] = np.eye(P, dtype=np.float32)
    chan = np.array([d * 16 + 4 * g + h for g in range(4) for h in range(4) for d in range(8)])
    m["wq0"] = cont(a["L0_xattn_to_q_w"].T[:, chan])
    m["wk0"] = cont(a["L0_xattn_to_k_w"].T[:, chan])
    m["wk0_rep"] = cont(np.tile(m["wk0"].reshape(P, 4, 1, 32), (1, 1, 3, 1)).reshape(P, 4, 96))
    m["proj_k"] = a["L0_xattn_proj_k"]
    m["wm0"] = cont(a["L0_xattn_merge_w"][:, chan])
    m["base"] = np.stack([cont(a[f"L0_ffn_mean_w{n}"].T.reshape(-1, P, k).transpose(1, 0, 2)).reshape(P, 7168) for n, k in ((1, 1792), (3, 1792), (2, 512))])
    m["w"] = np.stack([cont(a[f"L0_ffn_w{n}"].T.reshape(-1, P, k).transpose(1, 0, 2)).reshape(P, 7168) for n, k in ((1, 1792), (3, 1792), (2, 512))])
    m["wq1"], m["wk1"] = (cont(a["L1_xattn_" + n].reshape(DC, P, D).transpose(1, 0, 2)) for n in ("Wq", "Wk"))
    m["cols1"] = cont(np.concatenate([a["L1_xattn_" + n].reshape(DC, P).T for n in ("bq", "bk")], axis=1))
    m["ctxT_all"] = cont(a["ctx_4096"].reshape(NB, P, DC, P).transpose(3, 2, 0, 1))
    m["ctx"] = cont(a["ctx_4096"].transpose(1, 0, 2))
    by_chunk = lambda w: cont(w.reshape(DC, P, -1).transpose(1, 0, 2))
    m["w1f"] = by_chunk(a["L1_ffn_weight"].T)
    m["ag1"] = by_chunk(np.concatenate([a["L1_ffn_lora_A"].transpose(1, 0, 2).reshape(D, P), a["L1_ffn_gw1"].T], axis=1))
    m["lB1"] = a["L1_ffn_lora_B"].reshape(P, D)
    m["rows1"] = np.concatenate([a["L1_ffn_gb1"], a["L1_ffn_ln_gamma"], a["L1_ffn_ln_beta"], a["L1_ffn_gw2"].reshape(-1),
                                 a["L1_ffn_gb2"], 8.0 - np.arange(8, dtype=np.float32)])[None, :]
    m["wq2"] = cont(a["L2_xattn_Wq"].reshape(DC, P, 8, 4, 16).transpose(1, 0, 3, 2, 4).reshape(P, DC, 4, P))
    m["wk2"] = cont(np.tile(a["L2_xattn_Wk"].reshape(DC, P, 4, 1, 32), (1, 1, 1, 3, 1)).transpose(1, 0, 2, 3, 4).reshape(P, DC, 4, 96))
    m["wv2"] = by_chunk(a["L2_xattn_Wv"])
    m["wo2"] = cont(a["L2_xattn_Wo"].reshape(8, 4, 16, D).transpose(0, 2, 1, 3).reshape(P, 4, D))
    m["w2f"] = by_chunk(a["L2_ffn_W_base"].T)
    m["zl2"] = by_chunk(np.concatenate([a["L2_ffn_lora_A"].reshape(P, D).T, a["L2_ffn_router_W"].T], axis=1))
    m["lB2"] = cont(a["L2_ffn_lora_B"].transpose(0, 2, 1).reshape(P, D))
    m["b_base"] = a["L2_ffn_b_base"][None, :]
    m["rows2"] = np.concatenate([np.arange(16, dtype=np.float32), a["L2_ffn_router_b"], a["L2_ffn_domain_prior"]])[None, :]
    m["active"] = a["L2_ffn_active"][None, :]
    m["qw"] = cont(a["L3_ffn_qweight"][:4].reshape(4, DC, P, 16).transpose(2, 0, 1, 3).reshape(P, 4, 64))
    m["lut4"] = a["L3_ffn_lut4"]
    m["b3"] = a["L3_ffn_bias"][None, :]
    w1t = a["L0_xattn_mlp_w1"].T
    m["w1x0"], m["w1m0"] = cont(w1t[:P]), cont(w1t[P:])
    m["w2_0"] = cont(a["L0_xattn_mlp_w2"].T.reshape(2, P, P).transpose(1, 0, 2))
    bk = a["L0_xattn_to_k_b"][chan]
    two = lambda n: a[n].reshape(2, P).T
    m["cols0"] = cont(np.concatenate([
        a["L0_xattn_to_q_b"][chan][:, None], np.tile(bk.reshape(4, 32).T, (4, 1)), np.zeros((P, 1), np.float32),
        a["L0_xattn_merge_b"][:, None], a["L0_xattn_mlp_b2"][:, None], two("L0_xattn_bn_gamma"), two("L0_xattn_bn_beta"),
        two("L0_xattn_bn_mean"), two("L0_xattn_bn_var"), two("L0_xattn_mlp_b1")], axis=1))
    m["bk0_row"] = cont(bk[None, :])
    for HL in (4, 2):
        w = 32 // HL
        head = np.arange(32) // w
        eye = np.eye(HL, dtype=np.float32)
        m[f"mask{HL}"] = cont(np.tile(eye[head], (3, 1)))
        m[f"ones{HL}"] = cont(np.tile(eye[:, head][None], (P, 1, 1)))
        neg = np.zeros((4, 2, HL, 4, HL, P), np.float32)
        for g in range(4):
            for h in range(HL):
                neg[g, :, h, g, h, :] = -1.0
        full = np.zeros((32, 4, HL * P), np.float32)
        full[:8 * HL] = neg.reshape(8 * HL, 4, HL * P)
        m[f"neg{HL}"] = full
    return m


def kernel(**inputs):
    import concourse.bacc as _bacc
    from concourse.bass_utils import run_bass_kernel_spmd as _run

    nc = _bacc.Bacc("TRN2", target_bir_lowering=False, num_devices=1)
    arrays = {f"in_{k}": v for k, v in lay_out(inputs).items()}
    t = {k[3:]: nc.dram_tensor(k, v.shape, mybir.dt.from_np(v.dtype), kind="ExternalInput").ap() for k, v in arrays.items()}
    out = nc.dram_tensor("out", (NB, P, D), F32, kind="ExternalOutput").ap()
    build(nc, t, out)
    return _run(nc, [arrays], core_ids=[0]).results[0]["out"]
```

```python
from contextlib import ExitStack

import concourse.bass as bass
from concourse import mybir

F32 = mybir.dt.float32
F32R = mybir.dt.float32r
BF16 = mybir.dt.bfloat16
I32 = mybir.dt.int32
U8 = mybir.dt.uint8
ALU = mybir.AluOpType
ACT = mybir.ActivationFunctionType
AX = mybir.AxisListType

P = 128
NB = 8
D = 512
DC = D // P
LN_EPS = 1e-5
BN_EPS = 1e-3


CONSTANTS = 4


class Shared:
    pass


def symbolic(b):
    return not isinstance(b, int)


def has_before(b, n):
    return symbolic(b) or b >= n


def has_after(b, n, of=NB):
    return symbolic(b) or b + n < of


def slots(engine, slot, n=NB):
    slot(0, 0)
    slot(1, 1)
    with engine.Fori(1, n // 2 - 1) as i:
        for p in range(2):
            slot(2 * i + p, p)
    slot(n - 2, 0)
    slot(n - 1, 1)


class NoSide:
    @staticmethod
    def sp(sp, b, p, parts=()):
        pass
    pool = act = sp


def packed_attention(nc, s, name, HL, scale, load, prep, tail, side=NoSide):
    J = 4 * HL
    W = P * HL
    PER = 512 // W
    Q, KB, VE = s.Q, s.KB, s.VE
    sem = s.sem
    q_packed = sem(name + "_q_packed")
    kb_ready = sem(name + "_kb_ready")
    s_ready = sem(name + "_s_ready")
    s_taken = sem(name + "_s_taken")
    max_split = sem(name + "_max_split")
    max_turned = sem(name + "_max_turned")
    max_rows = sem(name + "_max_rows")
    t_ready = sem(name + "_t_ready")
    exp_done = sem(name + "_exp_done")
    den_done = sem(name + "_den_done")
    pv_done = sem(name + "_pv_done")
    rden_done = sem(name + "_rden_done")
    msg_done = sem(name + "_msg_done")
    hi_done = sem(name + "_hi_done")

    def s_tile(j):
        return j * PER // 4, j * PER % 4

    def pe_scores(pe, b, p, j):
        g, q0 = s_tile(j)
        if j == 0:
            pe.wait_ge(q_packed, (b + 1) * 192)
            pe.wait_ge(kb_ready, b + 1)
        if j >= 2:
            pe.wait_ge(s_taken, b * J + j - 1)
        for r in range(PER):
            last = nc.tensor.matmul(s.ps[:, j % 2, r * W:(r + 1) * W], Q[0:96, p, g, (q0 + r) * P:(q0 + r + 1) * P],
                                    KB[0:96, p, g, 0:W], start=True, stop=True)
        last.then_inc(s_ready, 1)

    def dve_max(dve, b, p, j):
        g, q0 = s_tile(j)
        dve.wait_ge(s_ready, b * J + j + 1)
        if j == 0:
            dve.wait_ge(max_split, b)
        nc.vector.tensor_reduce(s.mx[:, q0:q0 + PER, g, 0:HL],
                                s.ps[:, j % 2, :].rearrange("p (q h k) -> p q h k", q=PER, h=HL), AX.X, ALU.max
                                ).then_inc(s_taken, 1)
        if j == J - 1:
            dve.wait_ge(s_taken, (b + 1) * J)
            dve.wait_ge(max_turned, b)
            if has_before(b, 1):
                dve.wait_ge(t_ready, b * J)
            nc.vector.tensor_copy(s.m8[:, :, :, 0, 0:HL], s.mx[:, :, :, 0:HL]).then_inc(hi_done, 1)
            dve.wait_ge(hi_done, b + 1)
            nc.vector.tensor_tensor(s.m8[:, :, :, 1, 0:HL], s.mx[:, :, :, 0:HL], s.m8[:, :, :, 0, 0:HL],
                                    ALU.subtract).then_inc(max_split, 1)

    def pe_max_turn(pe, b):
        pe.wait_ge(max_split, b + 1)
        if symbolic(b) or b:
            pe.wait_ge(s.v_done, b + 2 if symbolic(b) else min(b + 2, NB))
            pe.wait_ge(max_rows, b)
        else:
            pe.wait_ge(s.v_done, 1)
        for q in range(4):
            last = nc.tensor.matmul(s.ps[96:96 + 8 * HL, s.A, q * P:(q + 1) * P],
                                    s.m8[:, q, :, :, :].rearrange("p g t h -> p (g t h)"),
                                    s.ident_bf[:, :], start=True, stop=True)
        last.then_inc(max_turned, 1)

    def act_max_rows(act, b, p):
        act.wait_ge(max_turned, b + 1)
        nc.scalar.activation(Q[96:96 + 8 * HL, p, :, :], s.ps[96:96 + 8 * HL, s.A, :].unsqueeze(1).broadcast_to([8 * HL, 4, 512]), ACT.Copy
                             ).then_inc(max_rows, 1)

    def pe_turned(pe, b, p, h, g):
        j = 4 * h + g
        if j == 0:
            pe.wait_ge(max_rows, b + 1)
        if j >= 2:
            pe.wait_ge(exp_done, b * J + j - 1)
        nc.tensor.matmul(s.ps[:, 2 + j % 2, :], KB[:, p, g, h * P:(h + 1) * P], Q[:, p, g, :],
                         start=True, stop=True).then_inc(t_ready, 1)

    def act_exp(act, b, h, g):
        j = 4 * h + g
        act.wait_ge(t_ready, b * J + j + 1)
        if h >= 2 and g == 0:
            act.wait_ge(pv_done, b * HL + h - 1)
        nc.scalar.activation(s.PT[:, j % 8, :], s.ps[:, 2 + j % 2, :], ACT.Exp, scale=scale).then_inc(exp_done, 1)

    def pe_values(pe, b, p, h):
        pe.wait_ge(exp_done, b * J + 4 * h + 4)
        if h == 0:
            pe.wait_ge(msg_done, b)
            pe.wait_ge(tail.written, b)
        for g in range(4):
            w = s.PT[:, (4 * h + g) % 8, :]
            last = nc.tensor.matmul(s.ps[32 * g:32 * g + 32, 5, :], s.ones_blk[HL][:, h, :], w, start=(h == 0), stop=(h == HL - 1))
        last.then_inc(den_done, 1)
        for g in range(4):
            w = s.PT[:, (4 * h + g) % 8, :]
            last = nc.tensor.matmul(s.ps[32 * g:32 * g + 32, 4, :], VE[:, p, g, h, :], w, start=(h == 0), stop=(h == HL - 1))
        last.then_inc(pv_done, 1)

    def dve_normalise(dve, b):
        dve.wait_ge(den_done, (b + 1) * HL)
        nc.vector.reciprocal(s.rden[:, :], s.ps[:, 5, :]).then_inc(rden_done, 1)
        dve.wait_ge(rden_done, b + 1)
        dve.wait_ge(pv_done, (b + 1) * HL)
        tail.wait_msg_free(dve, b)
        nc.vector.tensor_tensor(s.msg[:, :], s.ps[:, 4, :], s.rden[:, :], ALU.mult).then_inc(msg_done, 1)

    s.q_packed, s.kb_ready, s.msg_done, s.max_rows, s.pv_done, s.t_ready, s.hi_done = q_packed, kb_ready, msg_done, max_rows, pv_done, t_ready, hi_done
    s.J = J

    with nc.Block() as block:
        @block.sync
        def _(sp):
            load(sp, 0, 0)
            load(sp, 1, 1)
            prep.sp(sp, 0, 0)
            prep.sp(sp, 1, 1)
            side.sp(sp, 0, 0)

            def slot(b, p):
                if has_after(b, 2):
                    load(sp, b + 2, p)
                    prep.sp(sp, b + 2, p)
                if has_after(b, 1):
                    side.sp(sp, b + 1, 1 - p)
            slots(sp, slot)

        @block.gpsimd
        def _(pool):
            def slot(b, p):
                side.pool(pool, b, p)
                if has_after(b, 2):
                    prep.pool(pool, b + 2, p)
                if has_before(b, 2):
                    s.front.pool_rstd(pool, b - 2, p)
            prep.pool(pool, 0, 0)
            prep.pool(pool, 1, 1)
            slots(pool, slot)
            s.front.pool_rstd(pool, NB - 2, 0)
            s.front.pool_rstd(pool, NB - 1, 1)

        @block.tensor
        def _(pe):
            prep.pe_queries(pe, 0, 0)
            prep.pe_keys(pe, 0, 0)
            for j in range(J):
                pe_scores(pe, 0, 0, j)
            pe_max_turn(pe, 0)
            prep.pe_queries(pe, 1, 1)
            prep.pe_keys(pe, 1, 1)

            def slot(b, p):
                for h in range(HL):
                    if h == HL // 2 and has_after(b, 2):
                        prep.pe_keys(pe, b + 2, p)
                    for g in range(4):
                        pe_turned(pe, b, p, h, g)
                        if has_after(b, 1):
                            pe_scores(pe, b + 1, 1 - p, 4 * h + g)
                        if h == HL // 2 - 1 and g == 1 and has_after(b, 2):
                            prep.pe_queries(pe, b + 2, p)
                    if h:
                        pe_values(pe, b, p, h - 1)
                pe_values(pe, b, p, HL - 1)
                if has_after(b, 1):
                    pe_max_turn(pe, b + 1)
                tail.pe_early(pe, b, p)
                tail.pe(pe, b, p)

            slots(pe, slot)

        @block.scalar
        def _(act):
            prep.act_context(act, 0, 0)
            prep.act_queries(act, 0, 0)
            act_max_rows(act, 0, 0)
            prep.act_context(act, 1, 1)
            prep.act_queries(act, 1, 1)

            def slot(b, p):
                for h in range(HL):
                    for g in range(4):
                        act_exp(act, b, h, g)
                        if h == HL // 2 - 1 and g == 1 and has_after(b, 2):
                            prep.act_context(act, b + 2, p)
                            prep.act_queries(act, b + 2, p)
                if has_after(b, 1):
                    act_max_rows(act, b + 1, 1 - p)
                side.act(act, b, p, (0, 1))
                tail.act(act, b, p)
                side.act(act, b, p, (2,))

            slots(act, slot)

        @block.vector
        def _(dve):
            prep.dve_queries(dve, 0, 0)
            prep.dve_keys(dve, 0, 0)
            for j in range(J):
                dve_max(dve, 0, 0, j)
            prep.dve_queries(dve, 1, 1)
            prep.dve_keys(dve, 1, 1)

            def slot(b, p):
                for j in range(J):
                    if j == J // 2 - 2 and has_after(b, 2):
                        prep.dve_queries(dve, b + 2, p)
                    if j == J // 2 and has_after(b, 2):
                        prep.dve_keys(dve, b + 2, p)
                    if has_after(b, 1):
                        dve_max(dve, b + 1, 1 - p, j)
                dve_normalise(dve, b)
                tail.dve(dve, b, p)

            slots(dve, slot)
            s.front.dve_last_moments(dve, tail.written)
    s.front.mbase += NB


def linked(engine, semaphore):
    count = [0]

    def link(instruction):
        count[0] += 1
        instruction.then_inc(semaphore, 1)
        engine.wait_ge(semaphore, count[0])
    return link


def setup(nc, s, t):
    x_in = [s.sem(f"x_in{b}") for b in range(NB)]
    w_in = s.sem("l0_w_in")
    fold_ready, fold_taken = s.sem("l0_fold_ready"), s.sem("l0_fold_taken")
    chain, stats, moments, rstd, bn_chain, bn_rstd, eps_added = (s.sem(n) for n in ("setup_chain", "ln0_stats", "ln0_moments", "ln0_rstd", "bn_chain", "bn_rstd", "eps_added"))
    loads = [(s.ident, t["ident"]), (s.wq0, t["wq0"]), (s.wk0, t["wk0"]), (s.wk0_rep, t["wk0_rep"]),
             (s.proj, t["proj_k"].rearrange("(c p) k -> p c k", p=P)), (s.wm0, t["wm0"]), (s.w1m0, t["w1m0"]),
             (s.w1x0, t["w1x0"]), (s.w2_0, t["w2_0"]), (s.cols0, t["cols0"]), (s.bk0_row, t["bk0_row"].broadcast_to([P, P])),
             (s.ones_blk[4], t["ones4"]), (s.ones_blk[2], t["ones2"]), (s.mask4, t["mask4"]), (s.mask2, t["mask2"]),
             (s.neg[96:128], t["neg4"])]
    with nc.Block() as block:
        @block.sync
        def _(sp):
            for b in range(NB):
                sp.dma_start(s.X[:, b, :], t["x"][b]).then_inc(x_in[b], 16)

        @block.scalar
        def _(act):
            for to, of in loads:
                act.dma_start(to, of).then_inc(w_in, 16)

        @block.gpsimd
        def _(pool):
            nc.gpsimd.memset(s.ones[:, :], 1.0).then_inc(s.ones_ready, 1)
            nc.gpsimd.memset(s.eps[:, :], LN_EPS).then_inc(s.ones_ready, 1)
            nc.gpsimd.memset(s.minus_half[:, :], -0.5).then_inc(s.ones_ready, 1)
            nc.gpsimd.memset(s.VE[:, :, :, :, :], 0.0).then_inc(s.ones_ready, 1)
            pool.wait_ge(w_in, 16 * len(loads))
            pool.wait_ge(s.ones_ready, CONSTANTS)
            nc.gpsimd.tensor_scalar(s.bn[:, 12:14], s.cols0[:, 14:16], BN_EPS, None, ALU.add).then_inc(eps_added, 1)
            pool.wait_ge(eps_added, 1)
            nc.gpsimd.tensor_tensor(s.bn[:, 0:2], s.bn[:, 12:14], s.minus_half[:, 0:2], ALU.pow).then_inc(bn_rstd, 1)
            pool.wait_ge(moments, NB)
            nc.gpsimd.tensor_scalar(s.var_eps[:, :], s.mv[:, :, 1], LN_EPS, None, ALU.add).then_inc(eps_added, 1)
            pool.wait_ge(eps_added, 2)
            nc.gpsimd.tensor_tensor(s.rstd[:, :, 0], s.var_eps[:, :], s.minus_half[:, :], ALU.pow).then_inc(rstd, 1)

        @block.tensor
        def _(pe):
            pe.wait_ge(w_in, 16 * len(loads))
            pe.wait_ge(s.ones_ready, CONSTANTS)
            for c in range(DC):
                nc.tensor.matmul(s.ps[:, 0, 0:1], s.proj[:, c, :], s.ones[:, 0:1], start=(c == 0), stop=(c == DC - 1))
            for c in range(DC):
                nc.tensor.matmul(s.ps[:, 1, 0:P], s.ones[:, :], s.proj[:, c, :], start=(c == 0), stop=(c == DC - 1))
            nc.tensor.matmul(s.ps[:, 2, 0:256], s.wm0, s.w1m0, start=True, stop=True)
            for h in range(2):
                last = nc.tensor.matmul(s.ps[:, 3, h:h + 1], s.w1m0[:, h * P:(h + 1) * P], s.cols0[:, 6:7], start=(h == 0), stop=(h == 1), skip_group_check=True)
            last.then_inc(fold_ready, 1)

        @block.vector
        def _(dve):
            link = linked(dve, bn_chain)
            for b in range(NB):
                dve.wait_ge(x_in[b], 16)
                nc.vector.bn_stats(s.stats[:, b, :], s.X[:, b, :]).then_inc(stats, 1)
            for b in range(NB):
                dve.wait_ge(stats, b + 1)
                nc.vector.bn_aggr(s.mv[:, b, :], s.stats[:, b, :]).then_inc(moments, 1)
            dve.wait_ge(w_in, 16 * len(loads))
            nc.vector.tensor_copy(s.ident_bf[:, :], s.ident).then_inc(fold_taken, 1)
            for p in range(2):
                nc.vector.tensor_copy(s.KB[96:128, p, :, :], s.neg[96:128, :, :]).then_inc(fold_taken, 1)
            dve.wait_ge(fold_ready, 1)
            nc.vector.tensor_copy(s.colsum[:, :], s.ps[:, 0, 0:1]).then_inc(fold_taken, 1)
            nc.vector.tensor_copy(s.colsum_row[:, :], s.ps[:, 1, 0:P]).then_inc(fold_taken, 1)
            nc.vector.tensor_copy(s.weff[:, :], s.ps[:, 2, 0:256]).then_inc(fold_taken, 1)
            c = s.cols0
            dve.wait_ge(bn_rstd, 1)
            link(nc.vector.tensor_tensor(s.bn[:, 2:4], s.bn[:, 0:2], c[:, 8:10], ALU.mult))
            link(nc.vector.tensor_tensor(s.bn[:, 4:6], c[:, 16:18], s.ps[:, 3, 0:2], ALU.add))
            link(nc.vector.tensor_tensor(s.bn[:, 6:8], s.bn[:, 4:6], c[:, 12:14], ALU.subtract))
            link(nc.vector.tensor_tensor(s.bn[:, 8:10], s.bn[:, 6:8], s.bn[:, 2:4], ALU.mult))
            link(nc.vector.tensor_tensor(s.bn[:, 10:12], s.bn[:, 8:10], c[:, 10:12], ALU.add))
            dve.wait_ge(rstd, 1)
            with dve.Fori(0, NB) as b:
                nc.vector.tensor_scalar(s.XN[:, b, :], s.X[:, b, :], s.mv[:, b, 0:1], s.rstd[:, b, :], ALU.subtract, ALU.mult).then_inc(chain, 1)


def linear_attention_of_channels(nc, s, t):
    sem = s.sem
    ct_in, c_ready, c_taken = (sem("l0_ct_in0"), sem("l0_ct_in1")), sem("l0_c_ready"), sem("l0_c_taken")
    q_ready, qhi_done, qlo_done = sem("l0_q_ready"), sem("l0_qhi_done"), sem("l0_qlo_done")
    kr_ready, v_ready, kf_done, kh_done, kx_done, v_done = (sem("l0_" + n) for n in (
        "kr_ready", "v_ready", "kf_done", "kh_done", "kx_done", "v_done"))
    h_ready, relu_done, o_ready, res_done = sem("l0_h_ready"), sem("l0_relu_done"), sem("l0_o_ready"), sem("l0_res_done")
    A, B = s.A, s.B
    ps = s.ps
    fe = s.front

    def load(sp, b, p):
        if has_before(b, 2):
            sp.wait_ge(c_ready, b - 1)
        sp.dma_start(s.ctxT_s[:, p, :, :], t["ctxT"][b].rearrange("(c p) k -> p c k", p=P)).then_inc(ct_in[p], 16)

    class prep:
        @staticmethod
        def pe_queries(pe, b, p):
            pe.wait_ge(ct_in[p], 8 * (b - p) + 16)
            if has_before(b, 1):
                pe.wait_ge(kf_done, b)
            for c in range(DC):
                last = nc.tensor.matmul(ps[:, B, 0:P], s.ctxT_s[:, p, c, :], s.proj[:, c, :], start=(c == 0), stop=(c == DC - 1))
            last.then_inc(c_ready, 1)
            if has_before(b, 1):
                pe.wait_ge(s.max_rows, b - 1 if has_before(b, 2) else 1)
                pe.wait_ge(v_done, b)
            nc.tensor.matmul(ps[:, A, :], s.wq0, s.XN[:, b, :], start=True, stop=True).then_inc(q_ready, 1)

        @staticmethod
        def pe_keys(pe, b, p):
            pe.wait_ge(c_taken, b + 1)
            for g in range(4):
                last = nc.tensor.matmul(ps[0:96, B, g * P:(g + 1) * P], s.wk0_rep[:, g, :], s.C[:, :], start=(g == 0), stop=(g == 3), skip_group_check=True)
            last.then_inc(kr_ready, 1)
            pe.wait_ge(qlo_done, b + 1)
            nc.tensor.matmul(ps[:, A, 0:P], s.C[:, :], s.wk0, start=True, stop=True).then_inc(v_ready, 1)

        @staticmethod
        def act_context(act, b, p):
            act.wait_ge(c_ready, b + 1)
            if has_before(b, 1):
                act.wait_ge(v_ready, b)
            nc.scalar.activation(s.C[:, :], ps[:, B, 0:P], ACT.Copy).then_inc(c_taken, 1)

        @staticmethod
        def act_queries(act, b, p):
            act.wait_ge(q_ready, b + 1)
            if has_before(b, 1):
                act.wait_ge(s.q_packed, 192 * b)
            nc.scalar.activation(s.QH[:, :], ps[:, A, :], ACT.Identity, bias=s.cols0[:, 0:1]).then_inc(qhi_done, 1)

        @staticmethod
        def dve_queries(dve, b, p):
            dve.wait_ge(qhi_done, b + 1)
            nc.vector.scalar_tensor_tensor(s.QL[:, :], ps[:, A, :], s.cols0[:, 0:1], s.QH[:, :].bitcast(F32), ALU.add, ALU.subtract).then_inc(qlo_done, 1)

        @staticmethod
        def dve_keys(dve, b, p):
            dve.wait_ge(kr_ready, b + 1)
            for g in range(4):
                last = nc.vector.scalar_tensor_tensor(s.KF[0:96, g, :], s.colsum_row[0:96, :], s.cols0[0:96, 1 + g:2 + g],
                                                      ps[0:96, B, g * P:(g + 1) * P], ALU.mult, ALU.add)
            last.then_inc(kf_done, 1)
            dve.wait_ge(kf_done, b + 1)
            if has_before(b, 1):
                dve.wait_ge(s.kb_ready, b)
            nc.vector.tensor_copy(s.KH[0:96, :, :], s.KF[0:96, :, :]).then_inc(kh_done, 1)
            dve.wait_ge(kh_done, b + 1)
            nc.vector.tensor_tensor(s.KH[32:64, :, :], s.KF[32:64, :, :], s.KH[32:64, :, :], ALU.subtract).then_inc(kx_done, 1)
            dve.wait_ge(v_ready, b + 1)
            nc.vector.scalar_tensor_tensor(s.VS[:, :], s.bk0_row, s.colsum[:, 0:1], ps[:, A, 0:P], ALU.mult, ALU.add).then_inc(v_done, 1)

        @staticmethod
        def pool(pool, b, p):
            spread(nc, s, pool, b, p, 4, s.mask4, kx_done, v_done)

        @staticmethod
        def sp(sp, b, p):
            pack_queries(nc, s, sp, b, p, qlo_done)

    class tail:
        written = res_done

        @staticmethod
        def wait_msg_free(dve, b):
            dve.wait_ge(h_ready, 2 * b)

        @staticmethod
        def pe_early(pe, b, p):
            for h in range(2):
                nc.tensor.matmul(ps[:, 2 + h, :], s.w1x0[:, h * P:(h + 1) * P], s.XN[:, b, :], start=True, stop=False)

        @staticmethod
        def pe(pe, b, p):
            pe.wait_ge(s.msg_done, b + 1)
            for h in range(2):
                nc.tensor.matmul(ps[:, 2 + h, :], s.weff[:, h * P:(h + 1) * P], s.msg[:, :], start=False, stop=True).then_inc(h_ready, 1)
            for h in range(2):
                pe.wait_ge(relu_done, 2 * b + 1 + h)
                last = nc.tensor.matmul(ps[:, 5, :], s.w2_0[:, h, :], s.H[:, h, :], start=(h == 0), stop=(h == 1))
            last.then_inc(o_ready, 1)

        @staticmethod
        def act(act, b, p):
            act.wait_ge(o_ready, b)
            for h in range(2):
                act.wait_ge(h_ready, 2 * b + h + 1)
                nc.scalar.activation(s.H[:, h, :], ps[:, 2 + h, :], ACT.Relu, bias=s.bn[:, 10 + h:11 + h], scale=s.bn[:, 2 + h:3 + h]).then_inc(relu_done, 1)

        @staticmethod
        def dve(dve, b, p):
            dve.wait_ge(o_ready, b + 1)
            fe.before_write(dve, b, res_done)
            nc.vector.scalar_tensor_tensor(s.X[:, b, :], ps[:, 5, :], s.cols0[:, 7:8], s.X[:, b, :], ALU.add, ALU.add).then_inc(res_done, 1)
            fe.after_write(b, p)

    s.v_done = v_done
    packed_attention(nc, s, "l0", 4, 8 ** -0.5, load, prep, tail, distances(nc, s, t))


PAIRS = 7


def distances(nc, s, t):
    w_in = [s.sem(f"bw_in{p}") for p in range(2)]
    diff_done, abs_done = s.sem("bw_diff"), s.sem("bw_abs")

    class side:
        @staticmethod
        def sp(sp, b, p):
            if not has_after(b, 1):
                return
            if has_before(b, 2):
                sp.wait_ge(abs_done, 3 * (b - 1))
            sp.dma_start(s.SW[:, p, :, :, :], t["w"][b]).then_inc(w_in[p], 16)
            sp.dma_start(s.SB[:, p, :, :, :], t["base"][b]).then_inc(w_in[p], 16)

        @staticmethod
        def pool(pool, b, p):
            if has_after(b, 1):
                pool.wait_ge(w_in[p], 16 * (b - p) + 32)
                nc.gpsimd.tensor_tensor(s.SW[:, p, :, :, :], s.SW[:, p, :, :, :], s.SB[:, p, :, :, :], ALU.subtract).then_inc(diff_done, 1)

        @staticmethod
        def act(act, b, p, parts):
            if has_after(b, 1):
                act.wait_ge(diff_done, b + 1)
                for m in parts:
                    if m or not isinstance(b, int) or b:
                        act.wait_ge(abs_done, 3 * b + m)
                    nc.scalar.activation(s.wscr[:, :, :], s.SW[:, p, :, m, :], ACT.Abs, accum_out=s.wabs[:, b, m:m + 1]).then_inc(abs_done, 1)
    return side


def spread(nc, s, pool, b, p, HL, mask, kx_done, v_done):
    W = 32 // HL
    pool.wait_ge(kx_done, b + 1)
    if has_before(b, 2):
        pool.wait_ge(s.t_ready, (b - 1) * s.J)
    for g in range(4):
        if g == 3:
            pool.wait_ge(v_done, b + 1)
            if has_before(b, 2):
                pool.wait_ge(s.pv_done, (b - 1) * HL)
        nc.gpsimd.tensor_tensor(s.KB[0:96, p, g, 0:HL * P].rearrange("p (h k) -> p h k", h=HL),
                                s.KH[0:96, g, :].bitcast(F32).unsqueeze(1).broadcast_to([96, HL, P]),
                                mask[0:96].unsqueeze(2).broadcast_to([96, HL, P]), ALU.mult)
    for h in range(HL):
        last = nc.gpsimd.tensor_copy(s.VE[:, p, :, h, h * W:(h + 1) * W], s.VS[:, :].rearrange("p (g h d) -> p g h d", g=4, h=HL)[:, :, h, :])
    last.then_inc(s.kb_ready, 1)


def pack_queries(nc, s, sp, b, p, qlo_done):
    if has_before(b, 2):
        sp.wait_ge(s.hi_done, b)
    else:
        sp.wait_ge(qlo_done, b + 1)
    for g in range(4):
        for quadrant, part in enumerate((s.QH, s.QH, s.QL)):
            sp.dma_start(s.Q[32 * quadrant:32 * quadrant + 32, p, g, :].bitcast(F32),
                         part[32 * g:32 * g + 32, :].bitcast(F32)).then_inc(s.q_packed, 16)


class Front:
    def __init__(self, nc, s):
        self.nc, self.s, self.base, self.mbase = nc, s, 0, 0
        sem = s.sem
        self.stats, self.moments, self.eps_added, self.rstd = (sem("fe_" + n) for n in ("stats", "moments", "eps_added", "rstd"))
        self.xn_ready = sem("fe_xn_ready")
        self.turned = sem("fe_turned")
        self.ready = sem("fe_xnT_ready")

    def before_write(self, dve, b, written):
        n = self.mbase + b
        if has_before(b, 1):
            dve.wait_ge(written, b)
            dve.wait_ge(self.stats, n - 1)
        if has_before(b, 2) or self.mbase:
            dve.wait_ge(self.rstd, n - 2)

    def after_write(self, b, p):
        if has_before(b, 1):
            self.dve_stats(b - 1, 1 - p)
        if has_before(b, 2):
            self.dve_moments(p)

    def dve_stats(self, b, p):
        self.nc.vector.bn_stats(self.s.mstats[:, p, :], self.s.X[:, b, :]).then_inc(self.stats, 1)

    def dve_moments(self, p):
        self.nc.vector.bn_aggr(self.s.mmv[:, p, :], self.s.mstats[:, p, :]).then_inc(self.moments, 1)

    def dve_last_moments(self, dve, written):
        n = self.mbase + NB
        dve.wait_ge(written, NB)
        dve.wait_ge(self.rstd, n - 2)
        self.dve_stats(NB - 1, 1)
        dve.wait_ge(self.stats, n - 1)
        self.dve_moments(0)
        dve.wait_ge(self.stats, n)
        self.dve_moments(1)

    def late_waits(self, dve, b, written):
        if has_before(b, 2):
            dve.wait_ge(written, b - 1)
            dve.wait_ge(self.moments, self.mbase + b - 3)

    def late_stats(self, b, p):
        if has_before(b, 2):
            self.dve_stats(b - 2, p)

    def late_before_write(self, dve, b):
        if has_before(b, 2):
            dve.wait_ge(self.stats, self.mbase + b - 1)
            dve.wait_ge(self.rstd, self.mbase + b - 3)

    def late_after_write(self, b, p):
        if has_before(b, 2):
            self.dve_moments(p)

    def late_last_moments(self, dve, written):
        for b in (NB, NB + 1):
            self.late_waits(dve, b, written)
            self.late_stats(b, b % 2)
            self.late_before_write(dve, b)
            self.late_after_write(b, b % 2)

    def dve_all_moments(self, dve, written):
        for b in range(NB):
            dve.wait_ge(written, b + 1)
            if b >= 2:
                dve.wait_ge(self.moments, self.mbase + b - 1)
            self.dve_stats(b, b % 2)
            dve.wait_ge(self.stats, self.mbase + b + 1)
            if b >= 2:
                dve.wait_ge(self.rstd, self.mbase + b - 1)
            self.dve_moments(b % 2)

    def pool_rstd(self, pool, b, p):
        s, n, g = self.s, self.mbase + b, self.nc.gpsimd
        pool.wait_ge(self.moments, n + 1)
        g.tensor_tensor(s.var_eps[:, p:p + 1], s.mmv[:, p, 1:2], s.eps[:, 0:1], ALU.add).then_inc(self.eps_added, 1)
        g.tensor_copy(s.mean[:, b, :], s.mmv[:, p, 0:1])
        pool.wait_ge(self.eps_added, n + 1)
        g.tensor_tensor(s.rstd[:, b, :], s.var_eps[:, p:p + 1], s.minus_half[:, 0:1], ALU.pow).then_inc(self.rstd, 1)

    def dve_normalise(self, dve, b, p):
        s, n = self.s, self.base + b
        if has_before(b, 2):
            dve.wait_ge(self.turned, n - 1)
        self.nc.vector.tensor_scalar(s.xn[:, p, :], s.X[:, b, :], s.mean[:, b, :], s.rstd[:, b, :], ALU.subtract, ALU.mult
                                     ).then_inc(self.xn_ready, 1)

    def pe_turn(self, pe, b, p, bank=0):
        s, n = self.s, self.base + b
        pe.wait_ge(self.xn_ready, n + 1)
        pe.wait_ge(self.ready, n)
        for c in range(DC):
            last = self.nc.tensor.transpose(s.ps[:, bank, c * P:(c + 1) * P], s.xn[:, p, c * P:(c + 1) * P], s.ident)
        last.then_inc(self.turned, 1)


def binary_gated_ffn(nc, s, t):
    sem = s.sem
    fe = s.front
    I = 2 * PAIRS
    names = ("g_ready", "u_ready", "silu_done", "h_done", "o_ready", "out_ready", "res_done", "xlo_done", "sums_done", "total_done",
             "coeff_done", "diff_done", "sign_done", "wp_done", "whi_done", "wlo_done", "hhi_done", "hlo_done")
    (g_ready, u_ready, silu_done, h_done, o_ready, out_ready, res_done, xlo_done, sums_done, total_done,
     coeff_done, diff_done, sign_done, wp_done, whi_done, wlo_done, hhi_done, hlo_done) = (sem("ff_" + n) for n in names)
    w_in = [sem(f"ff_w_in{p}") for p in range(2)]
    ps = s.ps

    def part(tile, first, p):
        return tile[:, p, 0:2, :] if first == 0 else tile[:, p, 0, :]

    def step(first, j):
        return j if first == 0 else I + j

    def sp_load(sp, first, i, p):
        for to, of in ((s.RW, t["w"]), (s.RB, t["base"])):
            sp.dma_start(part(to, first, p), of[i][:, p, 0:2, :] if first == 0 else of[i][:, p, 2, :]).then_inc(w_in[p], 16)

    def pool_diff(pool, first, j, p):
        pool.wait_ge(w_in[p], 16 * (step(first, j) - p) + 32)
        nc.gpsimd.tensor_tensor(part(s.RW, first, p), part(s.RW, first, p), part(s.RB, first, p), ALU.subtract).then_inc(diff_done, 1)

    def act_weights(act, first, j, p):
        n = step(first, j)
        act.wait_ge(diff_done, n + 1)
        nc.scalar.activation(part(s.SG, first, p), part(s.RW, first, p), ACT.Sign).then_inc(sign_done, 1)
        act.wait_ge(wp_done, n + 1)
        if first and has_before(j, 2):
            act.wait_ge(o_ready, j - 1)
        elif first or has_before(j, 2):
            act.wait_ge(u_ready, n - 1)
        nc.scalar.activation(part(s.WH, first, p), part(s.RB, first, p), ACT.Copy).then_inc(whi_done, 1)

    def dve_weights(dve, first, j, p):
        n = step(first, j)
        dve.wait_ge(sign_done, n + 1)
        for m in range(2 if first == 0 else 1):
            last = nc.vector.scalar_tensor_tensor(s.RB[:, p, m, :], s.SG[:, p, m, :], s.coeff[:, first + m:first + m + 1], s.RB[:, p, m, :], ALU.mult, ALU.add)
        last.then_inc(wp_done, 1)
        dve.wait_ge(whi_done, n + 1)
        nc.vector.tensor_tensor(part(s.WLO, first, p), part(s.RB, first, p), part(s.WH, first, p).bitcast(F32), ALU.subtract).then_inc(wlo_done, 1)

    def pe_gate_up(pe, j, p):
        pe.wait_ge(wlo_done, j + 1)
        if has_before(j, 2):
            pe.wait_ge(h_done, j - 1)
        for m, ready in enumerate((g_ready, u_ready)):
            for c in range(DC):
                for k, (w, x) in enumerate(((s.WH, s.XH), (s.WH, s.XLO), (s.WLO, s.XH))):
                    for h in range(2):
                        last = nc.tensor.matmul(ps[:, 4 * p + 2 * m + h, :], w[:, p, m, c * P:(c + 1) * P],
                                                x[:, c, 4 * h:4 * h + 4, :].rearrange("p b t -> p (b t)"),
                                                start=(c == 0 and k == 0), stop=(c == DC - 1 and k == 2))
            last.then_inc(ready, 1)

    def act_silu(act, j, p):
        act.wait_ge(g_ready, j + 1)
        nc.scalar.activation(s.SL[:, p, :, :], ps[:, 4 * p:4 * p + 2, :], ACT.Silu).then_inc(silu_done, 1)

    def dve_hidden(dve, j, p):
        dve.wait_ge(silu_done, j + 1)
        dve.wait_ge(u_ready, j + 1)
        nc.vector.tensor_tensor(s.HF[:, j, :, :], ps[:, 4 * p + 2:4 * p + 4, :], s.SL[:, p, :, :], ALU.mult).then_inc(h_done, 1)

    def act_split_hidden(act, j, p):
        act.wait_ge(h_done, j + 1)
        if has_before(j, 2):
            act.wait_ge(o_ready, j - 1)
        nc.scalar.activation(s.HH[:, p, :, :], s.HF[:, j, :, :], ACT.Copy).then_inc(hhi_done, 1)

    def dve_split_hidden(dve, j, p):
        dve.wait_ge(hhi_done, j + 1)
        nc.vector.tensor_tensor(s.HLO[:, p, :, :], s.HF[:, j, :, :], s.HH[:, p, :, :].bitcast(F32), ALU.subtract).then_inc(hlo_done, 1)

    def pe_down(pe, j, p):
        pe.wait_ge(wlo_done, I + j + 1)
        pe.wait_ge(hlo_done, j + 1)
        if not has_before(j, 1):
            pe.wait_ge(h_done, I)
        for q in range(NB):
            tokens = lambda tile: tile[:, p, :, :].rearrange("p h t -> p (h t)")[:, q * P:(q + 1) * P]
            for k, (h, w) in enumerate(((s.HH, s.WH), (s.HH, s.WLO), (s.HLO, s.WH))):
                last = nc.tensor.matmul(ps[:, q, :], tokens(h), w[:, p, 0, :], start=(not has_before(j, 1) and k == 0), stop=(not has_after(j, 1, I) and k == 2))
            if not has_after(j, 1, I):
                last.then_inc(out_ready, 1)
        if has_after(j, 1, I):
            last.then_inc(o_ready, 1)

    with nc.Block() as block:
        @block.gpsimd
        def _(pool):
            def diff(first):
                return lambda j, p: pool_diff(pool, first, j, p)
            for first in (0, 2):
                slots(pool, diff(first), I)
            for handle in s.retired:
                pool.sem_clear(handle)
            slots(pool, lambda b, p: fe.pool_rstd(pool, b, p))

        @block.sync
        def _(sp):
            for first in (0, 2):
                for p in range(2):
                    if first:
                        sp.wait_ge(wlo_done, I + p - 1)
                    sp_load(sp, first, 0, p)
                with sp.Fori(1, PAIRS) as i:
                    for p in range(2):
                        sp.wait_ge(wlo_done, step(first, 2 * i + p) - 1)
                        sp_load(sp, first, i, p)

        @block.tensor
        def _(pe):
            def turn(b, p):
                pe.wait_ge(fe.xn_ready, fe.base + b + 1)
                if has_before(b, 2):
                    pe.wait_ge(xlo_done, b - 1)
                for c in range(DC):
                    last = nc.tensor.transpose(ps[:, p, c * P:(c + 1) * P], s.xn[:, p, c * P:(c + 1) * P], s.ident)
                last.then_inc(fe.turned, 1)
            slots(pe, turn)
            pe.wait_ge(sums_done, 1)
            nc.tensor.matmul(ps[:, 7, 0:3], s.ones[:, :], s.wsum[:, 0:3], start=True, stop=True).then_inc(total_done, 1)
            pe.wait_ge(xlo_done, NB)
            slots(pe, lambda j, p: pe_gate_up(pe, j, p), I)
            slots(pe, lambda j, p: pe_down(pe, j, p), I)

        @block.scalar
        def _(act):
            def take(b, p):
                act.wait_ge(fe.turned, fe.base + b + 1)
                nc.scalar.activation(s.XH[:, :, b, :], ps[:, p, :].rearrange("p (c t) -> p c t", c=DC), ACT.Copy).then_inc(fe.ready, 1)
            slots(act, take)
            act_weights(act, 0, 0, 0)

            def gate(j, p):
                if has_after(j, 1, I):
                    act_weights(act, 0, j + 1, 1 - p)
                else:
                    act_weights(act, 2, 0, 0)
                act_silu(act, j, p)
            slots(act, gate, I)
            act_split_hidden(act, 0, 0)

            def down(j, p):
                if has_after(j, 1, I):
                    act_weights(act, 2, j + 1, 1 - p)
                    act_split_hidden(act, j + 1, 1 - p)
            slots(act, down, I)

        @block.vector
        def _(dve):
            nc.vector.tensor_reduce(s.wsum[:, 0:3], s.wabs[:, :, :].rearrange("p k m -> p m k"), AX.X, ALU.add).then_inc(sums_done, 1)

            def split(b, p):
                dve.wait_ge(fe.ready, fe.base + b + 1)
                nc.vector.tensor_tensor(s.XLO[:, :, b, :], ps[:, p, :].rearrange("p (c t) -> p c t", c=DC), s.XH[:, :, b, :].bitcast(F32), ALU.subtract).then_inc(xlo_done, 1)
                if has_after(b, 2):
                    fe.dve_normalise(dve, b + 2, p)
            for b in range(2):
                fe.dve_normalise(dve, b, b)
            slots(dve, split)
            dve.wait_ge(total_done, 1)
            nc.vector.tensor_scalar(s.coeff[:, 0:3], ps[:, 7, 0:3], 1.0 / (I * P * D), None, ALU.mult).then_inc(coeff_done, 1)
            dve.wait_ge(coeff_done, 1)
            dve_weights(dve, 0, 0, 0)

            def gate(j, p):
                if has_after(j, 1, I):
                    dve_weights(dve, 0, j + 1, 1 - p)
                else:
                    dve_weights(dve, 2, 0, 0)
                dve_hidden(dve, j, p)
            slots(dve, gate, I)
            dve_split_hidden(dve, 0, 0)

            def down(j, p):
                if has_after(j, 1, I):
                    dve_weights(dve, 2, j + 1, 1 - p)
                    dve_split_hidden(dve, j + 1, 1 - p)
            slots(dve, down, I)
            for b in range(NB):
                dve.wait_ge(out_ready, b + 1)
                fe.before_write(dve, b, res_done)
                nc.vector.tensor_tensor(s.X[:, b, :], ps[:, b, :], s.X[:, b, :], ALU.add).then_inc(res_done, 1)
                fe.after_write(b, b % 2)
            fe.dve_last_moments(dve, res_done)
    fe.base += NB
    fe.mbase += NB


def fold_text_attention(nc, s, t):
    sem = s.sem
    w_in, mt_ready, mt_taken, g_ready, g_taken, v_ready, v_taken, step = (sem("fa_" + n) for n in (
        "w_in", "mt_ready", "mt_taken", "g_ready", "g_taken", "v_ready", "v_taken", "step"))
    WQ, WK, MT = s.wq1, s.wk1, s.mt1
    loads = [(WQ[:, :, :], t["wq1"]), (WK[:, :, :], t["wk1"]), (s.cols1[:, :], t["cols1"]),
             (s.ctxT[:, :, :, :], t["ctxT_all"]), (s.ctx[:, :, :], t["ctx"])]
    with nc.Block() as block:
        @block.sync
        def _(sp):
            for to, of in loads:
                sp.dma_start(to, of).then_inc(w_in, 16)

        @block.tensor
        def _(pe):
            pe.wait_ge(w_in, 16 * len(loads))
            for y in range(DC):
                for c in range(DC):
                    nc.tensor.matmul(s.ps[:, 7, y:y + 1], WK[:, c, y * P:(y + 1) * P], s.cols1[:, c:c + 1], start=(y == 0 and c == 0), stop=False, skip_group_check=True)
            for y in range(DC):
                for c in range(DC):
                    last = nc.tensor.matmul(s.ps[:, 7, 4 + y:5 + y], WQ[:, c, y * P:(y + 1) * P], s.cols1[:, 4 + c:5 + c], start=False, stop=(y == DC - 1 and c == DC - 1), skip_group_check=True)
            last.then_inc(v_ready, 1)
            for y in range(DC):
                for c in range(DC):
                    last = nc.tensor.matmul(s.ps[:, y, :], WK[:, c, y * P:(y + 1) * P], WQ[:, c, :], start=(c == 0), stop=(c == DC - 1))
                last.then_inc(mt_ready, 1)
            pe.wait_ge(v_taken, 2)
            nc.tensor.matmul(s.ps[:, 7, 8:9], s.ones[:, :], s.bqk[:, 0:1], start=True, stop=True).then_inc(v_ready, 1)
            pe.wait_ge(mt_taken, DC)
            for n in range(2 * DC):
                x, h = divmod(n, 2)
                if n >= 2:
                    pe.wait_ge(g_taken, n - 1)
                for c in range(DC):
                    last = nc.tensor.matmul(s.ps[:, 4 + n % 2, :], MT[:, c, x * P:(x + 1) * P], s.ctxT[:, c, 4 * h:4 * h + 4, :].rearrange("p b k -> p (b k)"), start=(c == 0), stop=(c == DC - 1))
                last.then_inc(g_ready, 1)
            pe.wait_ge(v_taken, 4)
            for h in range(2):
                pe.wait_ge(g_taken, 2 * DC - 1 + h)
                for c in range(DC):
                    last = nc.tensor.matmul(s.ps[:, 4 + h, :], s.vrep[:, c, :], s.ctxT[:, c, 4 * h:4 * h + 4, :].rearrange("p b k -> p (b k)"), start=(c == 0), stop=(c == DC - 1))
                last.then_inc(g_ready, 1)

        @block.scalar
        def _(act):
            for y in range(DC):
                act.wait_ge(mt_ready, y + 1)
                nc.scalar.activation(MT[:, y, :], s.ps[:, y, :], ACT.Copy).then_inc(mt_taken, 1)

        @block.vector
        def _(dve):
            dve.wait_ge(w_in, 16 * len(loads))
            nc.vector.tensor_tensor(s.bqk[:, 4:8], s.cols1[:, 0:4], s.cols1[:, 4:8], ALU.mult).then_inc(step, 1)
            dve.wait_ge(step, 1)
            nc.vector.tensor_reduce(s.bqk[:, 0:1], s.bqk[:, 4:8], AX.X, ALU.add).then_inc(v_taken, 1)
            dve.wait_ge(v_ready, 1)
            nc.vector.tensor_copy(s.v1[:, :], s.ps[:, 7, 0:8]).then_inc(v_taken, 1)
            dve.wait_ge(v_ready, 2)
            nc.vector.tensor_copy(s.bqk[:, 1:2], s.ps[:, 7, 8:9]).then_inc(v_taken, 1)
            dve.wait_ge(v_taken, 3)
            for c in range(DC):
                last = nc.vector.tensor_copy(s.vrep[:, c, :], s.v1[:, c:c + 1].broadcast_to([P, P]))
            last.then_inc(v_taken, 1)
            for n in range(2 * DC):
                x, h = divmod(n, 2)
                dve.wait_ge(g_ready, n + 1)
                nc.vector.tensor_scalar(s.G[:, x, 4 * h:4 * h + 4, :].rearrange("p b k -> p (b k)"), s.ps[:, 4 + n % 2, :], s.v1[:, 4 + x:5 + x], None, ALU.add).then_inc(g_taken, 1)
            for h in range(2):
                dve.wait_ge(g_ready, 2 * DC + 1 + h)
                nc.vector.tensor_scalar(s.R[:, 4 * h:4 * h + 4, :].rearrange("p b k -> p (b k)"), s.ps[:, 4 + h, :], s.bqk[:, 1:2], None, ALU.add).then_inc(g_taken, 1)


def context_attention(nc, s, name, KT, R, scale):
    sem = s.sem
    fe = s.front
    s_ready, r_added, max_done, neg_done, e_done, et_ready, et_taken, den_done, o_ready, res_done = (sem(name + n) for n in (
        "_s_ready", "_r_added", "_max", "_neg", "_e", "_et_ready", "_et_taken", "_den", "_o_ready", "_res"))
    SC, OUT, ET = (1, 2), (4, 5), 3
    with nc.Block() as block:
        @block.gpsimd
        def _(pool):
            slots(pool, lambda b, p: fe.pool_rstd(pool, b, p))

        @block.tensor
        def _(pe):
            def turn_weights(b, p):
                pe.wait_ge(e_done, b + 1)
                pe.wait_ge(et_taken, b)
                nc.tensor.transpose(s.ps[:, ET, 0:P], s.E[:, p, :], s.ident).then_inc(et_ready, 1)

            def out(b, p):
                pe.wait_ge(et_taken, b + 1)
                if has_before(b, 2):
                    pe.wait_ge(res_done, b - 1)
                nc.tensor.matmul(s.ps[:, OUT[p], :], s.EWT[:, p, :], s.ctx[:, b, :], start=True, stop=True).then_inc(o_ready, 1)

            def slot(b, p):
                if has_before(b, 1):
                    turn_weights(b - 1, 1 - p)
                pe.wait_ge(fe.ready, fe.base + b + 1)
                if has_before(b, 2):
                    pe.wait_ge(e_done, b - 1)
                for c in range(DC):
                    last = nc.tensor.matmul(s.ps[:, SC[p], 0:P], s.xnT[:, p, c, :], KT[:, c, b, :], start=(c == 0), stop=(c == DC - 1))
                last.then_inc(s_ready, 1)
                if has_after(b, 2):
                    fe.pe_turn(pe, b + 2, p)
                if has_before(b, 1):
                    out(b - 1, 1 - p)
            fe.pe_turn(pe, 0, 0)
            fe.pe_turn(pe, 1, 1)
            slots(pe, slot)
            turn_weights(NB - 1, 1)
            out(NB - 1, 1)

        @block.scalar
        def _(act):
            def take_weights(b, p):
                act.wait_ge(et_ready, b + 1)
                if has_before(b, 2):
                    act.wait_ge(o_ready, b - 1)
                nc.scalar.activation(s.EWT[:, p, :], s.ps[:, ET, 0:P], ACT.Copy).then_inc(et_taken, 1)

            def take(b, p):
                act.wait_ge(fe.turned, fe.base + b + 1)
                if has_before(b, 2):
                    act.wait_ge(s_ready, b - 1)
                nc.scalar.activation(s.xnT[:, p, :, :].rearrange("p c t -> p (c t)"), s.ps[:, 0, :], ACT.Copy).then_inc(fe.ready, 1)

            def slot(b, p):
                if has_before(b, 1):
                    take_weights(b - 1, 1 - p)
                act.wait_ge(neg_done, b + 1)
                if has_before(b, 2):
                    act.wait_ge(et_ready, b - 1)
                    act.wait_ge(res_done, b - 1)
                source = s.SR[:, p, :] if R is not None else s.ps[:, SC[p], 0:P]
                nc.scalar.activation(s.E[:, p, :], source, ACT.Exp, bias=s.negm[:, p:p + 1], scale=scale, accum_out=s.den[:, p:p + 1]).then_inc(e_done, 1)
                if has_after(b, 2):
                    take(b + 2, p)
            take(0, 0)
            take(1, 1)
            slots(act, slot)
            take_weights(NB - 1, 1)

        @block.vector
        def _(dve):
            def add(b, p):
                dve.wait_ge(o_ready, b + 1)
                nc.vector.scalar_tensor_tensor(s.X[:, b, :], s.ps[:, OUT[p], :], s.rd[:, p:p + 1], s.X[:, b, :], ALU.mult, ALU.add).then_inc(res_done, 1)

            def invert(b, p):
                dve.wait_ge(e_done, b + 1)
                if has_before(b, 2):
                    dve.wait_ge(res_done, b - 1)
                nc.vector.reciprocal(s.rd[:, p:p + 1], s.den[:, p:p + 1]).then_inc(den_done, 1)
                dve.wait_ge(den_done, b + 1)

            def slot(b, p):
                dve.wait_ge(s_ready, b + 1)
                if R is not None:
                    if has_before(b, 2):
                        dve.wait_ge(e_done, b - 1)
                    nc.vector.tensor_tensor(s.SR[:, p, :], s.ps[:, SC[p], 0:P], R[:, b, :], ALU.add).then_inc(r_added, 1)
                    dve.wait_ge(r_added, b + 1)
                source = s.SR[:, p, :] if R is not None else s.ps[:, SC[p], 0:P]
                if has_before(b, 1):
                    dve.wait_ge(neg_done, b)
                fe.late_waits(dve, b, res_done)
                nc.vector.tensor_reduce(s.smax[:, p:p + 1], source, AX.X, ALU.max).then_inc(max_done, 1)
                fe.late_stats(b, p)
                dve.wait_ge(max_done, b + 1)
                if has_before(b, 2):
                    dve.wait_ge(e_done, b - 1)
                nc.vector.tensor_scalar(s.negm[:, p:p + 1], s.smax[:, p:p + 1], -scale, None, ALU.mult).then_inc(neg_done, 1)
                if has_before(b, 1):
                    invert(b - 1, 1 - p)
                if has_after(b, 2):
                    fe.dve_normalise(dve, b + 2, p)
                if has_before(b, 1):
                    fe.late_before_write(dve, b)
                    add(b - 1, 1 - p)
                    fe.late_after_write(b, p)
            for b in range(2):
                fe.dve_normalise(dve, b, b)
            slots(dve, slot)
            invert(NB - 1, 1)
            add(NB - 1, 1)
            fe.late_last_moments(dve, res_done)
    fe.base += NB
    fe.mbase += NB


def dense(nc, s, name, W, AG, bias, out=None):
    sem = s.sem
    fe = s.front
    y_ready, ag_ready, ag_taken, bias_done, res_done = (sem(name + n) for n in ("_y", "_ag", "_ag_taken", "_bias", "_res"))
    with nc.Block() as block:
        if out is not None:
            @block.sync
            def _(sp):
                with sp.Fori(0, NB) as b:
                    sp.wait_ge(res_done, b + 1)
                    sp.dma_start(out[b], s.X[:, b, :]).then_inc(s.x_out, 16)
                sp.wait_ge(s.x_out, 16 * NB)

        @block.gpsimd
        def _(pool):
            def slot(b, p):
                pool.wait_ge(fe.xn_ready, fe.base + b + 1)
                nc.gpsimd.tensor_tensor(s.X[:, b, :], s.X[:, b, :], bias, ALU.add).then_inc(bias_done, 1)
            if bias is not None:
                slots(pool, slot)

        @block.tensor
        def _(pe):
            def slot(b, p):
                pe.wait_ge(fe.ready, fe.base + b + 1)
                if AG is not None:
                    if has_before(b, 2):
                        pe.wait_ge(ag_taken, b - 1)
                    for c in range(DC):
                        last = nc.tensor.matmul(s.ps[:, 3 + p, 0:160], s.xnT[:, p, c, :], AG[:, c, :], start=(c == 0), stop=(c == DC - 1))
                    last.then_inc(ag_ready, 1)
                if has_before(b, 2):
                    pe.wait_ge(res_done, b - 1)
                for c in range(DC):
                    last = nc.tensor.matmul(s.ps[:, 1 + p, :], s.xnT[:, p, c, :], W[:, c, :], start=(c == 0), stop=(c == DC - 1))
                last.then_inc(y_ready, 1)
                if has_after(b, 2):
                    fe.pe_turn(pe, b + 2, p)
            fe.pe_turn(pe, 0, 0)
            fe.pe_turn(pe, 1, 1)
            slots(pe, slot)

        @block.scalar
        def _(act):
            def take(b, p):
                act.wait_ge(fe.turned, fe.base + b + 1)
                if has_before(b, 2):
                    act.wait_ge(y_ready, b - 1)
                nc.scalar.activation(s.xnT[:, p, :, :].rearrange("p c t -> p (c t)"), s.ps[:, 0, :], ACT.Copy).then_inc(fe.ready, 1)

            def slot(b, p):
                if AG is not None:
                    act.wait_ge(ag_ready, b + 1)
                    nc.scalar.activation(s.AGS[:, b, :], s.ps[:, 3 + p, 0:160], ACT.Copy).then_inc(ag_taken, 1)
                if has_after(b, 2):
                    take(b + 2, p)
            take(0, 0)
            take(1, 1)
            slots(act, slot)

        @block.vector
        def _(dve):
            def slot(b, p):
                if has_after(b, 2):
                    fe.dve_normalise(dve, b + 2, p)
                dve.wait_ge(y_ready, b + 1)
                if bias is not None:
                    dve.wait_ge(bias_done, b + 1)
                nc.vector.tensor_tensor(s.X[:, b, :], s.ps[:, 1 + p, :], s.X[:, b, :], ALU.add).then_inc(res_done, 1)
            for b in range(2):
                fe.dve_normalise(dve, b, b)
            slots(dve, slot)
    fe.base += NB


def expert_gates(nc, s, t):
    E, GH, R = 8, 32, 16
    CAPACITY = int(3.0 * NB * P / E)
    step, var_ready, rstd_ready, gap_ready, exp_ready, mine_ready, all_ready = (s.sem("eg_" + n) for n in (
        "step", "var", "rstd", "gap", "exp", "mine", "all"))
    row = s.rows1
    gb1, gamma, beta = (row[:, 32 * k:32 * k + 32].unsqueeze(1).broadcast_to([P, NB, GH]) for k in range(3))
    gw2 = row[:, 96:352].rearrange("p (e j) -> p e j", e=E).unsqueeze(1).broadcast_to([P, NB, E, GH])
    gb2 = row[:, 352:360].unsqueeze(1).broadcast_to([P, NB, E])
    first = row[:, 360:368].unsqueeze(1).broadcast_to([P, NB, E])
    h, sm = s.gh, s.gsm
    over_h = lambda k: sm[:, k, :].unsqueeze(2).broadcast_to([P, NB, GH])
    over_e = lambda k: sm[:, k, :].unsqueeze(2).broadcast_to([P, NB, E])
    g = lambda k: s.gg[:, k, :, :]
    with nc.Block() as block:
        @block.vector
        def _(dve):
            link = linked(dve, step)
            v = nc.vector
            link(v.tensor_tensor(h[:, :, :], s.AGS[:, :, 128:160], gb1, ALU.add))
            link(v.tensor_reduce(sm[:, 0, :], h[:, :, :], AX.X, ALU.add))
            link(v.tensor_scalar(sm[:, 1, :], sm[:, 0, :], 1.0 / GH, None, ALU.mult))
            link(v.tensor_tensor(h[:, :, :], h[:, :, :], over_h(1), ALU.subtract))
            link(v.tensor_tensor(s.gprod[:, :, 0, :], h[:, :, :], h[:, :, :], ALU.mult))
            link(v.tensor_reduce(sm[:, 2, :], s.gprod[:, :, 0, :], AX.X, ALU.add))
            v.tensor_scalar(sm[:, 3, :], sm[:, 2, :], 1.0 / GH, LN_EPS, ALU.mult, ALU.add).then_inc(var_ready, 1)
            dve.wait_ge(rstd_ready, 1)
            link(v.tensor_tensor(h[:, :, :], h[:, :, :], over_h(4), ALU.mult))
            link(v.tensor_tensor(h[:, :, :], h[:, :, :], gamma, ALU.mult))
            link(v.tensor_tensor(h[:, :, :], h[:, :, :], beta, ALU.add))
            link(v.tensor_scalar(h[:, :, :], h[:, :, :], 0.0, None, ALU.max))
            link(v.tensor_tensor(s.gprod[:, :, :, :], h[:, :, :].unsqueeze(2).broadcast_to([P, NB, E, GH]), gw2, ALU.mult))
            link(v.tensor_reduce(g(0), s.gprod[:, :, :, :], AX.X, ALU.add))
            link(v.tensor_tensor(g(0), g(0), gb2, ALU.add))
            for k in range(2):
                link(v.tensor_reduce(sm[:, 5 + k, :], g(0), AX.X, ALU.max))
                link(v.tensor_tensor(g(3), g(0), over_e(5 + k), ALU.is_equal))
                link(v.tensor_tensor(g(3), g(3), first, ALU.mult))
                link(v.tensor_reduce(sm[:, 7, :], g(3), AX.X, ALU.max))
                link(v.tensor_tensor(g(1 + k), g(3), over_e(7), ALU.is_equal))
                link(v.tensor_reduce(s.gcount[:, k, :], g(1 + k).rearrange("p b e -> p e b"), AX.X, ALU.add))
                if k == 0:
                    link(v.scalar_tensor_tensor(g(0), g(1), -1e30, g(0), ALU.mult, ALU.add))
            v.tensor_tensor(sm[:, 8, :], sm[:, 6, :], sm[:, 5, :], ALU.subtract).then_inc(gap_ready, 1)
            dve.wait_ge(exp_ready, 1)
            link(v.tensor_scalar(sm[:, 10, :], sm[:, 9, :], 1.0, None, ALU.add))
            link(v.reciprocal(sm[:, 11, :], sm[:, 10, :]))
            link(v.tensor_tensor(sm[:, 12, :], sm[:, 9, :], sm[:, 11, :], ALU.mult))
            dve.wait_ge(all_ready, 1)
            link(v.tensor_scalar(s.gallow[:, :], s.ps[:, 7, 0:16], float(CAPACITY), 1.0 / R, ALU.is_le, ALU.mult))
            for k in range(2):
                link(v.tensor_tensor(g(1 + k), g(1 + k), over_e(11 + k), ALU.mult))
                link(v.tensor_tensor(g(1 + k), g(1 + k), s.gallow[:, 8 * k:8 * k + 8].unsqueeze(1).broadcast_to([P, NB, E]), ALU.mult))
            link(v.tensor_tensor(s.gw[:, :, :], g(1), g(2), ALU.add))

        @block.gpsimd
        def _(pool):
            pool.wait_ge(var_ready, 1)
            nc.gpsimd.tensor_tensor(sm[:, 4, :], sm[:, 3, :], s.minus_half[:, :], ALU.pow).then_inc(rstd_ready, 1)

        @block.scalar
        def _(act):
            act.wait_ge(gap_ready, 1)
            nc.scalar.activation(sm[:, 9, :], sm[:, 8, :], ACT.Exp).then_inc(exp_ready, 1)

        @block.tensor
        def _(pe):
            pe.wait_ge(gap_ready, 1)
            nc.tensor.matmul(s.ps[:, 7, 0:16], s.ones[:, :], s.gcount[:, :, :].rearrange("p k e -> p (k e)"), start=True, stop=True).then_inc(all_ready, 1)

    fe = s.front
    tw_ready, tw_turned, tw_taken, y_ready, res_done = (s.sem("ex_" + n) for n in ("tw", "turned", "taken", "y", "res"))
    with nc.Block() as block:
        @block.vector
        def _(dve):
            def weigh(b, p):
                if has_before(b, 2):
                    dve.wait_ge(tw_turned, b - 1)
                nc.vector.tensor_tensor(s.tw[:, p, :].rearrange("p (e r) -> p e r", e=E), s.AGS[:, b, 0:128].rearrange("p (e r) -> p e r", e=E),
                                        s.gw[:, b, :].unsqueeze(2).broadcast_to([P, E, R]), ALU.mult).then_inc(tw_ready, 1)

            def slot(b, p):
                if has_after(b, 2):
                    weigh(b + 2, p)
                dve.wait_ge(y_ready, b + 1)
                fe.before_write(dve, b, res_done)
                nc.vector.tensor_tensor(s.X[:, b, :], s.ps[:, 2 + p, :], s.X[:, b, :], ALU.add).then_inc(res_done, 1)
                fe.after_write(b, p)
            weigh(0, 0)
            weigh(1, 1)
            slots(dve, slot)
            fe.dve_last_moments(dve, res_done)

        @block.gpsimd
        def _(pool):
            slots(pool, lambda b, p: fe.pool_rstd(pool, b, p))

        @block.tensor
        def _(pe):
            def turn(b, p):
                pe.wait_ge(tw_ready, b + 1)
                if has_before(b, 2):
                    pe.wait_ge(tw_taken, b - 1)
                nc.tensor.transpose(s.ps[:, p, 0:P], s.tw[:, p, :], s.ident).then_inc(tw_turned, 1)

            def slot(b, p):
                if has_after(b, 1):
                    turn(b + 1, 1 - p)
                pe.wait_ge(tw_taken, b + 1)
                if has_before(b, 2):
                    pe.wait_ge(res_done, b - 1)
                nc.tensor.matmul(s.ps[:, 2 + p, :], s.twT[:, p, :], s.lB1, start=True, stop=True).then_inc(y_ready, 1)
            turn(0, 0)
            slots(pe, slot)

        @block.scalar
        def _(act):
            def slot(b, p):
                act.wait_ge(tw_turned, b + 1)
                if has_before(b, 2):
                    act.wait_ge(y_ready, b - 1)
                nc.scalar.activation(s.twT[:, p, :], s.ps[:, p, 0:P], ACT.Copy).then_inc(tw_taken, 1)
            slots(act, slot)
    fe.mbase += NB


def grouped_query_attention(nc, s, t):
    sem = s.sem
    ct_in, w_in = (sem("l2_ct_in0"), sem("l2_ct_in1")), sem("l2_w_in")
    xn_ready, xt_ready, xt_taken, q_ready, qhi_done, qlo_done, kr_ready, khi_done, kx_done, v_ready, v_done = (sem("l2_" + n) for n in (
        "xn", "xt_ready", "xt_taken", "q_ready", "qhi", "qlo", "kr_ready", "khi", "kx", "v_ready", "v_done"))
    o_ready, res_done = sem("l2_o_ready"), sem("l2_res")
    cleared = sem("l2_cleared")
    A, B, ps, fe = s.A, s.B, s.ps, s.front
    loads = [(s.wq2[:, :, :, :], t["wq2"]), (s.wk2[:, :, :, :], t["wk2"]), (s.wv2[:, :, :], t["wv2"]), (s.wo2[:, :, :], t["wo2"]), (s.neg[96:128], t["neg2"])]
    with nc.Block() as block:
        @block.sync
        def _(sp):
            for to, of in loads:
                sp.dma_start(to, of).then_inc(w_in, 16)

        @block.gpsimd
        def _(pool):
            nc.gpsimd.memset(s.VE[:, :, :, :, :], 0.0).then_inc(cleared, 1)

        @block.vector
        def _(dve):
            nc.vector.memset(s.Q[96:128, :, :, :].bitcast(F32), 0.0).then_inc(cleared, 1)
            dve.wait_ge(w_in, 16 * len(loads))
            for p in range(2):
                nc.vector.tensor_copy(s.KB[96:128, p, :, :], s.neg[96:128, :, :]).then_inc(cleared, 1)

    def load(sp, b, p):
        if has_before(b, 2):
            sp.wait_ge(v_ready, b - 1)
        sp.dma_start(s.ctxT_s[:, p, :, :], t["ctxT"][b].rearrange("(c p) k -> p c k", p=P)).then_inc(ct_in[p], 16)

    class prep:
        @staticmethod
        def pe_queries(pe, b, p):
            pe.wait_ge(xn_ready, b + 1)
            if has_before(b, 1):
                pe.wait_ge(kx_done, b)
            for c in range(DC):
                last = nc.tensor.transpose(ps[:, B, c * P:(c + 1) * P], s.xn[:, 0, c * P:(c + 1) * P], s.ident)
            last.then_inc(xt_ready, 1)
            pe.wait_ge(xt_taken, b + 1)
            if has_before(b, 1):
                pe.wait_ge(s.max_rows, b - 1 if has_before(b, 2) else 1)
            if has_before(b, 1):
                pe.wait_ge(v_done, b)
            for r in range(4):
                for c in range(DC):
                    last = nc.tensor.matmul(ps[:, A, r * P:(r + 1) * P], s.wq2[:, c, r, :], s.xnT[:, 0, c, :], start=(c == 0), stop=(c == DC - 1))
            last.then_inc(q_ready, 1)

        @staticmethod
        def pe_keys(pe, b, p):
            pe.wait_ge(ct_in[p], 8 * (b - p) + 16)
            for g in range(4):
                for c in range(DC):
                    last = nc.tensor.matmul(ps[0:96, B, g * P:(g + 1) * P], s.wk2[:, c, g, :], s.ctxT_s[:, p, c, :], start=(c == 0), stop=(c == DC - 1))
            last.then_inc(kr_ready, 1)
            pe.wait_ge(qlo_done, b + 1)
            for c in range(DC):
                last = nc.tensor.matmul(ps[:, A, 0:P], s.ctxT_s[:, p, c, :], s.wv2[:, c, :], start=(c == 0), stop=(c == DC - 1))
            last.then_inc(v_ready, 1)

        @staticmethod
        def act_context(act, b, p):
            act.wait_ge(xt_ready, b + 1)
            if has_before(b, 1):
                act.wait_ge(q_ready, b)
            nc.scalar.activation(s.xnT[:, 0, :, :].rearrange("p c t -> p (c t)"), ps[:, B, :], ACT.Copy).then_inc(xt_taken, 1)

        @staticmethod
        def act_queries(act, b, p):
            act.wait_ge(q_ready, b + 1)
            if has_before(b, 1):
                act.wait_ge(s.q_packed, 192 * b)
            nc.scalar.activation(s.QH[:, :], ps[:, A, :], ACT.Copy).then_inc(qhi_done, 1)

        @staticmethod
        def dve_queries(dve, b, p):
            if has_before(b, 1):
                dve.wait_ge(xt_ready, b)
            nc.vector.tensor_scalar(s.xn[:, 0, :], s.X[:, b, :], s.mean[:, b, :], s.rstd[:, b, :], ALU.subtract, ALU.mult).then_inc(xn_ready, 1)
            dve.wait_ge(qhi_done, b + 1)
            nc.vector.tensor_tensor(s.QL[:, :], ps[:, A, :], s.QH[:, :].bitcast(F32), ALU.subtract).then_inc(qlo_done, 1)

        @staticmethod
        def dve_keys(dve, b, p):
            dve.wait_ge(kr_ready, b + 1)
            if has_before(b, 1):
                dve.wait_ge(s.kb_ready, b)
            nc.vector.tensor_copy(s.KH[0:96, :, :].rearrange("p g k -> p (g k)"), ps[0:96, B, :]).then_inc(khi_done, 1)
            dve.wait_ge(khi_done, b + 1)
            nc.vector.tensor_tensor(s.KH[32:64, :, :].rearrange("p g k -> p (g k)"), ps[32:64, B, :],
                                    s.KH[32:64, :, :].rearrange("p g k -> p (g k)").bitcast(F32), ALU.subtract).then_inc(kx_done, 1)
            dve.wait_ge(v_ready, b + 1)
            nc.vector.tensor_copy(s.VS[:, :], ps[:, A, 0:P]).then_inc(v_done, 1)

        @staticmethod
        def pool(pool, b, p):
            spread(nc, s, pool, b, p, 2, s.mask2, kx_done, v_done)

        @staticmethod
        def sp(sp, b, p):
            pack_queries(nc, s, sp, b, p, qlo_done)

    class tail:
        written = res_done

        @staticmethod
        def wait_msg_free(dve, b):
            dve.wait_ge(o_ready, b)

        @staticmethod
        def pe_early(pe, b, p):
            pass

        @staticmethod
        def pe(pe, b, p):
            pe.wait_ge(s.msg_done, b + 1)
            for r in range(4):
                last = nc.tensor.matmul(ps[:, 5, :], s.msg[:, r * P:(r + 1) * P], s.wo2[:, r, :], start=(r == 0), stop=(r == 3))
            last.then_inc(o_ready, 1)

        @staticmethod
        def act(act, b, p):
            pass

        @staticmethod
        def dve(dve, b, p):
            dve.wait_ge(o_ready, b + 1)
            fe.before_write(dve, b, res_done)
            nc.vector.tensor_tensor(s.X[:, b, :], ps[:, 5, :], s.X[:, b, :], ALU.add).then_inc(res_done, 1)
            fe.after_write(b, p)

    s.v_done = v_done
    packed_attention(nc, s, "l2", 2, 16 ** -0.5, load, prep, tail)


def routed_ffn(nc, s, t):
    E, R = 16, 8
    sem = s.sem
    fe = s.front
    step, log_done = sem("rf_step"), sem("rf_log")
    w_in = sem("rf_w_in")
    (y_open, y_ready, zl_ready, l_done, max_done, neg_done, exp_done, c_done, sum_done, inv_done, alpha_done, zw_done, z_turned, z_taken,
     bias_done, res_done) = (sem("rf_" + n) for n in ("y_open", "y", "zl", "l", "max", "neg", "exp", "c", "sum", "inv", "alpha", "zw", "turned", "taken", "bias", "res"))
    loads = [(s.w2f[:, :, :], t["w2f"]), (s.zl2[:, :, :], t["zl2"]), (s.lB2, t["lB2"]), (s.rows2[:, 0:512], t["b_base"].broadcast_to([P, D])),
             (s.rows2[:, 512:560], t["rows2"].broadcast_to([P, 48])), (s.active[:, :], t["active"].broadcast_to([P, 4]))]
    iota, rb, prior = (s.rows2[:, 512 + 16 * k:528 + 16 * k] for k in range(3))
    with nc.Block() as block:
        @block.sync
        def _(sp):
            for to, of in loads:
                sp.dma_start(to, of).then_inc(w_in, 16)

        @block.scalar
        def _(act):
            act.wait_ge(step, 1)
            nc.scalar.activation(s.ladj[:, 1, :], s.ladj[:, 0, :], ACT.Ln).then_inc(log_done, 1)

        @block.vector
        def _(dve):
            link = linked(dve, step)
            dve.wait_ge(w_in, 16 * len(loads))
            link(nc.vector.tensor_scalar(s.ladj[:, 0, :], prior, 1e-12, None, ALU.add))
            link(nc.vector.tensor_copy(s.activef[:, :], s.active[:, :]))
            link(nc.vector.tensor_scalar(s.cnt[:, :], iota, s.activef[:, 0:1], None, ALU.is_equal))
            for j in range(1, 4):
                link(nc.vector.scalar_tensor_tensor(s.cnt[:, :], iota, s.activef[:, j:j + 1], s.cnt[:, :], ALU.is_equal, ALU.add))
            link(nc.vector.tensor_scalar(s.ladj[:, 2, :], s.cnt[:, :], 0.0, -1e30, ALU.is_equal, ALU.mult))
            link(nc.vector.tensor_tensor(s.ladj[:, 3, :], s.ladj[:, 2, :], rb, ALU.add))
            dve.wait_ge(log_done, 1)
            link(nc.vector.tensor_tensor(s.ladj[:, 4, :], s.ladj[:, 3, :], s.ladj[:, 1, :], ALU.add))

    with nc.Block() as block:
        @block.gpsimd
        def _(pool):
            def slot(b, p):
                pool.wait_ge(fe.xn_ready, fe.base + b + 1)
                nc.gpsimd.tensor_tensor(s.X[:, b, :], s.X[:, b, :], s.rows2[:, 0:512], ALU.add).then_inc(bias_done, 1)
                if has_before(b, 2):
                    fe.pool_rstd(pool, b - 2, p)
            slots(pool, slot)
            fe.pool_rstd(pool, NB - 2, 0)
            fe.pool_rstd(pool, NB - 1, 1)

        @block.tensor
        def _(pe):
            def turn(b, p):
                pe.wait_ge(zw_done, b + 1)
                pe.wait_ge(z_taken, b)
                nc.tensor.transpose(s.ps[:, 5, 0:P], s.zw[:, p, :], s.ident).then_inc(z_turned, 1)

            def experts(b, p):
                pe.wait_ge(z_taken, b + 1)
                nc.tensor.matmul(s.ps[:, 1 + p, :], s.zwT[:, p, :], s.lB2, start=False, stop=True).then_inc(y_ready, 1)

            def slot(b, p):
                pe.wait_ge(fe.ready, fe.base + b + 1)
                if has_before(b, 2):
                    pe.wait_ge(zw_done, b - 1)
                for c in range(DC):
                    last = nc.tensor.matmul(s.ps[:, 3 + p, 0:144], s.xnT[:, p, c, :], s.zl2[:, c, :], start=(c == 0), stop=(c == DC - 1))
                last.then_inc(zl_ready, 1)
                if has_before(b, 1):
                    turn(b - 1, 1 - p)
                if has_before(b, 2):
                    pe.wait_ge(res_done, b - 1)
                for c in range(DC):
                    last = nc.tensor.matmul(s.ps[:, 1 + p, :], s.xnT[:, p, c, :], s.w2f[:, c, :], start=(c == 0), stop=False)
                last.then_inc(y_open, 1)
                if has_after(b, 2):
                    fe.pe_turn(pe, b + 2, p)
                if has_before(b, 1):
                    experts(b - 1, 1 - p)
            fe.pe_turn(pe, 0, 0)
            fe.pe_turn(pe, 1, 1)
            slots(pe, slot)
            turn(NB - 1, 1)
            experts(NB - 1, 1)

        @block.scalar
        def _(act):
            def take(b, p):
                act.wait_ge(fe.turned, fe.base + b + 1)
                if has_before(b, 2):
                    act.wait_ge(y_open, b - 1)
                nc.scalar.activation(s.xnT[:, p, :, :].rearrange("p c t -> p (c t)"), s.ps[:, 0, :], ACT.Copy).then_inc(fe.ready, 1)

            def take_z(b, p):
                act.wait_ge(z_turned, b + 1)
                if has_before(b, 2):
                    act.wait_ge(y_ready, b - 1)
                nc.scalar.activation(s.zwT[:, p, :], s.ps[:, 5, 0:P], ACT.Copy).then_inc(z_taken, 1)

            def slot(b, p):
                if has_before(b, 1):
                    take_z(b - 1, 1 - p)
                act.wait_ge(neg_done, b + 1)
                if has_before(b, 2):
                    act.wait_ge(c_done, b - 1)
                nc.scalar.activation(s.rex[:, p, :], s.rl[:, p, :], ACT.Exp, bias=s.negm[:, p:p + 1]).then_inc(exp_done, 1)
                if has_after(b, 2):
                    take(b + 2, p)
            take(0, 0)
            take(1, 1)
            slots(act, slot)
            take_z(NB - 1, 1)

        @block.vector
        def _(dve):
            v = nc.vector

            def add(b, p):
                dve.wait_ge(y_ready, b + 1)
                dve.wait_ge(bias_done, b + 1)
                v.tensor_tensor(s.X[:, b, :], s.ps[:, 1 + p, :], s.X[:, b, :], ALU.add).then_inc(res_done, 1)

            def slot(b, p):
                dve.wait_ge(zl_ready, b + 1)
                if has_before(b, 2):
                    dve.wait_ge(exp_done, b - 1)
                v.tensor_tensor(s.rl[:, p, :], s.ps[:, 3 + p, 128:144], s.ladj[:, 4, :], ALU.add).then_inc(l_done, 1)
                dve.wait_ge(l_done, b + 1)
                dve.wait_ge(neg_done, b)
                fe.late_waits(dve, b, res_done)
                v.tensor_reduce(s.smax[:, p:p + 1], s.rl[:, p, :], AX.X, ALU.max).then_inc(max_done, 1)
                fe.late_stats(b, p)
                dve.wait_ge(max_done, b + 1)
                v.tensor_scalar(s.negm[:, p:p + 1], s.smax[:, p:p + 1], -1.0, None, ALU.mult).then_inc(neg_done, 1)
                dve.wait_ge(exp_done, b + 1)
                dve.wait_ge(alpha_done, b)
                v.tensor_tensor(s.rc[:, p, :], s.rex[:, p, :], s.cnt[:, :], ALU.mult).then_inc(c_done, 1)
                dve.wait_ge(c_done, b + 1)
                dve.wait_ge(inv_done, b)
                v.tensor_reduce(s.den[:, p:p + 1], s.rc[:, p, :], AX.X, ALU.add).then_inc(sum_done, 1)
                dve.wait_ge(sum_done, b + 1)
                v.reciprocal(s.rd[:, p:p + 1], s.den[:, p:p + 1]).then_inc(inv_done, 1)
                dve.wait_ge(inv_done, b + 1)
                dve.wait_ge(zw_done, b)
                v.tensor_scalar(s.ra[:, p, :], s.rc[:, p, :], s.rd[:, p:p + 1], 16.0 / 8.0, ALU.mult, ALU.mult).then_inc(alpha_done, 1)
                dve.wait_ge(alpha_done, b + 1)
                if has_before(b, 2):
                    dve.wait_ge(z_turned, b - 1)
                v.tensor_tensor(s.zw[:, p, :].rearrange("p (e r) -> p e r", e=E), s.ps[:, 3 + p, 0:128].rearrange("p (e r) -> p e r", e=E),
                                s.ra[:, p, :].unsqueeze(2).broadcast_to([P, E, R]), ALU.mult).then_inc(zw_done, 1)
                if has_after(b, 2):
                    fe.dve_normalise(dve, b + 2, p)
                if has_before(b, 1):
                    fe.late_before_write(dve, b)
                    add(b - 1, 1 - p)
                    fe.late_after_write(b, p)
            for b in range(2):
                fe.dve_normalise(dve, b, b)
            slots(dve, slot)
            add(NB - 1, 1)
            fe.late_last_moments(dve, res_done)
    fe.base += NB
    fe.mbase += NB


def dequantise(nc, s, t):
    LANES = 0x11111111
    w_in, step, bit_step, code_done, hot_done, added, turned, taken = (s.sem("dq_" + n) for n in ("w_in", "step", "bit", "code", "hot", "added", "turned", "taken"))
    with nc.Block() as block:
        @block.sync
        def _(sp):
            sp.dma_start(s.qw[:, :, :], t["qw"]).then_inc(w_in, 16)
            sp.dma_start(s.lut[:, :, :], t["lut4"].rearrange("(c p) v -> p c v", p=P)).then_inc(w_in, 16)

        @block.vector
        def _(dve):
            v = nc.vector
            link = linked(dve, step)
            dve.wait_ge(w_in, 32)
            for r in range(4):
                link(v.tensor_scalar(s.T4[:, :, r], s.qw[:, 0, :], r, LANES, ALU.logical_shift_right, ALU.bitwise_and))
                for p in range(1, 4):
                    link(v.tensor_scalar(s.tq[:, :], s.qw[:, p, :], r, LANES, ALU.logical_shift_right, ALU.bitwise_and))
                    link(v.scalar_tensor_tensor(s.T4[:, :, r], s.tq[:, :], p, s.T4[:, :, r], ALU.logical_shift_left, ALU.bitwise_or))
            for a in range(8):
                link(v.tensor_scalar(s.code[:, :, a, :], s.T4[:, :, :], 4 * a, 15, ALU.logical_shift_right, ALU.bitwise_and))
            link(v.tensor_copy(s.codef[:, :, :], s.code[:, :, :, :].rearrange("p (o w) a r -> p o (w a r)", o=DC)))
            n = 0
            for o in range(DC):
                for k in range(16):
                    if n >= 2:
                        dve.wait_ge(added, n - 1)
                    v.tensor_scalar(s.hot[:, n % 2, :], s.codef[:, o, :], float(k), s.lut[:, o, k:k + 1], ALU.is_equal, ALU.mult).then_inc(hot_done, 1)
                    n += 1

        @block.gpsimd
        def _(pool):
            n = 0
            for o in range(DC):
                for k in range(16):
                    pool.wait_ge(hot_done, n + 1)
                    if k:
                        pool.wait_ge(added, n)
                        nc.gpsimd.tensor_tensor(s.WO[:, o, :], s.WO[:, o, :], s.hot[:, n % 2, :], ALU.add).then_inc(added, 1)
                    else:
                        nc.gpsimd.tensor_copy(s.WO[:, o, :], s.hot[:, n % 2, :]).then_inc(added, 1)
                    n += 1

        @block.tensor
        def _(pe):
            for o in range(DC):
                pe.wait_ge(added, 16 * (o + 1))
                if o >= 2:
                    pe.wait_ge(taken, o - 1)
                for c in range(DC):
                    last = nc.tensor.transpose(s.ps[:, o % 2, c * P:(c + 1) * P], s.WO[:, o, c * P:(c + 1) * P], s.ident)
                last.then_inc(turned, 1)

        @block.scalar
        def _(act):
            for o in range(DC):
                act.wait_ge(turned, o + 1)
                nc.scalar.activation(s.WL[:, :, o * P:(o + 1) * P], s.ps[:, o % 2, :].rearrange("p (c o) -> p c o", c=DC), ACT.Copy).then_inc(taken, 1)


def build(nc, t, out, stop=99):
    s = Shared()
    with ExitStack() as top:
        def sb_in(stack):
            return lambda name, shape, dt=F32: stack.enter_context(nc.sbuf_tensor(name, shape, dt))
        sb = sb_in(top)
        s.retired, s.current = [], []

        def sem(name):
            handle = nc.alloc_semaphore(name=name)
            s.current.append(handle)
            return handle
        s.sem = sem
        s.X = sb("X", [P, NB, D])
        s.ident = sb("ident", [P, P])[:]
        s.ident_bf = sb("ident_bf", [P, P], BF16)
        s.ones = sb("ones", [P, P])
        s.ones_blk = {4: sb("ones4", [P, 4, 32])[:], 2: sb("ones2", [P, 2, 32])[:]}
        s.mask4 = sb("mask4", [96, 4])[:]
        s.mask2 = sb("mask2", [96, 2])[:]
        s.ones_ready = s.sem("ones_ready")
        s.eps = sb("eps", [P, 1])
        s.minus_half, s.var_eps = sb("minus_half", [P, NB]), sb("var_eps", [P, NB])
        s.mstats, s.mmv, s.mean = sb("mstats", [P, 2, 6]), sb("mmv", [P, 2, 2]), sb("mean", [P, NB, 1])
        s.stats = sb("stats", [P, NB, 6])
        s.mv = sb("mv", [P, NB, 2])
        s.rstd = sb("rstd", [P, NB, 1])
        s.xn = sb("xn", [P, 2, D])
        s.xnT = sb("xnT", [P, 2, DC, P])
        s.ps = top.enter_context(nc.psum_tensor("ps", [P, 8, 512], F32))
        s.A, s.B = 6, 7
        s.wabs = sb("wabs", [P, PAIRS, 3])
        s.x_out = s.sem("x_out")
        s.front = Front(nc, s)

        def packed_buffers(sb, tag, HL):
            s.Q = sb("Q" + tag, [P, 2, 4, 512], F32R)
            s.KB = sb("KB" + tag, [P, 2, 4, HL * P], F32R)
            s.VE = sb("VE" + tag, [P, 2, 4, HL, 32])
            s.QH, s.QL = sb("QH" + tag, [P, 512], F32R), sb("QL" + tag, [P, 512], F32R)
            s.KF, s.KH = sb("KF" + tag, [96, 4, P]), sb("KH" + tag, [96, 4, P], F32R)
            s.VS = sb("VS" + tag, [P, P])
            s.PT = sb("PT" + tag, [P, 8, 512])
            s.mx = sb("mx" + tag, [P, 4, 4, HL])
            s.m8 = sb("m8" + tag, [P, 4, 4, 2, HL], BF16)
            s.rden, s.msg = sb("rden" + tag, [P, 512]), sb("msg" + tag, [P, 512])
            s.ctxT_s = sb("ctxT_s" + tag, [P, 2, DC, P])
            s.neg = sb("neg" + tag, [P, 4, HL * P])

        with ExitStack() as phase:
            sb = sb_in(phase)
            packed_buffers(sb, "0", 4)
            s.XN = sb("XN", [P, NB, D])
            s.wq0, s.wk0, s.wm0 = (sb(n, [P, P])[:] for n in ("wq0", "wk0", "wm0"))
            s.wk0_rep = sb("wk0_rep", [P, 4, 96])[:]
            s.proj = sb("proj", [P, DC, P])[:]
            s.w1m0, s.w1x0 = sb("w1m0", [P, 256])[:], sb("w1x0", [P, 256])[:]
            s.w2_0 = sb("w2_0", [P, 2, P])[:]
            s.cols0 = sb("cols0", [P, 18])[:]
            s.bk0_row = sb("bk0_row", [P, P])[:]
            s.colsum, s.colsum_row = sb("colsum", [P, 1]), sb("colsum_row", [P, P])
            s.weff, s.bn = sb("weff", [P, 256]), sb("bn", [P, 14])
            s.C, s.H = sb("C", [P, P]), sb("H", [P, 2, 512])
            s.SW, s.SB, s.wscr = sb("SW", [P, 2, 2, 3, D]), sb("SB", [P, 2, 2, 3, D]), sb("wscr", [P, 2, D], BF16)
            s.current = []
            setup(nc, s, t)
            linear_attention_of_channels(nc, s, t)
        s.retired, s.current = s.current, []
        if stop >= 1:
            with ExitStack() as phase:
                sb = sb_in(phase)
                s.XH, s.XLO = (sb(n, [P, DC, NB, P], F32R) for n in ("XH", "XLO"))
                s.RW, s.RB, s.SG = sb("RW", [P, 2, 2, D]), sb("RB", [P, 2, 2, D]), sb("SG", [P, 2, 2, D], BF16)
                s.WH, s.WLO = (sb(n, [P, 2, 2, D], F32R) for n in ("WH", "WLO"))
                s.HF, s.SL = sb("HF", [P, 2 * PAIRS, 2, 512]), sb("SL", [P, 2, 2, 512])
                s.HH, s.HLO = (sb(n, [P, 2, 2, 512], F32R) for n in ("HH", "HLO"))
                s.wsum, s.coeff = sb("wsum", [P, 3]), sb("coeff", [P, 3])
                binary_gated_ffn(nc, s, t)
            for handle in s.retired:
                nc.release_semaphore(handle)
        sb = sb_in(top)
        s.ctx = sb("ctx", [P, NB, D])
        s.ctxT = sb("ctxT", [P, DC, NB, P])
        s.E, s.EWT, s.SR = sb("E", [P, 2, P]), sb("EWT", [P, 2, P]), sb("SR", [P, 2, P])
        s.smax, s.negm, s.den, s.rd = (sb(n, [P, 2]) for n in ("smax", "negm", "den", "rd"))
        if stop >= 2:
            with ExitStack() as phase:
                sb = sb_in(phase)
                s.wq1, s.wk1, s.mt1 = (sb(n, [P, DC, D]) for n in ("wq1", "wk1", "mt1"))
                s.cols1, s.bqk, s.v1, s.vrep = sb("cols1", [P, 8]), sb("bqk", [P, 8]), sb("v1", [P, 8]), sb("vrep", [P, DC, P])
                s.G, s.R = sb("G", [P, DC, NB, P]), sb("R", [P, NB, P])
                fold_text_attention(nc, s, t)
                context_attention(nc, s, "l1", s.G, s.R, D ** -0.5)

        def load_all(loads):
            with nc.Block() as block:
                done = s.sem(f"in{len(loads)}_{load_all.n}")
                load_all.n += 1

                @block.sync
                def _(sp):
                    for to, of in loads:
                        sp.dma_start(to, of).then_inc(done, 16)
                    sp.wait_ge(done, 16 * len(loads))
        load_all.n = 0
        if stop >= 3:
            with ExitStack() as phase:
                sb = sb_in(phase)
                s.w1f, s.ag1 = sb("w1f", [P, DC, D]), sb("ag1", [P, DC, 160])
                s.rows1, s.lB1 = sb("rows1", [P, 368]), sb("lB1", [P, D])[:]
                s.AGS, s.gh, s.gsm, s.gg = sb("AGS", [P, NB, 160]), sb("gh", [P, NB, 32]), sb("gsm", [P, 13, NB]), sb("gg", [P, 4, NB, 8])
                s.gprod, s.gcount, s.gallow, s.gw = sb("gprod", [P, NB, 8, 32]), sb("gcount", [P, 2, 8]), sb("gallow", [P, 16]), sb("gw", [P, NB, 8])
                s.tw, s.twT = sb("tw", [P, 2, P]), sb("twT", [P, 2, P])
                load_all([(s.w1f[:, :, :], t["w1f"]), (s.ag1[:, :, :], t["ag1"]), (s.lB1, t["lB1"]), (s.rows1[:, :], t["rows1"].broadcast_to([P, 368]))])
                dense(nc, s, "l1f", s.w1f, s.ag1, None)
                expert_gates(nc, s, t)
        if stop >= 4:
            with ExitStack() as phase:
                sb = sb_in(phase)
                packed_buffers(sb, "2", 2)
                s.wq2, s.wk2, s.wv2, s.wo2 = sb("wq2", [P, DC, 4, P]), sb("wk2", [P, DC, 4, 96]), sb("wv2", [P, DC, P]), sb("wo2", [P, 4, D])
                grouped_query_attention(nc, s, t)
        if stop >= 5:
            with ExitStack() as phase:
                sb = sb_in(phase)
                s.w2f, s.zl2, s.lB2 = sb("w2f", [P, DC, D]), sb("zl2", [P, DC, 144]), sb("lB2", [P, D])[:]
                s.rows2, s.active, s.activef = sb("rows2", [P, 560]), sb("active", [P, 4], I32), sb("activef", [P, 4])
                s.ladj, s.cnt = sb("ladj", [P, 5, 16]), sb("cnt", [P, 16])
                s.rl, s.rex, s.rc, s.ra = (sb(n, [P, 2, 16]) for n in ("rl", "rex", "rc", "ra"))
                s.zw, s.zwT = sb("zw", [P, 2, P]), sb("zwT", [P, 2, P])
                routed_ffn(nc, s, t)
        if stop >= 6:
            with ExitStack() as phase:
                context_attention(nc, s, "l3", s.ctxT, None, 1.0)
        if stop >= 7:
            with ExitStack() as phase:
                sb = sb_in(phase)
                s.WL, s.b3 = sb("WL", [P, DC, D]), sb("b3", [P, D])
                s.qw, s.lut, s.T4, s.tq = sb("qw", [P, 4, 64], I32), sb("lut", [P, DC, 16]), sb("T4", [P, 64, 4], I32), sb("tq", [P, 64], I32)
                s.code, s.codef = sb("code", [P, 64, 8, 4], I32), sb("codef", [P, DC, D])
                s.hot, s.WO = sb("hot", [P, 2, D]), sb("WO", [P, DC, D])
                load_all([(s.b3[:, :], t["b3"].broadcast_to([P, D]))])
                dequantise(nc, s, t)
                dense(nc, s, "l3f", s.WL, None, s.b3[:, :], out)
                return

        with nc.Block() as block:
            @block.sync
            def _(sp):
                sp.dma_start(out.rearrange("b p d -> p b d"), s.X[:, :, :]).then_inc(s.x_out, 16)
                sp.wait_ge(s.x_out, 16)


def lay_out(inputs):
    import numpy as np
    a = {k: np.asarray(v) for k, v in inputs.items()}
    cont = np.ascontiguousarray
    m = {}
    m["x"] = a["x"]
    m["ctxT"] = cont(a["ctx_4096"].transpose(0, 2, 1))
    m["ident"] = np.eye(P, dtype=np.float32)
    chan = np.array([d * 16 + 4 * g + h for g in range(4) for h in range(4) for d in range(8)])
    m["wq0"] = cont(a["L0_xattn_to_q_w"].T[:, chan])
    m["wk0"] = cont(a["L0_xattn_to_k_w"].T[:, chan])
    m["wk0_rep"] = cont(np.tile(m["wk0"].reshape(P, 4, 1, 32), (1, 1, 3, 1)).reshape(P, 4, 96))
    m["proj_k"] = a["L0_xattn_proj_k"]
    m["wm0"] = cont(a["L0_xattn_merge_w"][:, chan])
    def ffn(n1, n3, n2):
        up = [a[n].reshape(PAIRS, 2, P, DC, P).transpose(0, 4, 1, 3, 2).reshape(PAIRS, P, 2, D) for n in (n1, n3)]
        return cont(np.stack([*up, a[n2].T.reshape(PAIRS, 2, P, D).transpose(0, 2, 1, 3)], axis=3))
    m["base"] = ffn(*(f"L0_ffn_mean_w{n}" for n in (1, 3, 2)))
    m["w"] = ffn(*(f"L0_ffn_w{n}" for n in (1, 3, 2)))
    m["wq1"], m["wk1"] = (cont(a["L1_xattn_" + n].reshape(DC, P, D).transpose(1, 0, 2)) for n in ("Wq", "Wk"))
    m["cols1"] = cont(np.concatenate([a["L1_xattn_" + n].reshape(DC, P).T for n in ("bq", "bk")], axis=1))
    m["ctxT_all"] = cont(a["ctx_4096"].reshape(NB, P, DC, P).transpose(3, 2, 0, 1))
    m["ctx"] = cont(a["ctx_4096"].transpose(1, 0, 2))
    by_chunk = lambda w: cont(w.reshape(DC, P, -1).transpose(1, 0, 2))
    m["w1f"] = by_chunk(a["L1_ffn_weight"].T)
    m["ag1"] = by_chunk(np.concatenate([a["L1_ffn_lora_A"].transpose(1, 0, 2).reshape(D, P), a["L1_ffn_gw1"].T], axis=1))
    m["lB1"] = a["L1_ffn_lora_B"].reshape(P, D)
    m["rows1"] = np.concatenate([a["L1_ffn_gb1"], a["L1_ffn_ln_gamma"], a["L1_ffn_ln_beta"], a["L1_ffn_gw2"].reshape(-1),
                                 a["L1_ffn_gb2"], 8.0 - np.arange(8, dtype=np.float32)])[None, :]
    m["wq2"] = cont(a["L2_xattn_Wq"].reshape(DC, P, 8, 4, 16).transpose(1, 0, 3, 2, 4).reshape(P, DC, 4, P))
    m["wk2"] = cont(np.tile(a["L2_xattn_Wk"].reshape(DC, P, 4, 1, 32), (1, 1, 1, 3, 1)).transpose(1, 0, 2, 3, 4).reshape(P, DC, 4, 96))
    m["wv2"] = by_chunk(a["L2_xattn_Wv"])
    m["wo2"] = cont(a["L2_xattn_Wo"].reshape(8, 4, 16, D).transpose(0, 2, 1, 3).reshape(P, 4, D))
    m["w2f"] = by_chunk(a["L2_ffn_W_base"].T)
    m["zl2"] = by_chunk(np.concatenate([a["L2_ffn_lora_A"].reshape(P, D).T, a["L2_ffn_router_W"].T], axis=1))
    m["lB2"] = cont(a["L2_ffn_lora_B"].transpose(0, 2, 1).reshape(P, D))
    m["b_base"] = a["L2_ffn_b_base"][None, :]
    m["rows2"] = np.concatenate([np.arange(16, dtype=np.float32), a["L2_ffn_router_b"], a["L2_ffn_domain_prior"]])[None, :]
    m["active"] = a["L2_ffn_active"][None, :]
    m["qw"] = cont(a["L3_ffn_qweight"][:4].reshape(4, DC, P, 16).transpose(2, 0, 1, 3).reshape(P, 4, 64))
    m["lut4"] = a["L3_ffn_lut4"]
    m["b3"] = a["L3_ffn_bias"][None, :]
    w1t = a["L0_xattn_mlp_w1"].T
    m["w1x0"], m["w1m0"] = cont(w1t[:P]), cont(w1t[P:])
    m["w2_0"] = cont(a["L0_xattn_mlp_w2"].T.reshape(2, P, P).transpose(1, 0, 2))
    bk = a["L0_xattn_to_k_b"][chan]
    two = lambda n: a[n].reshape(2, P).T
    m["cols0"] = cont(np.concatenate([
        a["L0_xattn_to_q_b"][chan][:, None], np.tile(bk.reshape(4, 32).T, (4, 1)), np.zeros((P, 1), np.float32),
        a["L0_xattn_merge_b"][:, None], a["L0_xattn_mlp_b2"][:, None], two("L0_xattn_bn_gamma"), two("L0_xattn_bn_beta"),
        two("L0_xattn_bn_mean"), two("L0_xattn_bn_var"), two("L0_xattn_mlp_b1")], axis=1))
    m["bk0_row"] = cont(bk[None, :])
    for HL in (4, 2):
        w = 32 // HL
        head = np.arange(32) // w
        eye = np.eye(HL, dtype=np.float32)
        m[f"mask{HL}"] = cont(np.tile(eye[head], (3, 1)))
        m[f"ones{HL}"] = cont(np.tile(eye[:, head][None], (P, 1, 1)))
        neg = np.zeros((4, 2, HL, 4, HL, P), np.float32)
        for g in range(4):
            for h in range(HL):
                neg[g, :, h, g, h, :] = -1.0
        full = np.zeros((32, 4, HL * P), np.float32)
        full[:8 * HL] = neg.reshape(8 * HL, 4, HL * P)
        m[f"neg{HL}"] = full
    return m


def kernel(**inputs):
    import concourse.bacc as _bacc
    from concourse.bass_utils import run_bass_kernel_spmd as _run

    nc = _bacc.Bacc("TRN2", target_bir_lowering=False, num_devices=1)
    arrays = {f"in_{k}": v for k, v in lay_out(inputs).items()}
    t = {k[3:]: nc.dram_tensor(k, v.shape, mybir.dt.from_np(v.dtype), kind="ExternalInput").ap() for k, v in arrays.items()}
    out = nc.dram_tensor("out", (NB, P, D), F32, kind="ExternalOutput").ap()
    build(nc, t, out)
    return _run(nc, [arrays], core_ids=[0]).results[0]["out"]
```

```python
from contextlib import ExitStack

import numpy as np

import concourse.bass as bass
from concourse import mybir

F32 = mybir.dt.float32
F32R = mybir.dt.float32r
BF16 = mybir.dt.bfloat16
I32 = mybir.dt.int32
U8 = mybir.dt.uint8
ALU = mybir.AluOpType
ACT = mybir.ActivationFunctionType
AX = mybir.AxisListType

P = 128
NB = 8
D = 512
DC = D // P
LN_EPS = 1e-5
BN_EPS = 1e-3


CONSTANTS = 4


class Shared:
    pass


def symbolic(b):
    return not isinstance(b, int)


def has_before(b, n):
    return symbolic(b) or b >= n


def has_after(b, n, of=NB):
    return symbolic(b) or b + n < of


def slots(engine, slot, n=NB):
    slot(0, 0)
    slot(1, 1)
    with engine.Fori(1, n // 2 - 1) as i:
        for p in range(2):
            slot(2 * i + p, p)
    slot(n - 2, 0)
    slot(n - 1, 1)


class NoSide:
    @staticmethod
    def sp(sp, b, p, parts=()):
        pass
    pool = act = sp


def packed_attention(nc, s, name, HL, scale, load, prep, tail, side=NoSide, ahead=()):
    J = 4 * HL
    W = P * HL
    PER = 512 // W
    Q, KB, VE = s.Q, s.KB, s.VE
    sem = s.sem
    q_packed = sem(name + "_q_packed")
    kb_ready = sem(name + "_kb_ready")
    s_ready = sem(name + "_s_ready")
    s_taken = sem(name + "_s_taken")
    max_split = sem(name + "_max_split")
    max_turned = sem(name + "_max_turned")
    max_rows = sem(name + "_max_rows")
    t_ready = sem(name + "_t_ready")
    exp_done = sem(name + "_exp_done")
    den_done = sem(name + "_den_done")
    pv_done = sem(name + "_pv_done")
    rden_done = sem(name + "_rden_done")
    msg_done = sem(name + "_msg_done")
    hi_done = sem(name + "_hi_done")
    ahead_in = sem(name + "_ahead_in")

    def s_tile(j):
        return j * PER // 4, j * PER % 4

    def pe_scores(pe, b, p, j):
        g, q0 = s_tile(j)
        if j == 0:
            pe.wait_ge(q_packed, (b + 1) * 192)
            pe.wait_ge(kb_ready, b + 1)
        if j >= 2:
            pe.wait_ge(s_taken, b * J + j - 1)
        for r in range(PER):
            last = nc.tensor.matmul(s.ps[:, j % 2, r * W:(r + 1) * W], Q[0:96, p, g, (q0 + r) * P:(q0 + r + 1) * P],
                                    KB[0:96, p, g, 0:W], start=True, stop=True)
        last.then_inc(s_ready, 1)

    def dve_max(dve, b, p, j):
        g, q0 = s_tile(j)
        dve.wait_ge(s_ready, b * J + j + 1)
        if j == 0:
            dve.wait_ge(max_split, b)
        nc.vector.tensor_reduce(s.mx[:, q0:q0 + PER, g, 0:HL],
                                s.ps[:, j % 2, :].rearrange("p (q h k) -> p q h k", q=PER, h=HL), AX.X, ALU.max
                                ).then_inc(s_taken, 1)
        if j == J - 1:
            dve.wait_ge(s_taken, (b + 1) * J)
            dve.wait_ge(max_turned, b)
            if has_before(b, 1):
                dve.wait_ge(t_ready, b * J)
            nc.vector.tensor_copy(s.m8[:, :, :, 0, 0:HL], s.mx[:, :, :, 0:HL]).then_inc(hi_done, 1)
            dve.wait_ge(hi_done, b + 1)
            nc.vector.tensor_tensor(s.m8[:, :, :, 1, 0:HL], s.mx[:, :, :, 0:HL], s.m8[:, :, :, 0, 0:HL],
                                    ALU.subtract).then_inc(max_split, 1)

    def pe_max_turn(pe, b):
        pe.wait_ge(max_split, b + 1)
        if symbolic(b) or b:
            if tail.late:
                pe.wait_ge(s.qlo_done, b + 2 if symbolic(b) else min(b + 2, NB))
            else:
                pe.wait_ge(s.v_done, b + 2 if symbolic(b) else min(b + 2, NB))
            pe.wait_ge(max_rows, b)
        else:
            pe.wait_ge(s.qlo_done, 2)
        for q in range(4):
            last = nc.tensor.matmul(s.ps[96:128, s.A, q * P:(q + 1) * P],
                                    s.m8[:, q, :, :, :].rearrange("p g t h -> p (g t h)"),
                                    s.ident_bf[:, :], start=True, stop=True)
        last.then_inc(max_turned, 1)

    def act_max_rows(act, b, p):
        act.wait_ge(max_turned, b + 1)
        nc.scalar.activation(Q[96:128, p, :, :], s.ps[96:128, s.A, :].unsqueeze(1).broadcast_to([32, 4, 512]), ACT.Copy
                             ).then_inc(max_rows, 1)

    def pe_turned(pe, b, p, h, g):
        j = 4 * h + g
        if j == 0:
            pe.wait_ge(max_rows, b + 1)
        if j >= 2:
            pe.wait_ge(exp_done, b * J + j - 1)
        nc.tensor.matmul(s.ps[:, 2 + j % 2, :], KB[:, p, g, h * P:(h + 1) * P], Q[:, p, g, :],
                         start=True, stop=True).then_inc(t_ready, 1)

    def act_exp(act, b, h, g):
        j = 4 * h + g
        act.wait_ge(t_ready, b * J + j + 1)
        if h >= 2 and g == 0:
            act.wait_ge(pv_done, b * HL + h - 1)
        nc.scalar.activation(s.PT[:, j % 8, :], s.ps[:, 2 + j % 2, :], ACT.Exp, scale=scale).then_inc(exp_done, 1)

    def pe_values(pe, b, p, h):
        pe.wait_ge(exp_done, b * J + 4 * h + 4)
        if h == 0:
            pe.wait_ge(msg_done, 2 * b)
            pe.wait_ge(tail.written, b)
        for g in range(4):
            w = s.PT[:, (4 * h + g) % 8, :]
            last = nc.tensor.matmul(s.ps[32 * g:32 * g + 32, 5, :], s.ones_blk[HL][:, h, :], w, start=(h == 0), stop=(h == HL - 1))
        last.then_inc(den_done, 1)
        for g in range(4):
            w = s.PT[:, (4 * h + g) % 8, :]
            last = nc.tensor.matmul(s.ps[32 * g:32 * g + 32, 4, :], VE[:, p, g, h, :], w, start=(h == 0), stop=(h == HL - 1))
        last.then_inc(pv_done, 1)

    def dve_normalise(dve, b):
        for half in range(2):
            part = slice(256 * half, 256 * half + 256)
            if half == 0:
                dve.wait_ge(den_done, (b + 1) * HL)
            nc.vector.reciprocal(s.rden[:, part], s.ps[:, 5, part]).then_inc(rden_done, 1)
            dve.wait_ge(rden_done, 2 * b + half + 1)
            if half == 0:
                dve.wait_ge(pv_done, (b + 1) * HL)
                tail.wait_msg_free(dve, b)
            nc.vector.tensor_tensor(s.msg[:, part], s.ps[:, 4, part], s.rden[:, part], ALU.mult).then_inc(msg_done, 1)

    s.q_packed, s.kb_ready, s.msg_done, s.max_rows, s.pv_done, s.t_ready, s.hi_done = q_packed, kb_ready, msg_done, max_rows, pv_done, t_ready, hi_done
    s.J = J

    with nc.Block() as block:
        @block.sync
        def _(sp):
            load(sp, 0, 0)
            load(sp, 1, 1)
            prep.sp(sp, 0, 0)
            prep.sp(sp, 1, 1)
            side.sp(sp, 0, 0)
            for to, of in ahead:
                sp.dma_start(to, of).then_inc(ahead_in, 16)

            def slot(b, p):
                if has_after(b, 2):
                    load(sp, b + 2, p)
                if has_after(b, 1):
                    side.sp(sp, b + 1, 1 - p)
                if has_after(b, 2):
                    prep.sp(sp, b + 2, p)
            slots(sp, slot)
            sp.wait_ge(ahead_in, 16 * len(ahead))

        @block.gpsimd
        def _(pool):
            def slot(b, p):
                side.pool(pool, b, p)
                if has_after(b, 2):
                    prep.pool(pool, b + 2, p)
                if has_before(b, 2):
                    s.front.pool_rstd(pool, b - 2, p)
            prep.pool(pool, 0, 0)
            prep.pool(pool, 1, 1)
            slots(pool, slot)
            s.front.pool_rstd(pool, NB - 2, 0)
            s.front.pool_rstd(pool, NB - 1, 1)

        @block.tensor
        def _(pe):
            prep.pe_first(pe, 0, 0)
            prep.pe_queries(pe, 0, 0)
            prep.pe_keys(pe, 0, 0)
            prep.pe_first(pe, 1, 1)
            prep.pe_queries(pe, 1, 1)
            for j in range(J):
                pe_scores(pe, 0, 0, j)
            pe_max_turn(pe, 0)
            prep.pe_keys(pe, 1, 1)

            def slot(b, p):
                for h in range(HL):
                    if h == HL // 2 and has_after(b, 2) and not tail.late:
                        prep.pe_keys(pe, b + 2, p)
                    for g in range(4):
                        pe_turned(pe, b, p, h, g)
                        if has_after(b, 1):
                            pe_scores(pe, b + 1, 1 - p, 4 * h + g)
                        if h == HL // 2 - 1 and has_after(b, 2):
                            if g == 0:
                                prep.pe_first(pe, b + 2, p)
                            elif g == 1:
                                prep.pe_queries(pe, b + 2, p)
                    if h:
                        pe_values(pe, b, p, h - 1)
                pe_values(pe, b, p, HL - 1)
                if has_after(b, 1):
                    pe_max_turn(pe, b + 1)
                if tail.late and has_after(b, 2):
                    prep.pe_keys(pe, b + 2, p)
                tail.pe_early(pe, b, p)
                tail.pe(pe, b, p)

            slots(pe, slot)

        @block.scalar
        def _(act):
            prep.act_context(act, 0, 0)
            prep.act_queries(act, 0, 0)
            prep.act_context(act, 1, 1)
            prep.act_queries(act, 1, 1)
            act_max_rows(act, 0, 0)

            def slot(b, p):
                for h in range(HL):
                    for g in range(4):
                        act_exp(act, b, h, g)
                        if h == HL // 2 - 1 and has_after(b, 2):
                            if g == 0:
                                prep.act_context(act, b + 2, p)
                            elif g == 1:
                                prep.act_queries(act, b + 2, p)
                if has_after(b, 1):
                    act_max_rows(act, b + 1, 1 - p)
                side.act(act, b, p, (0, 1))
                tail.act(act, b, p)
                side.act(act, b, p, (2,))

            slots(act, slot)

        @block.vector
        def _(dve):
            fe = s.front

            def keys(b, p):
                prep.dve_keys(dve, b, p)
                prep.dve_split_keys(dve, b, p)
                prep.dve_values(dve, b, p)

            if tail.late:
                prep.dve_x(dve, 0, 0)
            prep.dve_queries(dve, 0, 0)
            keys(0, 0)
            if tail.late:
                prep.dve_x(dve, 1, 1)
            prep.dve_queries(dve, 1, 1)
            for j in range(J):
                dve_max(dve, 0, 0, j)
            keys(1, 1)

            def moments(b, p, j):
                if j == 0:
                    fe.late_stats(b, p)
                elif j == 1 and has_before(b, 1):
                    fe.late_before_write(dve, b)
                    tail.add(dve, b - 1)
                elif j == 2:
                    fe.late_after_write(b, p)

            def slot(b, p):
                fe.late_waits(dve, b, tail.written)
                if tail.late:
                    if has_after(b, 2):
                        prep.dve_x(dve, b + 2, p)
                    for j in range(3):
                        moments(b, p, j)
                for j in range(J):
                    if has_after(b, 2):
                        if j == J // 2 - 1:
                            prep.dve_queries(dve, b + 2, p)
                        if not tail.late and J // 2 <= j < J // 2 + 3:
                            (prep.dve_keys, prep.dve_split_keys, prep.dve_values)[j - J // 2](dve, b + 2, p)
                    if has_after(b, 1):
                        dve_max(dve, b + 1, 1 - p, j)
                    if j in (2, 4, 6) and not tail.late:
                        moments(b, p, j // 2 - 1)
                dve_normalise(dve, b)
                if tail.late and has_after(b, 2):
                    keys(b + 2, p)

            slots(dve, slot)
            tail.add(dve, NB - 1)
            fe.late_last_moments(dve, tail.written)
    s.front.mbase += NB


def linked(engine, semaphore):
    count = [0]

    def link(instruction):
        count[0] += 1
        instruction.then_inc(semaphore, 1)
        engine.wait_ge(semaphore, count[0])
    return link


def setup(nc, s, t):
    x_in = [s.sem(f"x_in{b}") for b in range(NB)]
    w_in = s.sem("l0_w_in")
    fold_ready, fold_taken = s.sem("l0_fold_ready"), s.sem("l0_fold_taken")
    chain, bn_chain, bn_rstd, bn_eps = (s.sem(n) for n in ("setup_chain", "bn_chain", "bn_rstd", "bn_eps"))
    fe = s.front
    loads = [(s.ident, t["ident"]), (s.wq0, t["wq0"]), (s.wk0, t["wk0"]), (s.wk0_rep, t["wk0_rep"]),
             (s.proj, t["proj_k"].rearrange("(c p) k -> p c k", p=P)), (s.wm0, t["wm0"]), (s.w1m0, t["w1m0"]),
             (s.w1x0, t["w1x0"]), (s.w2_0, t["w2_0"]), (s.cols0, t["cols0"]), (s.bk0_row, t["bk0_row"].broadcast_to([P, P])),
             (s.ones_blk[4], t["ones4"]), (s.ones_blk[2], t["ones2"]), (s.mask4, t["mask4"]), (s.mask2, t["mask2"]),
             (s.neg[96:128], t["neg4"])]
    with nc.Block() as block:
        @block.sync
        def _(sp):
            for b in range(NB):
                sp.dma_start(s.X[:, b, :], t["x"][b]).then_inc(x_in[b], 16)

        @block.scalar
        def _(act):
            for to, of in loads:
                act.dma_start(to, of).then_inc(w_in, 16)

        @block.gpsimd
        def _(pool):
            nc.gpsimd.memset(s.ones[:, :], 1.0).then_inc(s.ones_ready, 1)
            nc.gpsimd.memset(s.eps[:, :], LN_EPS).then_inc(s.ones_ready, 1)
            nc.gpsimd.memset(s.minus_half[:, :], -0.5).then_inc(s.ones_ready, 1)
            nc.gpsimd.memset(s.VE[:, :, :, :, :], 0.0).then_inc(s.ones_ready, 1)
            pool.wait_ge(s.ones_ready, CONSTANTS)
            pool.wait_ge(fe.moments, NB)
            nc.gpsimd.tensor_scalar(s.var_eps[:, :], s.mv[:, :, 1], LN_EPS, None, ALU.add).then_inc(fe.eps_added, NB)
            pool.wait_ge(fe.eps_added, NB)
            nc.gpsimd.tensor_tensor(s.rstd[:, :, 0], s.var_eps[:, :], s.minus_half[:, :], ALU.pow).then_inc(fe.rstd, NB)
            pool.wait_ge(w_in, 16 * len(loads))
            nc.gpsimd.tensor_scalar(s.bn[:, 12:14], s.cols0[:, 14:16], BN_EPS, None, ALU.add).then_inc(bn_eps, 1)
            pool.wait_ge(bn_eps, 1)
            nc.gpsimd.tensor_tensor(s.bn[:, 0:2], s.bn[:, 12:14], s.minus_half[:, 0:2], ALU.pow).then_inc(bn_rstd, 1)

        @block.tensor
        def _(pe):
            pe.wait_ge(w_in, 16 * len(loads))
            pe.wait_ge(s.ones_ready, CONSTANTS)
            for c in range(DC):
                nc.tensor.matmul(s.ps[:, 0, 0:1], s.proj[:, c, :], s.ones[:, 0:1], start=(c == 0), stop=(c == DC - 1))
            for c in range(DC):
                nc.tensor.matmul(s.ps[:, 1, 0:P], s.ones[:, :], s.proj[:, c, :], start=(c == 0), stop=(c == DC - 1))
            nc.tensor.matmul(s.ps[:, 2, 0:256], s.wm0, s.w1m0, start=True, stop=True)
            for h in range(2):
                last = nc.tensor.matmul(s.ps[:, 3, h:h + 1], s.w1m0[:, h * P:(h + 1) * P], s.cols0[:, 6:7], start=(h == 0), stop=(h == 1), skip_group_check=True)
            last.then_inc(fold_ready, 1)

        @block.vector
        def _(dve):
            link = linked(dve, bn_chain)
            for b in range(NB):
                dve.wait_ge(x_in[b], 16)
                nc.vector.bn_stats(s.stats[:, b, :], s.X[:, b, :]).then_inc(fe.stats, 1)
            for b in range(NB):
                dve.wait_ge(fe.stats, b + 1)
                nc.vector.bn_aggr(s.mv[:, b, :], s.stats[:, b, :]).then_inc(fe.moments, 1)
            dve.wait_ge(fe.rstd, NB)
            with dve.Fori(0, NB // 2) as i:
                for b in (2 * i, 2 * i + 1):
                    nc.vector.tensor_scalar(s.XN[:, b, :], s.X[:, b, :], s.mv[:, b, 0:1], s.rstd[:, b, :], ALU.subtract, ALU.mult).then_inc(chain, 1)
            dve.wait_ge(w_in, 16 * len(loads))
            nc.vector.tensor_copy(s.ident_bf[:, :], s.ident).then_inc(fold_taken, 1)
            for p in range(2):
                nc.vector.tensor_copy(s.KB[96:128, p, :, :], s.neg[96:128, :, :]).then_inc(fold_taken, 1)
            dve.wait_ge(fold_ready, 1)
            nc.vector.tensor_copy(s.colsum[:, :], s.ps[:, 0, 0:1]).then_inc(fold_taken, 1)
            nc.vector.tensor_copy(s.colsum_row[:, :], s.ps[:, 1, 0:P]).then_inc(fold_taken, 1)
            nc.vector.tensor_copy(s.weff[:, :], s.ps[:, 2, 0:256]).then_inc(fold_taken, 1)
            c = s.cols0
            dve.wait_ge(bn_rstd, 1)
            link(nc.vector.tensor_tensor(s.bn[:, 2:4], s.bn[:, 0:2], c[:, 8:10], ALU.mult))
            link(nc.vector.tensor_tensor(s.bn[:, 4:6], c[:, 16:18], s.ps[:, 3, 0:2], ALU.add))
            link(nc.vector.tensor_tensor(s.bn[:, 6:8], s.bn[:, 4:6], c[:, 12:14], ALU.subtract))
            link(nc.vector.tensor_tensor(s.bn[:, 8:10], s.bn[:, 6:8], s.bn[:, 2:4], ALU.mult))
            link(nc.vector.tensor_tensor(s.bn[:, 10:12], s.bn[:, 8:10], c[:, 10:12], ALU.add))
    fe.mbase += NB


def linear_attention_of_channels(nc, s, t):
    sem = s.sem
    ct_in, c_ready, c_taken = (sem("l0_ct_in0"), sem("l0_ct_in1")), sem("l0_c_ready"), sem("l0_c_taken")
    q_ready, qhi_done, qlo_done = sem("l0_q_ready"), sem("l0_qhi_done"), sem("l0_qlo_done")
    kr_ready, v_ready, kf_done, kh_done, kx_done, v_done = (sem("l0_" + n) for n in (
        "kr_ready", "v_ready", "kf_done", "kh_done", "kx_done", "v_done"))
    h_ready, relu_done, o_ready, res_done = sem("l0_h_ready"), sem("l0_relu_done"), sem("l0_o_ready"), sem("l0_res_done")
    A, B = s.A, s.B
    ps = s.ps
    fe = s.front

    def load(sp, b, p):
        if has_before(b, 2):
            sp.wait_ge(c_ready, b - 1)
        sp.dma_start(s.ctxT_s[:, p, :, :], t["ctxT"][b].rearrange("(c p) k -> p c k", p=P)).then_inc(ct_in[p], 16)

    class prep:
        @staticmethod
        def pe_first(pe, b, p):
            pe.wait_ge(ct_in[p], 8 * (b - p) + 16)
            if has_before(b, 1):
                pe.wait_ge(kf_done, b)
            for c in range(DC):
                last = nc.tensor.matmul(ps[:, B, 0:P], s.ctxT_s[:, p, c, :], s.proj[:, c, :], start=(c == 0), stop=(c == DC - 1))
            last.then_inc(c_ready, 1)

        @staticmethod
        def pe_queries(pe, b, p):
            if has_before(b, 2):
                pe.wait_ge(s.max_rows, b - 1)
            if has_before(b, 1):
                pe.wait_ge(v_done, b)
            nc.tensor.matmul(ps[:, A, :], s.wq0, s.XN[:, b, :], start=True, stop=True).then_inc(q_ready, 1)

        @staticmethod
        def pe_keys(pe, b, p):
            pe.wait_ge(c_taken, b + 1)
            for g in range(4):
                last = nc.tensor.matmul(ps[0:96, B, g * P:(g + 1) * P], s.wk0_rep[:, g, :], s.C[:, :], start=(g == 0), stop=(g == 3), skip_group_check=True)
            last.then_inc(kr_ready, 1)
            pe.wait_ge(qlo_done, b + 1)
            if has_before(b, 1) and not has_before(b, 2):
                pe.wait_ge(s.max_rows, 1)
            nc.tensor.matmul(ps[:, A, 0:P], s.C[:, :], s.wk0, start=True, stop=True).then_inc(v_ready, 1)

        @staticmethod
        def act_context(act, b, p):
            act.wait_ge(c_ready, b + 1)
            if has_before(b, 1):
                act.wait_ge(v_ready, b)
            nc.scalar.activation(s.C[:, :], ps[:, B, 0:P], ACT.Copy).then_inc(c_taken, 1)

        @staticmethod
        def act_queries(act, b, p):
            act.wait_ge(q_ready, b + 1)
            if has_before(b, 1):
                act.wait_ge(s.q_packed, 192 * b)
            nc.scalar.activation(s.QH[:, :], ps[:, A, :], ACT.Identity, bias=s.cols0[:, 0:1]).then_inc(qhi_done, 1)

        @staticmethod
        def dve_queries(dve, b, p):
            dve.wait_ge(qhi_done, b + 1)
            nc.vector.scalar_tensor_tensor(s.QL[:, :], ps[:, A, :], s.cols0[:, 0:1], s.QH[:, :].bitcast(F32), ALU.add, ALU.subtract).then_inc(qlo_done, 1)

        @staticmethod
        def dve_keys(dve, b, p):
            dve.wait_ge(kr_ready, b + 1)
            for g in range(4):
                last = nc.vector.scalar_tensor_tensor(s.KF[0:96, g, :], s.colsum_row[0:96, :], s.cols0[0:96, 1 + g:2 + g],
                                                      ps[0:96, B, g * P:(g + 1) * P], ALU.mult, ALU.add)
            last.then_inc(kf_done, 1)

        @staticmethod
        def dve_split_keys(dve, b, p):
            dve.wait_ge(kf_done, b + 1)
            if has_before(b, 1):
                dve.wait_ge(s.kb_ready, b)
            nc.vector.tensor_copy(s.KH[0:96, :, :], s.KF[0:96, :, :]).then_inc(kh_done, 1)
            dve.wait_ge(kh_done, b + 1)
            nc.vector.tensor_tensor(s.KH[32:64, :, :], s.KF[32:64, :, :], s.KH[32:64, :, :], ALU.subtract).then_inc(kx_done, 1)

        @staticmethod
        def dve_values(dve, b, p):
            dve.wait_ge(v_ready, b + 1)
            nc.vector.scalar_tensor_tensor(s.VS[:, :], s.bk0_row, s.colsum[:, 0:1], ps[:, A, 0:P], ALU.mult, ALU.add).then_inc(v_done, 1)

        @staticmethod
        def pool(pool, b, p):
            spread(nc, s, pool, b, p, 4, s.mask4, kx_done, v_done)

        @staticmethod
        def sp(sp, b, p):
            pack_queries(nc, s, sp, b, p, qlo_done)

    class tail:
        written, late = res_done, False

        @staticmethod
        def wait_msg_free(dve, b):
            dve.wait_ge(h_ready, 2 * b)

        @staticmethod
        def pe_early(pe, b, p):
            for h in range(2):
                nc.tensor.matmul(ps[:, 2 + h, :], s.w1x0[:, h * P:(h + 1) * P], s.XN[:, b, :], start=True, stop=False)

        @staticmethod
        def pe(pe, b, p):
            for half in range(2):
                pe.wait_ge(s.msg_done, 2 * b + half + 1)
                part = slice(256 * half, 256 * half + 256)
                for h in range(2):
                    product = nc.tensor.matmul(ps[:, 2 + h, part], s.weff[:, h * P:(h + 1) * P], s.msg[:, part], start=False, stop=(half == 1))
                    if half:
                        product.then_inc(h_ready, 1)
            for h in range(2):
                pe.wait_ge(relu_done, 2 * b + 1 + h)
                last = nc.tensor.matmul(ps[:, 5, :], s.w2_0[:, h, :], s.H[:, h, :], start=(h == 0), stop=(h == 1))
            last.then_inc(o_ready, 1)

        @staticmethod
        def act(act, b, p):
            act.wait_ge(o_ready, b)
            for h in range(2):
                act.wait_ge(h_ready, 2 * b + h + 1)
                nc.scalar.activation(s.H[:, h, :], ps[:, 2 + h, :], ACT.Relu, bias=s.bn[:, 10 + h:11 + h], scale=s.bn[:, 2 + h:3 + h]).then_inc(relu_done, 1)

        @staticmethod
        def add(dve, b):
            dve.wait_ge(o_ready, b + 1)
            nc.vector.scalar_tensor_tensor(s.X[:, b, :], ps[:, 5, :], s.cols0[:, 7:8], s.X[:, b, :], ALU.add, ALU.add).then_inc(res_done, 1)

    s.v_done, s.qlo_done = v_done, qlo_done
    packed_attention(nc, s, "l0", 4, 8 ** -0.5, load, prep, tail, distances(nc, s, t))


PAIRS = 7


def distances(nc, s, t):
    w_in = [s.sem(f"bw_in{p}") for p in range(2)]
    diff_done, abs_done = s.sem("bw_diff"), s.sem("bw_abs")

    class side:
        @staticmethod
        def sp(sp, b, p):
            if not has_after(b, 1):
                return
            if has_before(b, 2):
                sp.wait_ge(abs_done, 3 * (b - 1))
            sp.dma_start(s.SW[:, p, :, :, :], t["w"][b]).then_inc(w_in[p], 16)
            sp.dma_start(s.SB[:, p, :, :, :], t["base"][b]).then_inc(w_in[p], 16)

        @staticmethod
        def pool(pool, b, p):
            if has_after(b, 1):
                pool.wait_ge(w_in[p], 16 * (b - p) + 32)
                nc.gpsimd.tensor_tensor(s.SW[:, p, :, :, :], s.SW[:, p, :, :, :], s.SB[:, p, :, :, :], ALU.subtract).then_inc(diff_done, 1)

        @staticmethod
        def act(act, b, p, parts):
            if has_after(b, 1):
                act.wait_ge(diff_done, b + 1)
                for m in parts:
                    if m or not isinstance(b, int) or b:
                        act.wait_ge(abs_done, 3 * b + m)
                    nc.scalar.activation(s.wscr[:, :, :], s.SW[:, p, :, m, :], ACT.Abs, accum_out=s.wabs[:, b, m:m + 1]).then_inc(abs_done, 1)
    return side


def spread(nc, s, pool, b, p, HL, mask, kx_done, v_done):
    W = 32 // HL
    pool.wait_ge(kx_done, b + 1)
    if has_before(b, 2):
        pool.wait_ge(s.t_ready, (b - 1) * s.J)
    for g in range(4):
        if g == 3:
            pool.wait_ge(v_done, b + 1)
            if has_before(b, 2):
                pool.wait_ge(s.pv_done, (b - 1) * HL)
        nc.gpsimd.tensor_tensor(s.KB[0:96, p, g, 0:HL * P].rearrange("p (h k) -> p h k", h=HL),
                                s.KH[0:96, g, :].bitcast(F32).unsqueeze(1).broadcast_to([96, HL, P]),
                                mask[0:96].unsqueeze(2).broadcast_to([96, HL, P]), ALU.mult)
    for h in range(HL):
        last = nc.gpsimd.tensor_copy(s.VE[:, p, :, h, h * W:(h + 1) * W], s.VS[:, :].rearrange("p (g h d) -> p g h d", g=4, h=HL)[:, :, h, :])
    last.then_inc(s.kb_ready, 1)


def pack_queries(nc, s, sp, b, p, qlo_done):
    if has_before(b, 2):
        sp.wait_ge(s.hi_done, b)
    else:
        sp.wait_ge(qlo_done, b + 1)
    for g in range(4):
        for quadrant, part in enumerate((s.QH, s.QH, s.QL)):
            sp.dma_start(s.Q[32 * quadrant:32 * quadrant + 32, p, g, :].bitcast(F32),
                         part[32 * g:32 * g + 32, :].bitcast(F32)).then_inc(s.q_packed, 16)


class Front:
    def __init__(self, nc, s):
        self.nc, self.s, self.base, self.mbase = nc, s, 0, 0
        sem = s.sem
        self.stats, self.moments, self.eps_added, self.rstd = (sem("fe_" + n) for n in ("stats", "moments", "eps_added", "rstd"))
        self.xn_ready = sem("fe_xn_ready")
        self.turned = sem("fe_turned")
        self.ready = sem("fe_xnT_ready")

    def before_write(self, dve, b, written):
        n = self.mbase + b
        if has_before(b, 1):
            dve.wait_ge(written, b)
            dve.wait_ge(self.stats, n - 1)
        dve.wait_ge(self.moments, n - 2)
        dve.wait_ge(self.rstd, n - 3)

    def after_write(self, b, p):
        if has_before(b, 1):
            self.dve_stats(b - 1, 1 - p)
        if has_before(b, 2):
            self.dve_moments(p)

    def dve_stats(self, b, p):
        self.nc.vector.bn_stats(self.s.mstats[:, p, :], self.s.X[:, b, :]).then_inc(self.stats, 1)

    def dve_moments(self, p):
        self.nc.vector.bn_aggr(self.s.mmv[:, p, :], self.s.mstats[:, p, :]).then_inc(self.moments, 1)

    def dve_last_moments(self, dve, written):
        n = self.mbase + NB
        dve.wait_ge(written, NB)
        dve.wait_ge(self.moments, n - 2)
        self.dve_stats(NB - 1, 1)
        dve.wait_ge(self.stats, n - 1)
        dve.wait_ge(self.rstd, n - 3)
        self.dve_moments(0)
        dve.wait_ge(self.stats, n)
        dve.wait_ge(self.rstd, n - 2)
        self.dve_moments(1)

    def late_waits(self, dve, b, written):
        if has_before(b, 2):
            dve.wait_ge(written, b - 1)
            dve.wait_ge(self.moments, self.mbase + b - 3)

    def late_stats(self, b, p):
        if has_before(b, 2):
            self.dve_stats(b - 2, p)

    def late_before_write(self, dve, b):
        if has_before(b, 2):
            dve.wait_ge(self.stats, self.mbase + b - 1)
            dve.wait_ge(self.rstd, self.mbase + b - 3)

    def late_after_write(self, b, p):
        if has_before(b, 2):
            self.dve_moments(p)

    def late_last_moments(self, dve, written):
        for b in (NB, NB + 1):
            self.late_waits(dve, b, written)
            self.late_stats(b, b % 2)
            self.late_before_write(dve, b)
            self.late_after_write(b, b % 2)

    def pool_rstd(self, pool, b, p):
        s, n, g = self.s, self.mbase + b, self.nc.gpsimd
        pool.wait_ge(self.moments, n + 1)
        g.tensor_tensor(s.var_eps[:, p:p + 1], s.mmv[:, p, 1:2], s.eps[:, 0:1], ALU.add).then_inc(self.eps_added, 1)
        g.tensor_copy(s.mean[:, b, :], s.mmv[:, p, 0:1])
        pool.wait_ge(self.eps_added, n + 1)
        g.tensor_tensor(s.rstd[:, b, :], s.var_eps[:, p:p + 1], s.minus_half[:, 0:1], ALU.pow).then_inc(self.rstd, 1)

    def dve_normalise(self, dve, b, p):
        s, n = self.s, self.base + b
        if has_before(b, 2):
            dve.wait_ge(self.turned, n - 1)
        self.nc.vector.tensor_scalar(s.xn[:, p, :], s.X[:, b, :], s.mean[:, b, :], s.rstd[:, b, :], ALU.subtract, ALU.mult
                                     ).then_inc(self.xn_ready, 1)

    def pe_turn(self, pe, b, p, bank=0):
        s, n = self.s, self.base + b
        pe.wait_ge(self.xn_ready, n + 1)
        pe.wait_ge(self.ready, n)
        for c in range(DC):
            last = self.nc.tensor.transpose(s.ps[:, bank, c * P:(c + 1) * P], s.xn[:, p, c * P:(c + 1) * P], s.ident)
        last.then_inc(self.turned, 1)


def binary_gated_ffn(nc, s, t):
    sem = s.sem
    fe = s.front
    I = 2 * PAIRS
    names = ("g_ready", "u_ready", "silu_done", "h_done", "o_ready", "out_ready", "res_done", "xlo_done", "sums_done", "total_done",
             "coeff_done", "diff_done", "sign_done", "wp_done", "whi_done", "wlo_done", "hhi_done", "hlo_done")
    (g_ready, u_ready, silu_done, h_done, o_ready, out_ready, res_done, xlo_done, sums_done, total_done,
     coeff_done, diff_done, sign_done, wp_done, whi_done, wlo_done, hhi_done, hlo_done) = (sem("ff_" + n) for n in names)
    w_in = [sem(f"ff_w_in{p}") for p in range(2)]
    ahead_in = sem("ff_ahead_in")
    ps = s.ps

    def part(tile, first, p):
        return tile[:, p, 0:2, :] if first == 0 else tile[:, p, 0, :]

    def step(first, j):
        return j if first == 0 else I + j

    def sp_load(sp, first, i, p):
        for to, of in ((s.RW, t["w"]), (s.RB, t["base"])):
            sp.dma_start(part(to, first, p), of[i][:, p, 0:2, :] if first == 0 else of[i][:, p, 2, :]).then_inc(w_in[p], 16)

    def pool_diff(pool, first, j, p):
        pool.wait_ge(w_in[p], 16 * (step(first, j) - p) + 32)
        nc.gpsimd.tensor_tensor(part(s.RW, first, p), part(s.RW, first, p), part(s.RB, first, p), ALU.subtract).then_inc(diff_done, 1)

    def act_weights(act, first, j, p):
        n = step(first, j)
        act.wait_ge(diff_done, n + 1)
        nc.scalar.activation(part(s.SG, first, p), part(s.RW, first, p), ACT.Sign).then_inc(sign_done, 1)
        act.wait_ge(wp_done, n + 1)
        if first and has_before(j, 2):
            act.wait_ge(o_ready, j - 1)
        elif first or has_before(j, 2):
            act.wait_ge(u_ready, n - 1)
        nc.scalar.activation(part(s.WH, first, p), part(s.RB, first, p), ACT.Copy).then_inc(whi_done, 1)

    def dve_weights(dve, first, j, p):
        n = step(first, j)
        dve.wait_ge(sign_done, n + 1)
        for m in range(2 if first == 0 else 1):
            last = nc.vector.scalar_tensor_tensor(s.RB[:, p, m, :], s.SG[:, p, m, :], s.coeff[:, first + m:first + m + 1], s.RB[:, p, m, :], ALU.mult, ALU.add)
        last.then_inc(wp_done, 1)
        dve.wait_ge(whi_done, n + 1)
        nc.vector.tensor_tensor(part(s.WLO, first, p), part(s.RB, first, p), part(s.WH, first, p).bitcast(F32), ALU.subtract).then_inc(wlo_done, 1)

    def pe_gate_up(pe, j, p):
        pe.wait_ge(wlo_done, j + 1)
        if has_before(j, 2):
            pe.wait_ge(h_done, j - 1)
        for m, ready in enumerate((g_ready, u_ready)):
            for c in range(DC):
                for k, (w, x) in enumerate(((s.WH, s.XH), (s.WH, s.XLO), (s.WLO, s.XH))):
                    for h in range(2):
                        last = nc.tensor.matmul(ps[:, 4 * p + 2 * m + h, :], w[:, p, m, c * P:(c + 1) * P],
                                                x[:, c, 4 * h:4 * h + 4, :].rearrange("p b t -> p (b t)"),
                                                start=(c == 0 and k == 0), stop=(c == DC - 1 and k == 2))
            last.then_inc(ready, 1)

    def act_silu(act, j, p):
        act.wait_ge(g_ready, j + 1)
        nc.scalar.activation(s.SL[:, p, :, :], ps[:, 4 * p:4 * p + 2, :], ACT.Silu).then_inc(silu_done, 1)

    def dve_hidden(dve, j, p):
        dve.wait_ge(silu_done, j + 1)
        dve.wait_ge(u_ready, j + 1)
        nc.vector.tensor_tensor(s.HF[:, j, :, :], ps[:, 4 * p + 2:4 * p + 4, :], s.SL[:, p, :, :], ALU.mult).then_inc(h_done, 1)

    def act_split_hidden(act, j, p):
        act.wait_ge(h_done, j + 1)
        if has_before(j, 2):
            act.wait_ge(o_ready, j - 1)
        nc.scalar.activation(s.HH[:, p, :, :], s.HF[:, j, :, :], ACT.Copy).then_inc(hhi_done, 1)

    def dve_split_hidden(dve, j, p):
        dve.wait_ge(hhi_done, j + 1)
        nc.vector.tensor_tensor(s.HLO[:, p, :, :], s.HF[:, j, :, :], s.HH[:, p, :, :].bitcast(F32), ALU.subtract).then_inc(hlo_done, 1)

    def pe_down(pe, j, p):
        pe.wait_ge(wlo_done, I + j + 1)
        pe.wait_ge(hlo_done, j + 1)
        if not has_before(j, 1):
            pe.wait_ge(h_done, I)
        for q in range(NB):
            tokens = lambda tile: tile[:, p, :, :].rearrange("p h t -> p (h t)")[:, q * P:(q + 1) * P]
            for k, (h, w) in enumerate(((s.HH, s.WH), (s.HH, s.WLO), (s.HLO, s.WH))):
                last = nc.tensor.matmul(ps[:, q, :], tokens(h), w[:, p, 0, :], start=(not has_before(j, 1) and k == 0), stop=(not has_after(j, 1, I) and k == 2))
            if not has_after(j, 1, I):
                last.then_inc(out_ready, 1)
        if has_after(j, 1, I):
            last.then_inc(o_ready, 1)

    with nc.Block() as block:
        @block.gpsimd
        def _(pool):
            def diff(first):
                return lambda j, p: pool_diff(pool, first, j, p)
            for first in (0, 2):
                slots(pool, diff(first), I)
            for handle in s.retired:
                pool.sem_clear(handle)

        @block.sync
        def _(sp):
            for first in (0, 2):
                for p in range(2):
                    if first:
                        sp.wait_ge(wlo_done, I + p - 1)
                    sp_load(sp, first, 0, p)
                with sp.Fori(1, PAIRS) as i:
                    for p in range(2):
                        sp.wait_ge(wlo_done, step(first, 2 * i + p) - 1)
                        sp_load(sp, first, i, p)

        @block.tensor
        def _(pe):
            def turn(b, p):
                pe.wait_ge(fe.xn_ready, fe.base + b + 1)
                if has_before(b, 2):
                    pe.wait_ge(xlo_done, b - 1)
                for c in range(DC):
                    last = nc.tensor.transpose(ps[:, p, c * P:(c + 1) * P], s.xn[:, p, c * P:(c + 1) * P], s.ident)
                last.then_inc(fe.turned, 1)
            slots(pe, turn)
            pe.wait_ge(sums_done, 1)
            nc.tensor.matmul(ps[:, 7, 0:3], s.ones[:, :], s.wsum[:, 0:3], start=True, stop=True).then_inc(total_done, 1)
            pe.wait_ge(xlo_done, NB)
            slots(pe, lambda j, p: pe_gate_up(pe, j, p), I)
            slots(pe, lambda j, p: pe_down(pe, j, p), I)

        @block.scalar
        def _(act):
            def take(b, p):
                act.wait_ge(fe.turned, fe.base + b + 1)
                nc.scalar.activation(s.XH[:, :, b, :], ps[:, p, :].rearrange("p (c t) -> p c t", c=DC), ACT.Copy).then_inc(fe.ready, 1)
            slots(act, take)
            act_weights(act, 0, 0, 0)

            def gate(j, p):
                if has_after(j, 1, I):
                    act_weights(act, 0, j + 1, 1 - p)
                else:
                    act_weights(act, 2, 0, 0)
                act_silu(act, j, p)
            slots(act, gate, I)
            act_split_hidden(act, 0, 0)

            ahead = [[(s.wk1, t["wk1"]), (s.cols1[:, :], t["cols1"])],
                     [(s.wq1, t["wq1"]), (s.qw[:, :, :], t["qw"]), (s.lut[:, :, :], t["lut4"].rearrange("(c p) v -> p c v", p=P))]]

            def down(j, p):
                if has_after(j, 1, I):
                    act_weights(act, 2, j + 1, 1 - p)
                    act_split_hidden(act, j + 1, 1 - p)
                if not has_before(j, 2):
                    for to, of in ahead[j]:
                        act.dma_start(to, of).then_inc(ahead_in, 16)
            act.wait_ge(h_done, I)
            slots(act, down, I)
            act.wait_ge(ahead_in, 16 * 5)

        @block.vector
        def _(dve):
            nc.vector.tensor_reduce(s.wsum[:, 0:3], s.wabs[:, :, :].rearrange("p k m -> p m k"), AX.X, ALU.add).then_inc(sums_done, 1)

            def split(b, p):
                dve.wait_ge(fe.ready, fe.base + b + 1)
                nc.vector.tensor_tensor(s.XLO[:, :, b, :], ps[:, p, :].rearrange("p (c t) -> p c t", c=DC), s.XH[:, :, b, :].bitcast(F32), ALU.subtract).then_inc(xlo_done, 1)
                if has_after(b, 2):
                    fe.dve_normalise(dve, b + 2, p)
            for b in range(2):
                fe.dve_normalise(dve, b, b)
            slots(dve, split)
            dve.wait_ge(total_done, 1)
            nc.vector.tensor_scalar(s.coeff[:, 0:3], ps[:, 7, 0:3], 1.0 / (I * P * D), None, ALU.mult).then_inc(coeff_done, 1)
            dve.wait_ge(coeff_done, 1)
            dve_weights(dve, 0, 0, 0)

            def gate(j, p):
                if has_after(j, 1, I):
                    dve_weights(dve, 0, j + 1, 1 - p)
                else:
                    dve_weights(dve, 2, 0, 0)
                dve_hidden(dve, j, p)
            slots(dve, gate, I)
            dve_split_hidden(dve, 0, 0)

            def down(j, p):
                if has_after(j, 1, I):
                    dve_weights(dve, 2, j + 1, 1 - p)
                    dve_split_hidden(dve, j + 1, 1 - p)
            slots(dve, down, I)
            for b in range(NB):
                dve.wait_ge(out_ready, b + 1)
                nc.vector.tensor_tensor(s.X[:, b, :], ps[:, b, :], s.X[:, b, :], ALU.add).then_inc(res_done, 1)
    fe.base += NB


def moments_of_all(nc, s):
    fe = s.front
    n = fe.mbase
    fe.mbase += NB

    class part:
        @staticmethod
        def dve(dve):
            for b in range(NB):
                nc.vector.bn_stats(s.stats[:, b, :], s.X[:, b, :]).then_inc(fe.stats, 1)
            for b in range(NB):
                dve.wait_ge(fe.stats, n + b + 1)
                nc.vector.bn_aggr(s.mv[:, b, :], s.stats[:, b, :]).then_inc(fe.moments, 1)

        @staticmethod
        def pool(pool):
            pool.wait_ge(fe.moments, n + NB)
            nc.gpsimd.tensor_scalar(s.var_eps[:, :], s.mv[:, :, 1], LN_EPS, None, ALU.add).then_inc(fe.eps_added, NB)
            nc.gpsimd.tensor_copy(s.mean[:, :, 0], s.mv[:, :, 0])
            pool.wait_ge(fe.eps_added, n + NB)
            nc.gpsimd.tensor_tensor(s.rstd[:, :, 0], s.var_eps[:, :], s.minus_half[:, :], ALU.pow).then_inc(fe.rstd, NB)

        @staticmethod
        def pe(pe):
            pass
        act = pe
    return part


def side_by_side(nc, s, parts, first_load, loads):
    arrived = s.sem("weights_in")
    s.ctxT_in = s.sem("ctxT_in")
    with nc.Block() as block:
        @block.sync
        def _(sp):
            sp.dma_start(*first_load).then_inc(s.ctxT_in, 16)
            for to, of in loads:
                sp.dma_start(to, of).then_inc(arrived, 16)
            sp.wait_ge(arrived, 16 * len(loads))

        @block.tensor
        def _(pe):
            for part in parts:
                part.pe(pe)

        @block.scalar
        def _(act):
            for part in parts:
                part.act(act)

        @block.vector
        def _(dve):
            for part in parts:
                part.dve(dve)

        @block.gpsimd
        def _(pool):
            for part in parts:
                part.pool(pool)


def fold_text_attention(nc, s, t):
    sem = s.sem
    mt_ready, mt_taken, g_ready, g_taken, v_ready, v_taken, step = (sem("fa_" + n) for n in (
        "mt_ready", "mt_taken", "g_ready", "g_taken", "v_ready", "v_taken", "step"))
    WQ, WK, MT = s.wq1, s.wk1, s.mt1
    class part:
        @staticmethod
        def pe(pe):
            for y in range(DC):
                for c in range(DC):
                    last = nc.tensor.matmul(s.ps[:, y, :], WK[:, c, y * P:(y + 1) * P], WQ[:, c, :], start=(c == 0), stop=(c == DC - 1))
                last.then_inc(mt_ready, 1)
            for y in range(DC):
                for c in range(DC):
                    nc.tensor.matmul(s.ps[:, 7, y:y + 1], WK[:, c, y * P:(y + 1) * P], s.cols1[:, c:c + 1], start=(y == 0 and c == 0), stop=False, skip_group_check=True)
            for y in range(DC):
                for c in range(DC):
                    last = nc.tensor.matmul(s.ps[:, 7, 4 + y:5 + y], WQ[:, c, y * P:(y + 1) * P], s.cols1[:, 4 + c:5 + c], start=False, stop=(y == DC - 1 and c == DC - 1), skip_group_check=True)
            last.then_inc(v_ready, 1)
            pe.wait_ge(v_taken, 2)
            nc.tensor.matmul(s.ps[:, 7, 8:9], s.ones[:, :], s.bqk[:, 0:1], start=True, stop=True).then_inc(v_ready, 1)
            pe.wait_ge(mt_taken, DC)
            pe.wait_ge(s.ctxT_in, 16)
            for n in range(2 * DC):
                x, h = divmod(n, 2)
                if n >= 2:
                    pe.wait_ge(g_taken, n - 1)
                for c in range(DC):
                    last = nc.tensor.matmul(s.ps[:, 4 + n % 2, :], MT[:, c, x * P:(x + 1) * P], s.ctxT[:, c, 4 * h:4 * h + 4, :].rearrange("p b k -> p (b k)"), start=(c == 0), stop=(c == DC - 1))
                last.then_inc(g_ready, 1)
            pe.wait_ge(v_taken, 4)
            for h in range(2):
                pe.wait_ge(g_taken, 2 * DC - 1 + h)
                for c in range(DC):
                    last = nc.tensor.matmul(s.ps[:, 4 + h, :], s.vrep[:, c, :], s.ctxT[:, c, 4 * h:4 * h + 4, :].rearrange("p b k -> p (b k)"), start=(c == 0), stop=(c == DC - 1))
                last.then_inc(g_ready, 1)

        @staticmethod
        def act(act):
            for y in range(DC):
                act.wait_ge(mt_ready, y + 1)
                nc.scalar.activation(MT[:, y, :], s.ps[:, y, :], ACT.Copy).then_inc(mt_taken, 1)
            act.wait_ge(v_ready, 1)
            nc.scalar.activation(s.v1[:, :], s.ps[:, 7, 0:8], ACT.Copy).then_inc(v_taken, 1)
            act.wait_ge(v_ready, 2)
            nc.scalar.activation(s.bqk[:, 1:2], s.ps[:, 7, 8:9], ACT.Copy).then_inc(v_taken, 1)
            act.wait_ge(v_taken, 3)
            for c in range(DC):
                last = nc.scalar.activation(s.vrep[:, c, :], s.v1[:, c:c + 1].broadcast_to([P, P]), ACT.Copy)
            last.then_inc(v_taken, 1)
            for n in range(2 * DC):
                x, h = divmod(n, 2)
                act.wait_ge(g_ready, n + 1)
                nc.scalar.activation(s.G[:, x, 4 * h:4 * h + 4, :].rearrange("p b k -> p (b k)"), s.ps[:, 4 + n % 2, :], ACT.Identity, bias=s.v1[:, 4 + x:5 + x]).then_inc(g_taken, 1)
            for h in range(2):
                act.wait_ge(g_ready, 2 * DC + 1 + h)
                nc.scalar.activation(s.R[:, 4 * h:4 * h + 4, :].rearrange("p b k -> p (b k)"), s.ps[:, 4 + h, :], ACT.Identity, bias=s.bqk[:, 1:2]).then_inc(g_taken, 1)

        @staticmethod
        def dve(dve):
            nc.vector.tensor_tensor(s.bqk[:, 4:8], s.cols1[:, 0:4], s.cols1[:, 4:8], ALU.mult).then_inc(step, 1)
            dve.wait_ge(step, 1)
            nc.vector.tensor_reduce(s.bqk[:, 0:1], s.bqk[:, 4:8], AX.X, ALU.add).then_inc(v_taken, 1)

        @staticmethod
        def pool(pool):
            pass
    return part


def context_attention(nc, s, name, KT, R, scale):
    sem = s.sem
    fe = s.front
    s_ready, r_added, max_done, neg_done, e_done, et_ready, et_taken, den_done, o_ready, res_done = (sem(name + n) for n in (
        "_s_ready", "_r_added", "_max", "_neg", "_e", "_et_ready", "_et_taken", "_den", "_o_ready", "_res"))
    SC, OUT, ET = (1, 2), (4, 5), 3
    with nc.Block() as block:
        @block.gpsimd
        def _(pool):
            slots(pool, lambda b, p: fe.pool_rstd(pool, b, p))

        @block.tensor
        def _(pe):
            def turn_weights(b, p):
                pe.wait_ge(e_done, b + 1)
                pe.wait_ge(et_taken, b)
                nc.tensor.transpose(s.ps[:, ET, 0:P], s.E[:, p, :], s.ident).then_inc(et_ready, 1)

            def out(b, p):
                pe.wait_ge(et_taken, b + 1)
                if has_before(b, 2):
                    pe.wait_ge(res_done, b - 1)
                nc.tensor.matmul(s.ps[:, OUT[p], :], s.EWT[:, p, :], s.ctx[:, b, :], start=True, stop=True).then_inc(o_ready, 1)

            def slot(b, p):
                if has_before(b, 1):
                    turn_weights(b - 1, 1 - p)
                pe.wait_ge(fe.ready, fe.base + b + 1)
                if has_before(b, 2):
                    pe.wait_ge(e_done, b - 1)
                for c in range(DC):
                    last = nc.tensor.matmul(s.ps[:, SC[p], 0:P], s.xnT[:, p, c, :], KT[:, c, b, :], start=(c == 0), stop=(c == DC - 1))
                last.then_inc(s_ready, 1)
                if has_after(b, 2):
                    fe.pe_turn(pe, b + 2, p)
                if has_before(b, 1):
                    out(b - 1, 1 - p)
            fe.pe_turn(pe, 0, 0)
            fe.pe_turn(pe, 1, 1)
            slots(pe, slot)
            turn_weights(NB - 1, 1)
            out(NB - 1, 1)

        @block.scalar
        def _(act):
            def take_weights(b, p):
                act.wait_ge(et_ready, b + 1)
                if has_before(b, 2):
                    act.wait_ge(o_ready, b - 1)
                nc.scalar.activation(s.EWT[:, p, :], s.ps[:, ET, 0:P], ACT.Copy).then_inc(et_taken, 1)

            def take(b, p):
                act.wait_ge(fe.turned, fe.base + b + 1)
                if has_before(b, 2):
                    act.wait_ge(s_ready, b - 1)
                nc.scalar.activation(s.xnT[:, p, :, :].rearrange("p c t -> p (c t)"), s.ps[:, 0, :], ACT.Copy).then_inc(fe.ready, 1)

            def slot(b, p):
                if has_before(b, 1):
                    take_weights(b - 1, 1 - p)
                act.wait_ge(neg_done, b + 1)
                if has_before(b, 2):
                    act.wait_ge(et_ready, b - 1)
                    act.wait_ge(res_done, b - 1)
                source = s.SR[:, p, :] if R is not None else s.ps[:, SC[p], 0:P]
                nc.scalar.activation(s.E[:, p, :], source, ACT.Exp, bias=s.negm[:, p:p + 1], scale=scale, accum_out=s.den[:, p:p + 1]).then_inc(e_done, 1)
                if has_after(b, 2):
                    take(b + 2, p)
            take(0, 0)
            take(1, 1)
            slots(act, slot)
            take_weights(NB - 1, 1)

        @block.vector
        def _(dve):
            def add(b, p):
                dve.wait_ge(o_ready, b + 1)
                nc.vector.scalar_tensor_tensor(s.X[:, b, :], s.ps[:, OUT[p], :], s.rd[:, p:p + 1], s.X[:, b, :], ALU.mult, ALU.add).then_inc(res_done, 1)

            def invert(b, p):
                dve.wait_ge(e_done, b + 1)
                if has_before(b, 2):
                    dve.wait_ge(res_done, b - 1)
                nc.vector.reciprocal(s.rd[:, p:p + 1], s.den[:, p:p + 1]).then_inc(den_done, 1)
                dve.wait_ge(den_done, b + 1)

            def slot(b, p):
                if has_after(b, 2):
                    fe.dve_normalise(dve, b + 2, p)
                dve.wait_ge(s_ready, b + 1)
                if R is not None:
                    if has_before(b, 2):
                        dve.wait_ge(e_done, b - 1)
                    nc.vector.tensor_tensor(s.SR[:, p, :], s.ps[:, SC[p], 0:P], R[:, b, :], ALU.add).then_inc(r_added, 1)
                    dve.wait_ge(r_added, b + 1)
                source = s.SR[:, p, :] if R is not None else s.ps[:, SC[p], 0:P]
                if has_before(b, 1):
                    dve.wait_ge(neg_done, b)
                fe.late_waits(dve, b, res_done)
                nc.vector.tensor_reduce(s.smax[:, p:p + 1], source, AX.X, ALU.max).then_inc(max_done, 1)
                dve.wait_ge(max_done, b + 1)
                if has_before(b, 2):
                    dve.wait_ge(e_done, b - 1)
                nc.vector.tensor_scalar(s.negm[:, p:p + 1], s.smax[:, p:p + 1], -scale, None, ALU.mult).then_inc(neg_done, 1)
                fe.late_stats(b, p)
                if has_before(b, 1):
                    invert(b - 1, 1 - p)
                if has_before(b, 1):
                    fe.late_before_write(dve, b)
                    add(b - 1, 1 - p)
                    fe.late_after_write(b, p)
            for b in range(2):
                fe.dve_normalise(dve, b, b)
            slots(dve, slot)
            invert(NB - 1, 1)
            add(NB - 1, 1)
            fe.late_last_moments(dve, res_done)
    fe.base += NB
    fe.mbase += NB


def project_gates(nc, s):
    fe = s.front
    ag_ready, ag_taken = s.sem("l1f_ag"), s.sem("l1f_ag_taken")
    with nc.Block() as block:
        @block.tensor
        def _(pe):
            def slot(b, p):
                pe.wait_ge(fe.ready, fe.base + b + 1)
                if has_before(b, 2):
                    pe.wait_ge(ag_taken, b - 1)
                for c in range(DC):
                    last = nc.tensor.matmul(s.ps[:, 3 + p, 0:160], s.xnT[:, p, c, :], s.ag1[:, c, :], start=(c == 0), stop=(c == DC - 1))
                last.then_inc(ag_ready, 1)
                if has_after(b, 2):
                    fe.pe_turn(pe, b + 2, p)
            fe.pe_turn(pe, 0, 0)
            fe.pe_turn(pe, 1, 1)
            slots(pe, slot)

        @block.scalar
        def _(act):
            def take(b, p):
                act.wait_ge(fe.turned, fe.base + b + 1)
                if has_before(b, 2):
                    act.wait_ge(ag_ready, b - 1)
                nc.scalar.activation(s.xnT[:, p, :, :].rearrange("p c t -> p (c t)"), s.ps[:, 0, :], ACT.Copy)
                nc.scalar.activation(s.XNT[:, b, :, :].rearrange("p c t -> p (c t)"), s.ps[:, 0, :], ACT.Copy).then_inc(fe.ready, 1)

            def slot(b, p):
                act.wait_ge(ag_ready, b + 1)
                nc.scalar.activation(s.AGS[:, b, :], s.ps[:, 3 + p, 0:160], ACT.Copy).then_inc(ag_taken, 1)
                if has_after(b, 2):
                    take(b + 2, p)
            take(0, 0)
            take(1, 1)
            slots(act, slot)

        @block.vector
        def _(dve):
            def slot(b, p):
                if has_after(b, 2):
                    fe.dve_normalise(dve, b + 2, p)
            for b in range(2):
                fe.dve_normalise(dve, b, b)
            slots(dve, slot)
    fe.base += NB


def dense(nc, s, name, W, bias, out=None):
    sem = s.sem
    fe = s.front
    y_ready, bias_done, res_done = (sem(name + n) for n in ("_y", "_bias", "_res"))
    with nc.Block() as block:
        if out is not None:
            @block.sync
            def _(sp):
                with sp.Fori(0, NB) as b:
                    sp.wait_ge(res_done, b + 1)
                    sp.dma_start(out[b], s.X[:, b, :]).then_inc(s.x_out, 16)
                sp.wait_ge(s.x_out, 16 * NB)

        @block.gpsimd
        def _(pool):
            def slot(b, p):
                pool.wait_ge(fe.xn_ready, fe.base + b + 1)
                nc.gpsimd.tensor_tensor(s.X[:, b, :], s.X[:, b, :], bias, ALU.add).then_inc(bias_done, 1)
            slots(pool, slot)

        @block.tensor
        def _(pe):
            def slot(b, p):
                pe.wait_ge(fe.ready, fe.base + b + 1)
                if has_before(b, 2):
                    pe.wait_ge(res_done, b - 1)
                for c in range(DC):
                    last = nc.tensor.matmul(s.ps[:, 1 + p, :], s.xnT[:, p, c, :], W[:, c, :], start=(c == 0), stop=(c == DC - 1))
                last.then_inc(y_ready, 1)
                if has_after(b, 2):
                    fe.pe_turn(pe, b + 2, p)
            fe.pe_turn(pe, 0, 0)
            fe.pe_turn(pe, 1, 1)
            slots(pe, slot)

        @block.scalar
        def _(act):
            def take(b, p):
                act.wait_ge(fe.turned, fe.base + b + 1)
                if has_before(b, 2):
                    act.wait_ge(y_ready, b - 1)
                nc.scalar.activation(s.xnT[:, p, :, :].rearrange("p c t -> p (c t)"), s.ps[:, 0, :], ACT.Copy).then_inc(fe.ready, 1)

            def slot(b, p):
                if has_after(b, 2):
                    take(b + 2, p)
            take(0, 0)
            take(1, 1)
            slots(act, slot)

        @block.vector
        def _(dve):
            def slot(b, p):
                if has_after(b, 2):
                    fe.dve_normalise(dve, b + 2, p)
                dve.wait_ge(y_ready, b + 1)
                dve.wait_ge(bias_done, b + 1)
                nc.vector.tensor_tensor(s.X[:, b, :], s.ps[:, 1 + p, :], s.X[:, b, :], ALU.add).then_inc(res_done, 1)
            for b in range(2):
                fe.dve_normalise(dve, b, b)
            slots(dve, slot)
    fe.base += NB


def expert_ffn(nc, s):
    E, GH, R = 8, 32, 16
    CAPACITY = int(3.0 * NB * P / E)
    step, var_ready, rstd_ready, gap_ready, exp_ready, mine_ready, all_ready = (s.sem("eg_" + n) for n in (
        "step", "var", "rstd", "gap", "exp", "mine", "all"))
    row = s.rows1
    gb1, gamma, beta = (row[:, 32 * k:32 * k + 32].unsqueeze(1).broadcast_to([P, NB, GH]) for k in range(3))
    gw2 = row[:, 96:352].rearrange("p (e j) -> p e j", e=E).unsqueeze(1).broadcast_to([P, NB, E, GH])
    gb2 = row[:, 352:360].unsqueeze(1).broadcast_to([P, NB, E])
    first = row[:, 360:368].unsqueeze(1).broadcast_to([P, NB, E])
    h, sm = s.gh, s.gsm
    over_h = lambda k: sm[:, k, :].unsqueeze(2).broadcast_to([P, NB, GH])
    over_e = lambda k: sm[:, k, :].unsqueeze(2).broadcast_to([P, NB, E])
    g = lambda k: s.gg[:, k, :, :]
    fe = s.front
    tw_ready, tw_turned, tw_taken, y_ready, res_done = (s.sem("ex_" + n) for n in ("tw", "turned", "taken", "y", "res"))
    BANKS = 6

    def bank(b):
        return b if symbolic(b) else b % BANKS
    with nc.Block() as block:
        @block.vector
        def _(dve):
            link = linked(dve, step)
            v = nc.vector
            link(v.tensor_tensor(h[:, :, :], s.AGS[:, :, 128:160], gb1, ALU.add))
            link(v.tensor_reduce(sm[:, 0, :], h[:, :, :], AX.X, ALU.add))
            link(v.tensor_scalar(sm[:, 1, :], sm[:, 0, :], 1.0 / GH, None, ALU.mult))
            link(v.tensor_tensor(h[:, :, :], h[:, :, :], over_h(1), ALU.subtract))
            link(v.tensor_tensor(s.gprod[:, :, 0, :], h[:, :, :], h[:, :, :], ALU.mult))
            link(v.tensor_reduce(sm[:, 2, :], s.gprod[:, :, 0, :], AX.X, ALU.add))
            v.tensor_scalar(sm[:, 3, :], sm[:, 2, :], 1.0 / GH, LN_EPS, ALU.mult, ALU.add).then_inc(var_ready, 1)
            dve.wait_ge(rstd_ready, 1)
            link(v.tensor_tensor(h[:, :, :], h[:, :, :], over_h(4), ALU.mult))
            link(v.tensor_tensor(h[:, :, :], h[:, :, :], gamma, ALU.mult))
            link(v.tensor_tensor(h[:, :, :], h[:, :, :], beta, ALU.add))
            link(v.tensor_scalar(h[:, :, :], h[:, :, :], 0.0, None, ALU.max))
            link(v.tensor_tensor(s.gprod[:, :, :, :], h[:, :, :].unsqueeze(2).broadcast_to([P, NB, E, GH]), gw2, ALU.mult))
            link(v.tensor_reduce(g(0), s.gprod[:, :, :, :], AX.X, ALU.add))
            link(v.tensor_tensor(g(0), g(0), gb2, ALU.add))
            for k in range(2):
                link(v.tensor_reduce(sm[:, 5 + k, :], g(0), AX.X, ALU.max))
                link(v.tensor_tensor(g(3), g(0), over_e(5 + k), ALU.is_equal))
                link(v.tensor_tensor(g(3), g(3), first, ALU.mult))
                link(v.tensor_reduce(sm[:, 7, :], g(3), AX.X, ALU.max))
                link(v.tensor_tensor(g(1 + k), g(3), over_e(7), ALU.is_equal))
                link(v.tensor_reduce(s.gcount[:, k, :], g(1 + k).rearrange("p b e -> p e b"), AX.X, ALU.add))
                if k == 0:
                    link(v.scalar_tensor_tensor(g(0), g(1), -1e30, g(0), ALU.mult, ALU.add))
            v.tensor_tensor(sm[:, 8, :], sm[:, 6, :], sm[:, 5, :], ALU.subtract).then_inc(gap_ready, 1)
            dve.wait_ge(exp_ready, 1)
            link(v.tensor_scalar(sm[:, 10, :], sm[:, 9, :], 1.0, None, ALU.add))
            link(v.reciprocal(sm[:, 11, :], sm[:, 10, :]))
            link(v.tensor_tensor(sm[:, 12, :], sm[:, 9, :], sm[:, 11, :], ALU.mult))
            dve.wait_ge(all_ready, 1)
            link(v.tensor_scalar(s.gallow[:, :], s.ps[:, 7, 0:16], float(CAPACITY), 1.0 / R, ALU.is_le, ALU.mult))
            for k in range(2):
                link(v.tensor_tensor(g(1 + k), g(1 + k), over_e(11 + k), ALU.mult))
                link(v.tensor_tensor(g(1 + k), g(1 + k), s.gallow[:, 8 * k:8 * k + 8].unsqueeze(1).broadcast_to([P, NB, E]), ALU.mult))
            link(v.tensor_tensor(s.gw[:, :, :], g(1), g(2), ALU.add))

            def weigh(b, p):
                if has_before(b, 2):
                    dve.wait_ge(tw_turned, b - 1)
                nc.vector.tensor_tensor(s.tw[:, p, :].rearrange("p (e r) -> p e r", e=E), s.AGS[:, b, 0:128].rearrange("p (e r) -> p e r", e=E),
                                        s.gw[:, b, :].unsqueeze(2).broadcast_to([P, E, R]), ALU.mult).then_inc(tw_ready, 1)

            def slot(b, p):
                if has_after(b, 2):
                    weigh(b + 2, p)
                dve.wait_ge(y_ready, b + 1)
                fe.before_write(dve, b, res_done)
                nc.vector.tensor_tensor(s.X[:, b, :], s.ps[:, bank(b), :], s.X[:, b, :], ALU.add).then_inc(res_done, 1)
                fe.after_write(b, p)
            weigh(0, 0)
            weigh(1, 1)
            slots(dve, slot)
            fe.dve_last_moments(dve, res_done)

        @block.gpsimd
        def _(pool):
            pool.wait_ge(var_ready, 1)
            nc.gpsimd.tensor_tensor(sm[:, 4, :], sm[:, 3, :], s.minus_half[:, :], ALU.pow).then_inc(rstd_ready, 1)
            slots(pool, lambda b, p: fe.pool_rstd(pool, b, p))

        @block.scalar
        def _(act):
            act.wait_ge(gap_ready, 1)
            nc.scalar.activation(sm[:, 9, :], sm[:, 8, :], ACT.Exp).then_inc(exp_ready, 1)

            def slot(b, p):
                act.wait_ge(tw_turned, b + 1)
                if has_before(b, 2):
                    act.wait_ge(y_ready, b - 1)
                nc.scalar.activation(s.twT[:, p, :], s.ps[:, BANKS + p, 0:P], ACT.Copy).then_inc(tw_taken, 1)
            slots(act, slot)

        @block.tensor
        def _(pe):
            def main(b):
                if b >= BANKS:
                    pe.wait_ge(res_done, b - BANKS + 1)
                for c in range(DC):
                    nc.tensor.matmul(s.ps[:, b % BANKS, :], s.XNT[:, b, c, :], s.w1f[:, c, :], start=(c == 0), stop=False)

            def turn(b, p):
                pe.wait_ge(tw_ready, b + 1)
                if has_before(b, 2):
                    pe.wait_ge(tw_taken, b - 1)
                nc.tensor.transpose(s.ps[:, BANKS + p, 0:P], s.tw[:, p, :], s.ident).then_inc(tw_turned, 1)

            def slot(b, p):
                if has_after(b, 1):
                    turn(b + 1, 1 - p)
                pe.wait_ge(tw_taken, b + 1)
                nc.tensor.matmul(s.ps[:, bank(b), :], s.twT[:, p, :], s.lB1, start=False, stop=True).then_inc(y_ready, 1)

            for b in range(4):
                main(b)
            pe.wait_ge(gap_ready, 1)
            nc.tensor.matmul(s.ps[:, 7, 0:16], s.ones[:, :], s.gcount[:, :, :].rearrange("p k e -> p (k e)"), start=True, stop=True).then_inc(all_ready, 1)
            for b in range(4, BANKS):
                main(b)
            turn(0, 0)
            slot(0, 0)
            slot(1, 1)
            for b in range(BANKS, NB):
                main(b)
            with pe.Fori(1, NB // 2 - 1) as i:
                for p in range(2):
                    slot(2 * i + p, p)
            slot(NB - 2, 0)
            slot(NB - 1, 1)
    fe.mbase += NB


def grouped_query_attention(nc, s, t):
    sem = s.sem
    ct_in = (sem("l2_ct_in0"), sem("l2_ct_in1"))
    xn_ready, xt_ready, xt_taken, q_ready, qhi_done, qlo_done, kr_ready, khi_done, kx_done, v_ready, v_done = (sem("l2_" + n) for n in (
        "xn", "xt_ready", "xt_taken", "q_ready", "qhi", "qlo", "kr_ready", "khi", "kx", "v_ready", "v_done"))
    o_ready, res_done = sem("l2_o_ready"), sem("l2_res")
    cleared = sem("l2_cleared")
    A, B, ps, fe = s.A, s.B, s.ps, s.front
    with nc.Block() as block:
        @block.gpsimd
        def _(pool):
            nc.gpsimd.memset(s.VE[:, :, :, :, :], 0.0).then_inc(cleared, 1)

        @block.vector
        def _(dve):
            nc.vector.memset(s.m8[:, :, :, :, :], 0.0).then_inc(cleared, 1)
            for p in range(2):
                nc.vector.tensor_copy(s.KB[96:128, p, :, :], s.neg2[96:128, :, :]).then_inc(cleared, 1)

    def load(sp, b, p):
        if has_before(b, 2):
            sp.wait_ge(v_ready, b - 1)
        sp.dma_start(s.ctxT_s[:, p, :, :], t["ctxT"][b].rearrange("(c p) k -> p c k", p=P)).then_inc(ct_in[p], 16)

    class prep:
        @staticmethod
        def pe_first(pe, b, p):
            pe.wait_ge(xn_ready, b + 1)
            if has_before(b, 1):
                pe.wait_ge(kx_done, b)
            for c in range(DC):
                last = nc.tensor.transpose(ps[:, B, c * P:(c + 1) * P], s.xn[:, 0, c * P:(c + 1) * P], s.ident)
            last.then_inc(xt_ready, 1)

        @staticmethod
        def pe_queries(pe, b, p):
            pe.wait_ge(xt_taken, b + 1)
            if has_before(b, 2):
                pe.wait_ge(s.max_rows, b - 1)
            if has_before(b, 1):
                pe.wait_ge(v_done, b)
            for r in range(4):
                for c in range(DC):
                    last = nc.tensor.matmul(ps[:, A, r * P:(r + 1) * P], s.wq2[:, c, r, :], s.xnT[:, 0, c, :], start=(c == 0), stop=(c == DC - 1))
            last.then_inc(q_ready, 1)

        @staticmethod
        def pe_keys(pe, b, p):
            pe.wait_ge(ct_in[p], 8 * (b - p) + 16)
            for g in range(4):
                for c in range(DC):
                    last = nc.tensor.matmul(ps[0:96, B, g * P:(g + 1) * P], s.wk2[:, c, g, :], s.ctxT_s[:, p, c, :], start=(c == 0), stop=(c == DC - 1))
            last.then_inc(kr_ready, 1)
            pe.wait_ge(qlo_done, b + 1)
            if has_before(b, 1):
                pe.wait_ge(s.max_rows, b)
            for c in range(DC):
                last = nc.tensor.matmul(ps[:, A, 0:P], s.ctxT_s[:, p, c, :], s.wv2[:, c, :], start=(c == 0), stop=(c == DC - 1))
            last.then_inc(v_ready, 1)

        @staticmethod
        def act_context(act, b, p):
            act.wait_ge(xt_ready, b + 1)
            if has_before(b, 1):
                act.wait_ge(q_ready, b)
            nc.scalar.activation(s.xnT[:, 0, :, :].rearrange("p c t -> p (c t)"), ps[:, B, :], ACT.Copy).then_inc(xt_taken, 1)

        @staticmethod
        def act_queries(act, b, p):
            act.wait_ge(q_ready, b + 1)
            if has_before(b, 1):
                act.wait_ge(s.q_packed, 192 * b)
            nc.scalar.activation(s.QH[:, :], ps[:, A, :], ACT.Copy).then_inc(qhi_done, 1)

        @staticmethod
        def dve_x(dve, b, p, waits=lambda: None):
            waits()
            if has_before(b, 1):
                dve.wait_ge(xt_ready, b)
            nc.vector.tensor_scalar(s.xn[:, 0, :], s.X[:, b, :], s.mean[:, b, :], s.rstd[:, b, :], ALU.subtract, ALU.mult).then_inc(xn_ready, 1)

        @staticmethod
        def dve_queries(dve, b, p):
            dve.wait_ge(qhi_done, b + 1)
            nc.vector.tensor_tensor(s.QL[:, :], ps[:, A, :], s.QH[:, :].bitcast(F32), ALU.subtract).then_inc(qlo_done, 1)

        @staticmethod
        def dve_keys(dve, b, p):
            dve.wait_ge(kr_ready, b + 1)
            if has_before(b, 1):
                dve.wait_ge(s.kb_ready, b)
            nc.vector.tensor_copy(s.KH[0:96, :, :].rearrange("p g k -> p (g k)"), ps[0:96, B, :]).then_inc(khi_done, 1)

        @staticmethod
        def dve_split_keys(dve, b, p):
            dve.wait_ge(khi_done, b + 1)
            nc.vector.tensor_tensor(s.KH[32:64, :, :].rearrange("p g k -> p (g k)"), ps[32:64, B, :],
                                    s.KH[32:64, :, :].rearrange("p g k -> p (g k)").bitcast(F32), ALU.subtract).then_inc(kx_done, 1)

        @staticmethod
        def dve_values(dve, b, p):
            dve.wait_ge(v_ready, b + 1)
            nc.vector.tensor_copy(s.VS[:, :], ps[:, A, 0:P]).then_inc(v_done, 1)

        @staticmethod
        def pool(pool, b, p):
            spread(nc, s, pool, b, p, 2, s.mask2, kx_done, v_done)

        @staticmethod
        def sp(sp, b, p):
            pack_queries(nc, s, sp, b, p, qlo_done)

    class tail:
        written, late = res_done, True

        @staticmethod
        def wait_msg_free(dve, b):
            dve.wait_ge(o_ready, b)

        @staticmethod
        def pe_early(pe, b, p):
            pass

        @staticmethod
        def pe(pe, b, p):
            for r in range(4):
                if r % 2 == 0:
                    pe.wait_ge(s.msg_done, 2 * b + 2)
                last = nc.tensor.matmul(ps[:, 5, :], s.msg[:, r * P:(r + 1) * P], s.wo2[:, r, :], start=(r == 0), stop=(r == 3))
            last.then_inc(o_ready, 1)

        @staticmethod
        def act(act, b, p):
            pass

        @staticmethod
        def add(dve, b):
            dve.wait_ge(o_ready, b + 1)
            nc.vector.tensor_tensor(s.X[:, b, :], ps[:, 5, :], s.X[:, b, :], ALU.add).then_inc(res_done, 1)

    s.v_done, s.qlo_done = v_done, qlo_done
    ahead = [(s.w2f[:, :, :], t["w2f"]), (s.zl2[:, :, :], t["zl2"]), (s.lB2, t["lB2"]), (s.rows2[:, 0:512], t["b_base"].broadcast_to([P, D])),
             (s.rows2[:, 512:560], t["rows2"].broadcast_to([P, 48])), (s.active[:, :], t["active"].broadcast_to([P, 4]))]
    packed_attention(nc, s, "l2", 2, 16 ** -0.5, load, prep, tail, ahead=ahead)


def routed_ffn(nc, s, t):
    E, R = 16, 8
    sem = s.sem
    fe = s.front
    step, log_done = sem("rf_step"), sem("rf_log")
    (y_open, y_ready, zl_ready, l_done, max_done, neg_done, exp_done, c_done, sum_done, inv_done, alpha_done, zw_done, z_turned, z_taken,
     bias_done, res_done) = (sem("rf_" + n) for n in ("y_open", "y", "zl", "l", "max", "neg", "exp", "c", "sum", "inv", "alpha", "zw", "turned", "taken", "bias", "res"))
    iota, rb, prior = (s.rows2[:, 512 + 16 * k:528 + 16 * k] for k in range(3))
    with nc.Block() as block:
        @block.scalar
        def _(act):
            act.wait_ge(step, 1)
            nc.scalar.activation(s.ladj[:, 1, :], s.ladj[:, 0, :], ACT.Ln).then_inc(log_done, 1)

        @block.vector
        def _(dve):
            link = linked(dve, step)
            link(nc.vector.tensor_scalar(s.ladj[:, 0, :], prior, 1e-12, None, ALU.add))
            link(nc.vector.tensor_copy(s.activef[:, :], s.active[:, :]))
            link(nc.vector.tensor_scalar(s.cnt[:, :], iota, s.activef[:, 0:1], None, ALU.is_equal))
            for j in range(1, 4):
                link(nc.vector.scalar_tensor_tensor(s.cnt[:, :], iota, s.activef[:, j:j + 1], s.cnt[:, :], ALU.is_equal, ALU.add))
            link(nc.vector.tensor_scalar(s.ladj[:, 2, :], s.cnt[:, :], 0.0, -1e30, ALU.is_equal, ALU.mult))
            link(nc.vector.tensor_tensor(s.ladj[:, 3, :], s.ladj[:, 2, :], rb, ALU.add))
            dve.wait_ge(log_done, 1)
            link(nc.vector.tensor_tensor(s.ladj[:, 4, :], s.ladj[:, 3, :], s.ladj[:, 1, :], ALU.add))

    with nc.Block() as block:
        @block.gpsimd
        def _(pool):
            def slot(b, p):
                pool.wait_ge(fe.xn_ready, fe.base + b + 1)
                nc.gpsimd.tensor_tensor(s.X[:, b, :], s.X[:, b, :], s.rows2[:, 0:512], ALU.add).then_inc(bias_done, 1)
                if has_before(b, 2):
                    fe.pool_rstd(pool, b - 2, p)
            slots(pool, slot)
            fe.pool_rstd(pool, NB - 2, 0)
            fe.pool_rstd(pool, NB - 1, 1)

        @block.tensor
        def _(pe):
            def turn(b, p):
                pe.wait_ge(zw_done, b + 1)
                pe.wait_ge(z_taken, b)
                nc.tensor.transpose(s.ps[:, 5, 0:P], s.zw[:, p, :], s.ident).then_inc(z_turned, 1)

            def experts(b, p):
                pe.wait_ge(z_taken, b + 1)
                nc.tensor.matmul(s.ps[:, 1 + p, :], s.zwT[:, p, :], s.lB2, start=False, stop=True).then_inc(y_ready, 1)

            def slot(b, p):
                pe.wait_ge(fe.ready, fe.base + b + 1)
                if has_before(b, 2):
                    pe.wait_ge(zw_done, b - 1)
                for c in range(DC):
                    last = nc.tensor.matmul(s.ps[:, 3 + p, 0:144], s.xnT[:, p, c, :], s.zl2[:, c, :], start=(c == 0), stop=(c == DC - 1))
                last.then_inc(zl_ready, 1)
                if has_before(b, 1):
                    turn(b - 1, 1 - p)
                if has_before(b, 2):
                    pe.wait_ge(res_done, b - 1)
                for c in range(DC):
                    last = nc.tensor.matmul(s.ps[:, 1 + p, :], s.xnT[:, p, c, :], s.w2f[:, c, :], start=(c == 0), stop=False)
                last.then_inc(y_open, 1)
                if has_after(b, 2):
                    fe.pe_turn(pe, b + 2, p)
                if has_before(b, 1):
                    experts(b - 1, 1 - p)
            fe.pe_turn(pe, 0, 0)
            fe.pe_turn(pe, 1, 1)
            slots(pe, slot)
            turn(NB - 1, 1)
            experts(NB - 1, 1)

        @block.scalar
        def _(act):
            def take(b, p):
                act.wait_ge(fe.turned, fe.base + b + 1)
                if has_before(b, 2):
                    act.wait_ge(y_open, b - 1)
                nc.scalar.activation(s.xnT[:, p, :, :].rearrange("p c t -> p (c t)"), s.ps[:, 0, :], ACT.Copy).then_inc(fe.ready, 1)

            def take_z(b, p):
                act.wait_ge(z_turned, b + 1)
                if has_before(b, 2):
                    act.wait_ge(y_ready, b - 1)
                nc.scalar.activation(s.zwT[:, p, :], s.ps[:, 5, 0:P], ACT.Copy).then_inc(z_taken, 1)

            def slot(b, p):
                if has_before(b, 1):
                    take_z(b - 1, 1 - p)
                act.wait_ge(neg_done, b + 1)
                if has_before(b, 2):
                    act.wait_ge(c_done, b - 1)
                nc.scalar.activation(s.rex[:, p, :], s.rl[:, p, :], ACT.Exp, bias=s.negm[:, p:p + 1]).then_inc(exp_done, 1)
                if has_after(b, 2):
                    take(b + 2, p)
            take(0, 0)
            take(1, 1)
            slots(act, slot)
            take_z(NB - 1, 1)

        @block.vector
        def _(dve):
            v = nc.vector

            def add(b, p):
                dve.wait_ge(y_ready, b + 1)
                dve.wait_ge(bias_done, b + 1)
                v.tensor_tensor(s.X[:, b, :], s.ps[:, 1 + p, :], s.X[:, b, :], ALU.add).then_inc(res_done, 1)

            def slot(b, p):
                if has_after(b, 2):
                    fe.dve_normalise(dve, b + 2, p)
                dve.wait_ge(zl_ready, b + 1)
                if has_before(b, 2):
                    dve.wait_ge(exp_done, b - 1)
                v.tensor_tensor(s.rl[:, p, :], s.ps[:, 3 + p, 128:144], s.ladj[:, 4, :], ALU.add).then_inc(l_done, 1)
                dve.wait_ge(l_done, b + 1)
                dve.wait_ge(neg_done, b)
                fe.late_waits(dve, b, res_done)
                v.tensor_reduce(s.smax[:, p:p + 1], s.rl[:, p, :], AX.X, ALU.max).then_inc(max_done, 1)
                fe.late_stats(b, p)
                dve.wait_ge(max_done, b + 1)
                v.tensor_scalar(s.negm[:, p:p + 1], s.smax[:, p:p + 1], -1.0, None, ALU.mult).then_inc(neg_done, 1)
                dve.wait_ge(exp_done, b + 1)
                dve.wait_ge(alpha_done, b)
                v.tensor_tensor(s.rc[:, p, :], s.rex[:, p, :], s.cnt[:, :], ALU.mult).then_inc(c_done, 1)
                dve.wait_ge(c_done, b + 1)
                dve.wait_ge(inv_done, b)
                v.tensor_reduce(s.den[:, p:p + 1], s.rc[:, p, :], AX.X, ALU.add).then_inc(sum_done, 1)
                dve.wait_ge(sum_done, b + 1)
                v.reciprocal(s.rd[:, p:p + 1], s.den[:, p:p + 1]).then_inc(inv_done, 1)
                dve.wait_ge(inv_done, b + 1)
                dve.wait_ge(zw_done, b)
                v.tensor_scalar(s.ra[:, p, :], s.rc[:, p, :], s.rd[:, p:p + 1], 16.0 / 8.0, ALU.mult, ALU.mult).then_inc(alpha_done, 1)
                dve.wait_ge(alpha_done, b + 1)
                if has_before(b, 2):
                    dve.wait_ge(z_turned, b - 1)
                v.tensor_tensor(s.zw[:, p, :].rearrange("p (e r) -> p e r", e=E), s.ps[:, 3 + p, 0:128].rearrange("p (e r) -> p e r", e=E),
                                s.ra[:, p, :].unsqueeze(2).broadcast_to([P, E, R]), ALU.mult).then_inc(zw_done, 1)
                if has_before(b, 1):
                    fe.late_before_write(dve, b)
                    add(b - 1, 1 - p)
                    fe.late_after_write(b, p)
            for b in range(2):
                fe.dve_normalise(dve, b, b)
            slots(dve, slot)
            add(NB - 1, 1)
            fe.late_last_moments(dve, res_done)
    fe.base += NB
    fe.mbase += NB


def dequantise(nc, s, t):
    LANES = 0x11111111
    step, hot_done, added, turned, taken, own_hot, own_added = (s.sem("dq_" + n) for n in (
        "step", "hot", "added", "turned", "taken", "own_hot", "own_added"))
    order = (0, 2, 1, 3)
    halves = [[(o, k) for o in pair for k in range(16)] for pair in ((0, 1), (2, 3))]

    def codes(o):
        return s.code[:, 16 * o:16 * o + 16, :, :].rearrange("p w a r -> p (w a r)")

    def finish(dve, n):
        o, k = halves[1][n]
        dve.wait_ge(own_hot, n + 1)
        dve.wait_ge(own_added, n)
        if k:
            nc.vector.tensor_tensor(s.WO[:, o, :], s.WO[:, o, :], s.own[:, n % 2, :], ALU.add).then_inc(own_added, 1)
        else:
            nc.vector.memset(s.own[:, n % 2, 0:1], 0.0).then_inc(own_added, 1)

    class part:
        @staticmethod
        def dve(dve):
            v = nc.vector
            link = linked(dve, step)
            for r in range(4):
                link(v.tensor_scalar(s.T4[:, :, r], s.qw[:, 0, :], r, LANES, ALU.logical_shift_right, ALU.bitwise_and))
                for p in range(1, 4):
                    link(v.tensor_scalar(s.tq[:, :], s.qw[:, p, :], r, LANES, ALU.logical_shift_right, ALU.bitwise_and))
                    link(v.scalar_tensor_tensor(s.T4[:, :, r], s.tq[:, :], p, s.T4[:, :, r], ALU.logical_shift_left, ALU.bitwise_or))
            for a in range(8):
                link(v.tensor_scalar(s.code[:, :, a, :], s.T4[:, :, :], 4 * a, 15, ALU.logical_shift_right, ALU.bitwise_and))
            for n, ((o, k), (ov, kv)) in enumerate(zip(*halves)):
                if n >= 2:
                    dve.wait_ge(added, n - 1)
                v.tensor_scalar(s.hot[:, n % 2, :], codes(o), float(k), s.lut[:, o, k:k + 1], ALU.is_equal, ALU.mult).then_inc(hot_done, 1)
                if n >= 2:
                    dve.wait_ge(own_added, n - 1)
                to = s.own[:, n % 2, :] if kv else s.WO[:, ov, :]
                v.tensor_scalar(to, codes(ov), float(kv), s.lut[:, ov, kv:kv + 1], ALU.is_equal, ALU.mult).then_inc(own_hot, 1)
                if n:
                    finish(dve, n - 1)
            finish(dve, n)

        @staticmethod
        def pool(pool):
            for n, (o, k) in enumerate(halves[0]):
                pool.wait_ge(hot_done, n + 1)
                if k:
                    pool.wait_ge(added, n)
                    nc.gpsimd.tensor_tensor(s.WO[:, o, :], s.WO[:, o, :], s.hot[:, n % 2, :], ALU.add).then_inc(added, 1)
                else:
                    nc.gpsimd.tensor_copy(s.WO[:, o, :], s.hot[:, n % 2, :]).then_inc(added, 1)

        @staticmethod
        def pe(pe):
            for n, o in enumerate(order):
                pe.wait_ge(added if o < 2 else own_added, 16 * (o % 2 + 1))
                if n >= 2:
                    pe.wait_ge(taken, n - 1)
                for c in range(DC):
                    last = nc.tensor.transpose(s.ps[:, n % 2, c * P:(c + 1) * P], s.WO[:, o, c * P:(c + 1) * P], s.ident)
                last.then_inc(turned, 1)

        @staticmethod
        def act(act):
            for n, o in enumerate(order):
                act.wait_ge(turned, n + 1)
                nc.scalar.activation(s.WL[:, :, o * P:(o + 1) * P], s.ps[:, n % 2, :].rearrange("p (c o) -> p c o", c=DC), ACT.Copy).then_inc(taken, 1)
    return part


def carver(memory):
    used = [0]

    def carve(*shape):
        size = int(np.prod(shape))
        used[0] += size
        part = memory[:, used[0] - size:used[0]]
        if len(shape) == 1:
            return part
        names = "abc"[:len(shape)]
        return part.rearrange(f"p ({' '.join(names)}) -> p {' '.join(names)}", **dict(zip(names, shape)))
    return carve


def build(nc, t, out):
    s = Shared()
    with ExitStack() as top:
        def sb_in(stack):
            return lambda name, shape, dt=F32: stack.enter_context(nc.sbuf_tensor(name, shape, dt))
        sb = sb_in(top)
        s.retired, s.current = [], []

        def sem(name):
            handle = nc.alloc_semaphore(name=name)
            s.current.append(handle)
            return handle
        s.sem = sem
        s.X = sb("X", [P, NB, D])
        s.ident = sb("ident", [P, P])[:]
        s.ident_bf = sb("ident_bf", [P, P], BF16)
        s.ones = sb("ones", [P, P])
        s.ones_blk = {4: sb("ones4", [P, 4, 32])[:], 2: sb("ones2", [P, 2, 32])[:]}
        s.mask4 = sb("mask4", [96, 4])[:]
        s.mask2 = sb("mask2", [96, 2])[:]
        s.ones_ready = s.sem("ones_ready")
        s.eps = sb("eps", [P, 1])
        s.minus_half, s.var_eps = sb("minus_half", [P, NB]), sb("var_eps", [P, NB])
        s.mstats, s.mmv, s.mean = sb("mstats", [P, 2, 6]), sb("mmv", [P, 2, 2]), sb("mean", [P, NB, 1])
        s.stats = sb("stats", [P, NB, 6])
        s.mv = sb("mv", [P, NB, 2])
        s.rstd = sb("rstd", [P, NB, 1])
        s.xn = sb("xn", [P, 2, D])
        s.xnT = sb("xnT", [P, 2, DC, P])
        s.ps = top.enter_context(nc.psum_tensor("ps", [P, 8, 512], F32))
        s.A, s.B = 6, 7
        s.wabs = sb("wabs", [P, PAIRS, 3])
        s.x_out = s.sem("x_out")
        s.front = Front(nc, s)

        def packed_buffers(sb, tag, HL):
            s.Q = sb("Q" + tag, [P, 2, 4, 512], F32R)
            s.KB = sb("KB" + tag, [P, 2, 4, HL * P], F32R)
            s.VE = sb("VE" + tag, [P, 2, 4, HL, 32])
            s.QH, s.QL = sb("QH" + tag, [P, 512], F32R), sb("QL" + tag, [P, 512], F32R)
            s.KF, s.KH = sb("KF" + tag, [96, 4, P]), sb("KH" + tag, [96, 4, P], F32R)
            s.VS = sb("VS" + tag, [P, P])
            s.PT = sb("PT" + tag, [P, 8, 512])
            s.mx = sb("mx" + tag, [P, 4, 4, HL])
            s.m8 = sb("m8" + tag, [P, 4, 4, 2, 4], BF16)
            s.rden, s.msg = sb("rden" + tag, [P, 512]), sb("msg" + tag, [P, 512])
            s.ctxT_s = sb("ctxT_s" + tag, [P, 2, DC, P])

        with ExitStack() as phase:
            sb = sb_in(phase)
            packed_buffers(sb, "0", 4)
            s.neg = sb("neg4", [P, 4, 4 * P])
            s.XN = sb("XN", [P, NB, D])
            s.wq0, s.wk0, s.wm0 = (sb(n, [P, P])[:] for n in ("wq0", "wk0", "wm0"))
            s.wk0_rep = sb("wk0_rep", [P, 4, 96])[:]
            s.proj = sb("proj", [P, DC, P])[:]
            s.w1m0, s.w1x0 = sb("w1m0", [P, 256])[:], sb("w1x0", [P, 256])[:]
            s.w2_0 = sb("w2_0", [P, 2, P])[:]
            s.cols0 = sb("cols0", [P, 18])[:]
            s.bk0_row = sb("bk0_row", [P, P])[:]
            s.colsum, s.colsum_row = sb("colsum", [P, 1]), sb("colsum_row", [P, P])
            s.weff, s.bn = sb("weff", [P, 256]), sb("bn", [P, 14])
            s.C, s.H = sb("C", [P, P]), sb("H", [P, 2, 512])
            s.SW, s.SB, s.wscr = sb("SW", [P, 2, 2, 3, D]), sb("SB", [P, 2, 2, 3, D]), sb("wscr", [P, 2, D], BF16)
            s.current = []
            setup(nc, s, t)
            linear_attention_of_channels(nc, s, t)
        s.retired, s.current = s.current, []

        sb = sb_in(top)
        hidden = sb("hidden_weights", [P, 2 * PAIRS * 1024])
        early = sb("gates_weights", [P, 4096])
        s.SL = carver(early)(2, 2, 512)
        carve = carver(early)
        s.wq1, s.wk1 = carve(DC, D), carve(DC, D)
        carve = carver(early)
        s.w2f, s.zl2, s.lB2, s.rows2 = carve(DC, D), carve(DC, 144), carve(D), carve(560)
        s.cols1, s.qw, s.lut = sb("cols1", [P, 8]), sb("qw", [P, 4, 64], I32), sb("lut", [P, DC, 16])
        s.E, s.EWT, s.SR = sb("E", [P, 2, P]), sb("EWT", [P, 2, P]), sb("SR", [P, 2, P])
        s.smax, s.negm, s.den, s.rd = (sb(n, [P, 2]) for n in ("smax", "negm", "den", "rd"))
        with ExitStack() as phase:
            sb = sb_in(phase)
            s.XH, s.XLO = (sb(n, [P, DC, NB, P], F32R) for n in ("XH", "XLO"))
            s.RW, s.RB, s.SG = sb("RW", [P, 2, 2, D]), sb("RB", [P, 2, 2, D]), sb("SG", [P, 2, 2, D], BF16)
            s.WH, s.WLO = (sb(n, [P, 2, 2, D], F32R) for n in ("WH", "WLO"))
            s.HF = hidden[:, :].rearrange("p (j h t) -> p j h t", h=2, t=512)
            s.HH, s.HLO = (sb(n, [P, 2, 2, 512], F32R) for n in ("HH", "HLO"))
            s.wsum, s.coeff = sb("wsum", [P, 3]), sb("coeff", [P, 3])
            binary_gated_ffn(nc, s, t)
        for handle in s.retired:
            nc.release_semaphore(handle)
        carve = carver(hidden)
        s.w1f, s.ag1, s.rows1, s.lB1 = carve(DC, D), carve(DC, 160), carve(368), carve(D)
        s.wq2, s.wk2, s.wv2, s.wo2, s.neg2 = carve(DC, 4, P), carve(DC, 4, 96), carve(DC, P), carve(4, D), carve(4, 2 * P)
        s.WL, s.b3 = carve(DC, D), carve(D)
        sb = sb_in(top)
        s.ctx, s.ctxT = sb("ctx", [P, NB, D]), sb("ctxT", [P, DC, NB, P])
        with ExitStack() as folding:
            sb = sb_in(folding)
            s.mt1 = sb("mt1", [P, DC, D])
            s.bqk, s.v1, s.vrep = sb("bqk", [P, 8]), sb("v1", [P, 8]), sb("vrep", [P, DC, P])
            s.G, s.R = sb("G", [P, DC, NB, P]), sb("R", [P, NB, P])
            with ExitStack() as phase:
                sb = sb_in(phase)
                s.T4, s.tq = sb("T4", [P, 64, 4], I32), sb("tq", [P, 64], I32)
                s.code = sb("code", [P, 64, 8, 4], I32)
                s.hot, s.own, s.WO = sb("hot", [P, 2, D]), sb("own", [P, 2, D]), sb("WO", [P, DC, D])
                side_by_side(nc, s, [fold_text_attention(nc, s, t), dequantise(nc, s, t), moments_of_all(nc, s)],
                             (s.ctxT[:, :, :, :], t["ctxT_all"]),
                             [(s.ctx[:, :, :], t["ctx"]), (s.w1f[:, :, :], t["w1f"]), (s.ag1[:, :, :], t["ag1"]), (s.lB1, t["lB1"]), (s.rows1[:, :], t["rows1"].broadcast_to([P, 368])),
                              (s.wq2[:, :, :, :], t["wq2"]), (s.wk2[:, :, :, :], t["wk2"]), (s.wv2[:, :, :], t["wv2"]), (s.wo2[:, :, :], t["wo2"]),
                              (s.neg2[96:128], t["neg2"]), (s.b3[:, :], t["b3"].broadcast_to([P, D]))])
            context_attention(nc, s, "l1", s.G, s.R, D ** -0.5)
        with ExitStack() as phase:
            sb = sb_in(phase)
            s.AGS, s.gh, s.gsm, s.gg = sb("AGS", [P, NB, 160]), sb("gh", [P, NB, 32]), sb("gsm", [P, 13, NB]), sb("gg", [P, 4, NB, 8])
            s.gprod, s.gcount, s.gallow, s.gw = sb("gprod", [P, NB, 8, 32]), sb("gcount", [P, 2, 8]), sb("gallow", [P, 16]), sb("gw", [P, NB, 8])
            s.tw, s.twT = sb("tw", [P, 2, P]), sb("twT", [P, 2, P])
            s.XNT = sb("XNT", [P, NB, DC, P])
            project_gates(nc, s)
            expert_ffn(nc, s)
        with ExitStack() as routed:
            sb = sb_in(routed)
            s.active, s.activef = sb("active", [P, 4], I32), sb("activef", [P, 4])
            with ExitStack() as phase:
                packed_buffers(sb_in(phase), "2", 2)
                grouped_query_attention(nc, s, t)
            s.ladj, s.cnt = sb("ladj", [P, 5, 16]), sb("cnt", [P, 16])
            s.rl, s.rex, s.rc, s.ra = (sb(n, [P, 2, 16]) for n in ("rl", "rex", "rc", "ra"))
            s.zw, s.zwT = sb("zw", [P, 2, P]), sb("zwT", [P, 2, P])
            routed_ffn(nc, s, t)
        context_attention(nc, s, "l3", s.ctxT, None, 1.0)
        dense(nc, s, "l3f", s.WL, s.b3[:, :], out)


def lay_out(inputs):
    a = {k: np.asarray(v) for k, v in inputs.items()}
    cont = np.ascontiguousarray
    m = {}
    m["x"] = a["x"]
    m["ctxT"] = cont(a["ctx_4096"].transpose(0, 2, 1))
    m["ident"] = np.eye(P, dtype=np.float32)
    chan = np.array([d * 16 + 4 * g + h for g in range(4) for h in range(4) for d in range(8)])
    m["wq0"] = cont(a["L0_xattn_to_q_w"].T[:, chan])
    m["wk0"] = cont(a["L0_xattn_to_k_w"].T[:, chan])
    m["wk0_rep"] = cont(np.tile(m["wk0"].reshape(P, 4, 1, 32), (1, 1, 3, 1)).reshape(P, 4, 96))
    m["proj_k"] = a["L0_xattn_proj_k"]
    m["wm0"] = cont(a["L0_xattn_merge_w"][:, chan])
    def ffn(n1, n3, n2):
        up = [a[n].reshape(PAIRS, 2, P, DC, P).transpose(0, 4, 1, 3, 2).reshape(PAIRS, P, 2, D) for n in (n1, n3)]
        return cont(np.stack([*up, a[n2].T.reshape(PAIRS, 2, P, D).transpose(0, 2, 1, 3)], axis=3))
    m["base"] = ffn(*(f"L0_ffn_mean_w{n}" for n in (1, 3, 2)))
    m["w"] = ffn(*(f"L0_ffn_w{n}" for n in (1, 3, 2)))
    m["wq1"], m["wk1"] = (cont(a["L1_xattn_" + n].reshape(DC, P, D).transpose(1, 0, 2)) for n in ("Wq", "Wk"))
    m["cols1"] = cont(np.concatenate([a["L1_xattn_" + n].reshape(DC, P).T for n in ("bq", "bk")], axis=1))
    m["ctxT_all"] = cont(a["ctx_4096"].reshape(NB, P, DC, P).transpose(3, 2, 0, 1))
    m["ctx"] = cont(a["ctx_4096"].transpose(1, 0, 2))
    by_chunk = lambda w: cont(w.reshape(DC, P, -1).transpose(1, 0, 2))
    m["w1f"] = by_chunk(a["L1_ffn_weight"].T)
    m["ag1"] = by_chunk(np.concatenate([a["L1_ffn_lora_A"].transpose(1, 0, 2).reshape(D, P), a["L1_ffn_gw1"].T], axis=1))
    m["lB1"] = a["L1_ffn_lora_B"].reshape(P, D)
    m["rows1"] = np.concatenate([a["L1_ffn_gb1"], a["L1_ffn_ln_gamma"], a["L1_ffn_ln_beta"], a["L1_ffn_gw2"].reshape(-1),
                                 a["L1_ffn_gb2"], 8.0 - np.arange(8, dtype=np.float32)])[None, :]
    m["wq2"] = cont(a["L2_xattn_Wq"].reshape(DC, P, 8, 4, 16).transpose(1, 0, 3, 2, 4).reshape(P, DC, 4, P))
    m["wk2"] = cont(np.tile(a["L2_xattn_Wk"].reshape(DC, P, 4, 1, 32), (1, 1, 1, 3, 1)).transpose(1, 0, 2, 3, 4).reshape(P, DC, 4, 96))
    m["wv2"] = by_chunk(a["L2_xattn_Wv"])
    m["wo2"] = cont(a["L2_xattn_Wo"].reshape(8, 4, 16, D).transpose(0, 2, 1, 3).reshape(P, 4, D))
    m["w2f"] = by_chunk(a["L2_ffn_W_base"].T)
    m["zl2"] = by_chunk(np.concatenate([a["L2_ffn_lora_A"].reshape(P, D).T, a["L2_ffn_router_W"].T], axis=1))
    m["lB2"] = cont(a["L2_ffn_lora_B"].transpose(0, 2, 1).reshape(P, D))
    m["b_base"] = a["L2_ffn_b_base"][None, :]
    m["rows2"] = np.concatenate([np.arange(16, dtype=np.float32), a["L2_ffn_router_b"], a["L2_ffn_domain_prior"]])[None, :]
    m["active"] = a["L2_ffn_active"][None, :]
    m["qw"] = cont(a["L3_ffn_qweight"][:4].reshape(4, DC, P, 16).transpose(2, 0, 1, 3).reshape(P, 4, 64))
    m["lut4"] = a["L3_ffn_lut4"]
    m["b3"] = a["L3_ffn_bias"][None, :]
    w1t = a["L0_xattn_mlp_w1"].T
    m["w1x0"], m["w1m0"] = cont(w1t[:P]), cont(w1t[P:])
    m["w2_0"] = cont(a["L0_xattn_mlp_w2"].T.reshape(2, P, P).transpose(1, 0, 2))
    bk = a["L0_xattn_to_k_b"][chan]
    two = lambda n: a[n].reshape(2, P).T
    m["cols0"] = cont(np.concatenate([
        a["L0_xattn_to_q_b"][chan][:, None], np.tile(bk.reshape(4, 32).T, (4, 1)), np.zeros((P, 1), np.float32),
        a["L0_xattn_merge_b"][:, None], a["L0_xattn_mlp_b2"][:, None], two("L0_xattn_bn_gamma"), two("L0_xattn_bn_beta"),
        two("L0_xattn_bn_mean"), two("L0_xattn_bn_var"), two("L0_xattn_mlp_b1")], axis=1))
    m["bk0_row"] = cont(bk[None, :])
    for HL in (4, 2):
        w = 32 // HL
        head = np.arange(32) // w
        eye = np.eye(HL, dtype=np.float32)
        m[f"mask{HL}"] = cont(np.tile(eye[head], (3, 1)))
        m[f"ones{HL}"] = cont(np.tile(eye[:, head][None], (P, 1, 1)))
        neg = np.zeros((4, 2, 4, 4, HL, P), np.float32)
        for g in range(4):
            for h in range(HL):
                neg[g, :, h, g, h, :] = -1.0
        m[f"neg{HL}"] = neg.reshape(32, 4, HL * P)
    return m


def kernel(**inputs):
    import concourse.bacc as _bacc
    from concourse.bass_utils import run_bass_kernel_spmd as _run

    nc = _bacc.Bacc("TRN2", target_bir_lowering=False, num_devices=1)
    arrays = {f"in_{k}": v for k, v in lay_out(inputs).items()}
    t = {k[3:]: nc.dram_tensor(k, v.shape, mybir.dt.from_np(v.dtype), kind="ExternalInput").ap() for k, v in arrays.items()}
    out = nc.dram_tensor("out", (NB, P, D), F32, kind="ExternalOutput").ap()
    build(nc, t, out)
    return _run(nc, [arrays], core_ids=[0]).results[0]["out"]
```
